# Optimizing a Trainium2 kernel written in Bass

```python
import numpy as np
import jax
import jax.numpy as jnp

def _softmax(x, axis=-1):
    return jax.nn.softmax(x, axis=axis)

def _gelu(x):
    return jax.nn.gelu(x, approximate=True)

def _silu(x):
    return jax.nn.silu(x)

def _sigmoid(x):
    return jax.nn.sigmoid(x)

def _layernorm(x, axis=-1, eps=1e-05):
    m = jnp.mean(x, axis=axis, keepdims=True)
    v = jnp.var(x, axis=axis, keepdims=True)
    return (x - m) / jnp.sqrt(v + eps)

def _scatter_add(tgt, idx, src, axis=0):
    return tgt.at[idx].add(src)

def _segment_sum(src, seg, n):
    return jax.ops.segment_sum(src, seg, n)
kernel_name = 'mk_xattn_ffn_d2_seqx_r8_b74d92'

def setup_inputs(seed: int=0):
    np.random.seed(seed)
    _w = jnp.asarray

    def _rec_inputs():
        import jax
        import jax.numpy as jnp
        _rk = jax.random.key(seed)
        x = -0.0002928 + 1 * jax.random.normal(jax.random.fold_in(_rk, 1), (8, 128, 128), jnp.float32)
        _lenS = 128 - jax.random.randint(jax.random.fold_in(_rk, 7), (8,), 0, max(1, 128 // 4) + 1, jnp.int32)
        _lenS2 = 128 - jax.random.randint(jax.random.fold_in(_rk, 8), (8,), 0, max(1, 128 // 4) + 1, jnp.int32)
        _ctx_1024P = jax.random.normal(jax.random.fold_in(_rk, 11), (8, 16, 128), jnp.float32)
        _ctx_1024c = jax.random.dirichlet(jax.random.fold_in(_rk, 511), 0.3 * jnp.ones((16,), jnp.float32), (8, 128))
        _ctx_1024t = jnp.einsum('bsk,bkd->bsd', _ctx_1024c, _ctx_1024P)
        _ctx_1024t = _ctx_1024t * jax.lax.rsqrt(jnp.mean(jnp.square(_ctx_1024t)) + 1e-12) * 0.953939
        ctx_1024 = -1.39393e-06 + 0.999914 * (_ctx_1024t + 0.3 * jax.random.normal(jax.random.fold_in(_rk, 611), (8, 128, 128), jnp.float32))
        return (x, ctx_1024)
    x, ctx_1024 = _rec_inputs()

    def _L0_xattn_setup():
        import jax, jax.numpy as jnp
        import numpy as np
        B, N, QD, CD, H, DH = (2, 256, 128, 128, 8, 64)
        INNER = H * DH
        SCALE = DH ** (-0.5)

        def _split_heads(t):
            b, n, _ = t.shape
            return t.reshape(b, n, H, DH).transpose(0, 2, 1, 3)
        key = jax.random.key(seed)
        ks = jax.random.split(key, 11)
        s = lambda fan: 1.0 / np.sqrt(fan)
        return {'x': jax.random.normal(ks[0], (B, N, QD), jnp.float32), 'context': jax.random.normal(ks[1], (B, N, CD), jnp.float32), 'Wq1': jax.random.normal(ks[2], (QD, INNER), jnp.float32) * s(QD), 'Wk1': jax.random.normal(ks[3], (QD, INNER), jnp.float32) * s(QD), 'Wv1': jax.random.normal(ks[4], (QD, INNER), jnp.float32) * s(QD), 'Wq2': jax.random.normal(ks[5], (CD, INNER), jnp.float32) * s(CD), 'Wk2': jax.random.normal(ks[6], (CD, INNER), jnp.float32) * s(CD), 'Wv2': jax.random.normal(ks[7], (CD, INNER), jnp.float32) * s(CD), 'alpha_attn': jnp.zeros((), jnp.float32), 'Wout': jax.random.normal(ks[8], (INNER, QD), jnp.float32) * s(INNER), 'bout': jnp.zeros((QD,), jnp.float32)}
    _L0_xattn_all = _L0_xattn_setup()
    _L0_xattn_in = {k: v for k, v in _L0_xattn_all.items() if k in ('Wq1', 'Wk1', 'Wv1', 'Wq2', 'Wk2', 'Wv2', 'alpha_attn', 'Wout', 'bout')}
    del _L0_xattn_all

    def _L0_ffn_setup():
        import jax, jax.numpy as jnp
        import numpy as np
        B, S, D = (4, 256, 128)
        E = 8
        CF = 1
        key = jax.random.key(seed)
        k_x, k_g, k_w, k_b = jax.random.split(key, 4)
        x = jax.random.normal(k_x, (B, S, D), dtype=jnp.float32)
        Wg = jax.random.normal(k_g, (D, E), dtype=jnp.float32) * (1.0 / np.sqrt(D))
        We = jax.random.normal(k_w, (D, D), dtype=jnp.float32) * (1.0 / np.sqrt(D))
        be = jax.random.normal(k_b, (D,), dtype=jnp.float32) * 0.01
        return {'x': x, 'Wg': Wg, 'We': We, 'be': be}
    _L0_ffn_all = _L0_ffn_setup()
    _L0_ffn_in = {k: v for k, v in _L0_ffn_all.items() if k in ('Wg', 'We', 'be')}
    del _L0_ffn_all

    def _L1_xattn_setup():
        import jax, jax.numpy as jnp
        import numpy as np
        DIM = 128
        NUM_HEADS = 8
        HEAD_DIM = 64
        INNER = NUM_HEADS * HEAD_DIM
        key = jax.random.key(seed)
        ks = jax.random.split(key, 7)
        B, N, M = (8, 64, 512)
        x = jax.random.normal(ks[0], (B, N, DIM), dtype=jnp.float32)
        context = jax.random.normal(ks[1], (B, M, DIM), dtype=jnp.float32)
        s_in = 1.0 / np.sqrt(DIM)
        s_inner = 1.0 / np.sqrt(INNER)
        Wq = jax.random.normal(ks[2], (DIM, INNER), dtype=jnp.float32) * s_in
        Wk = jax.random.normal(ks[3], (DIM, INNER), dtype=jnp.float32) * s_in
        Wv = jax.random.normal(ks[4], (DIM, INNER), dtype=jnp.float32) * s_in
        Wo = jax.random.normal(ks[5], (INNER, DIM), dtype=jnp.float32) * s_inner
        bo = jax.random.normal(ks[6], (DIM,), dtype=jnp.float32) * 0.01
        return {'x': x, 'context': context, 'Wq': Wq, 'Wk': Wk, 'Wv': Wv, 'Wo': Wo, 'bo': bo}
    _L1_xattn_all = _L1_xattn_setup()
    _L1_xattn_in = {k: v for k, v in _L1_xattn_all.items() if k in ('Wq', 'Wk', 'Wv', 'Wo', 'bo')}
    del _L1_xattn_all

    def _L1_ffn_setup():
        import math
        import jax, jax.numpy as jnp
        import numpy as np
        D_MODEL = 128
        D_FF = 512
        N_EXPERTS = 8
        CAPACITY_FACTOR = 1.25
        L, B = (64, 8)

        def _route(tokens, router_w):
            T = tokens.shape[0]
            E = router_w.shape[0]
            capacity = int(math.ceil(T / E * CAPACITY_FACTOR))
            logits = tokens @ router_w.T
            probs = jax.nn.softmax(logits, axis=-1)
            top1_idx = jnp.argmax(probs, axis=-1)
            top1_prob = jnp.max(probs, axis=-1)
            order = jnp.lexsort((-top1_prob, top1_idx))
            sorted_e = top1_idx[order]
            counts = jnp.bincount(top1_idx, length=E)
            start = jnp.cumsum(counts) - counts
            pos_in_group = jnp.arange(T) - start[sorted_e]
            keep_sorted = pos_in_group < capacity
            keep = jnp.zeros((T,), bool).at[order].set(keep_sorted)
            return jnp.where(keep, top1_idx, 0).astype(jnp.int32)
        key = jax.random.key(seed)
        ks = jax.random.split(key, 6)
        s_in = 1.0 / math.sqrt(D_MODEL)
        s_ff = 1.0 / math.sqrt(D_FF)
        return {'x': jax.random.normal(ks[0], (L, B, D_MODEL), dtype=jnp.float32), 'router_w': jax.random.uniform(ks[1], (N_EXPERTS, D_MODEL), minval=-s_in, maxval=s_in), 'W1': jax.random.uniform(ks[2], (N_EXPERTS, D_MODEL, D_FF), minval=-s_in, maxval=s_in), 'b1': jax.random.uniform(ks[3], (N_EXPERTS, D_FF), minval=-s_in, maxval=s_in), 'W2': jax.random.uniform(ks[4], (N_EXPERTS, D_FF, D_MODEL), minval=-s_ff, maxval=s_ff), 'b2': jax.random.uniform(ks[5], (N_EXPERTS, D_MODEL), minval=-s_ff, maxval=s_ff)}
    _L1_ffn_all = _L1_ffn_setup()
    _L1_ffn_in = {k: v for k, v in _L1_ffn_all.items() if k in ('router_w', 'W1', 'b1', 'W2', 'b2')}
    del _L1_ffn_all
    return {'x': x, 'ctx_1024': ctx_1024, 'L0_xattn_Wq1': _L0_xattn_in['Wq1'], 'L0_xattn_Wk1': _L0_xattn_in['Wk1'], 'L0_xattn_Wv1': _L0_xattn_in['Wv1'], 'L0_xattn_Wq2': _L0_xattn_in['Wq2'], 'L0_xattn_Wk2': _L0_xattn_in['Wk2'], 'L0_xattn_Wv2': _L0_xattn_in['Wv2'], 'L0_xattn_alpha_attn': _L0_xattn_in['alpha_attn'], 'L0_xattn_Wout': _L0_xattn_in['Wout'], 'L0_xattn_bout': _L0_xattn_in['bout'], 'L0_ffn_Wg': _L0_ffn_in['Wg'], 'L0_ffn_We': _L0_ffn_in['We'], 'L0_ffn_be': _L0_ffn_in['be'], 'L1_xattn_Wq': _L1_xattn_in['Wq'], 'L1_xattn_Wk': _L1_xattn_in['Wk'], 'L1_xattn_Wv': _L1_xattn_in['Wv'], 'L1_xattn_Wo': _L1_xattn_in['Wo'], 'L1_xattn_bo': _L1_xattn_in['bo'], 'L1_ffn_router_w': _L1_ffn_in['router_w'], 'L1_ffn_W1': _L1_ffn_in['W1'], 'L1_ffn_b1': _L1_ffn_in['b1'], 'L1_ffn_W2': _L1_ffn_in['W2'], 'L1_ffn_b2': _L1_ffn_in['b2']}

def reference(x, ctx_1024, L0_xattn_Wq1, L0_xattn_Wk1, L0_xattn_Wv1, L0_xattn_Wq2, L0_xattn_Wk2, L0_xattn_Wv2, L0_xattn_alpha_attn, L0_xattn_Wout, L0_xattn_bout, L0_ffn_Wg, L0_ffn_We, L0_ffn_be, L1_xattn_Wq, L1_xattn_Wk, L1_xattn_Wv, L1_xattn_Wo, L1_xattn_bo, L1_ffn_router_w, L1_ffn_W1, L1_ffn_b1, L1_ffn_W2, L1_ffn_b2):
    import jax
    import jax.numpy as jnp

    def _L0_xattn_ref(x, context, Wq1, Wk1, Wv1, Wq2, Wk2, Wv2, alpha_attn, Wout, bout):
        import jax, jax.numpy as jnp
        import numpy as np
        B, N, QD, CD, H, DH = (2, 256, 128, 128, 8, 64)
        INNER = H * DH
        SCALE = DH ** (-0.5)

        def _split_heads(t):
            b, n, _ = t.shape
            return t.reshape(b, n, H, DH).transpose(0, 2, 1, 3)
        q1 = _split_heads(x @ Wq1)
        k1 = _split_heads(x @ Wk1)
        v1 = _split_heads(x @ Wv1)
        q2 = _split_heads(context @ Wq2)
        k2 = _split_heads(context @ Wk2)
        v2 = _split_heads(context @ Wv2)
        sim1 = jnp.einsum('bhid,bhjd->bhij', q2, k1) * SCALE
        attn1 = jax.nn.softmax(sim1, axis=-1)
        out1 = jnp.einsum('bhij,bhjd->bhid', attn1, v1)
        sim2 = jnp.einsum('bhid,bhjd->bhij', q1, k2) * SCALE
        attn2 = jax.nn.softmax(sim2, axis=-1)
        out2 = jnp.einsum('bhij,bhjd->bhid', attn2, v2)
        alpha = jax.nn.sigmoid(alpha_attn)
        out = out1 * alpha + out2 * (1.0 - alpha)
        out = out.transpose(0, 2, 1, 3).reshape(out.shape[0], out.shape[2], INNER)
        return out @ Wout + bout

    def _L0_ffn_ref(x, Wg, We, be):
        import jax, jax.numpy as jnp
        import numpy as np
        B, S, D = (4, 256, 128)
        E = 8
        CF = 1
        b, s, d = x.shape
        n = b * s
        cap = n // E * CF
        h = x.reshape(n, d)
        router_logits = h @ Wg
        probs = jax.nn.softmax(router_logits, axis=1)
        best = jnp.argmax(probs, axis=1)
        mask = jax.nn.one_hot(best, E, dtype=probs.dtype)
        gate = jnp.sum(probs * mask, axis=1)
        locations = jnp.cumsum(mask, axis=0) - 1.0
        mask = mask * (locations < cap).astype(mask.dtype)
        loc_idx = jnp.sum(locations * mask, axis=1).astype(jnp.int32)
        new_gate = gate[:, None] * mask
        loc_oh = jax.nn.one_hot(loc_idx, cap, dtype=new_gate.dtype)
        combine = new_gate[:, :, None] * loc_oh[:, None, :]
        dispatch = (combine != 0).astype(h.dtype)
        dispatched = jnp.einsum('nec,nd->ecd', dispatch, h).reshape(E * cap, d)
        expert_out = dispatched @ We + be
        out = combine.reshape(n, E * cap) @ expert_out
        return out.reshape(b, s, d)

    def _L1_xattn_ref(x, context, Wq, Wk, Wv, Wo, bo):
        import jax, jax.numpy as jnp
        import numpy as np
        DIM = 128
        NUM_HEADS = 8
        HEAD_DIM = 64
        INNER = NUM_HEADS * HEAD_DIM
        B, N, _ = x.shape
        M = context.shape[1]
        scale = HEAD_DIM ** (-0.5)
        q = (x @ Wq).reshape(B, N, NUM_HEADS, HEAD_DIM).transpose(0, 2, 1, 3)
        k = (context @ Wk).reshape(B, M, NUM_HEADS, HEAD_DIM).transpose(0, 2, 1, 3)
        v = (context @ Wv).reshape(B, M, NUM_HEADS, HEAD_DIM).transpose(0, 2, 1, 3)
        attn = jax.nn.softmax(jnp.einsum('bhnd,bhmd->bhnm', q, k) * scale, axis=-1)
        out = jnp.einsum('bhnm,bhmd->bhnd', attn, v)
        out = out.transpose(0, 2, 1, 3).reshape(B, N, INNER)
        return out @ Wo + bo

    def _L1_ffn_ref(x, router_w, W1, b1, W2, b2):
        import math
        import jax, jax.numpy as jnp
        import numpy as np
        D_MODEL = 128
        D_FF = 512
        N_EXPERTS = 8
        CAPACITY_FACTOR = 1.25
        L, B = (64, 8)

        def _route(tokens, router_w):
            T = tokens.shape[0]
            E = router_w.shape[0]
            capacity = int(math.ceil(T / E * CAPACITY_FACTOR))
            logits = tokens @ router_w.T
            probs = jax.nn.softmax(logits, axis=-1)
            top1_idx = jnp.argmax(probs, axis=-1)
            top1_prob = jnp.max(probs, axis=-1)
            order = jnp.lexsort((-top1_prob, top1_idx))
            sorted_e = top1_idx[order]
            counts = jnp.bincount(top1_idx, length=E)
            start = jnp.cumsum(counts) - counts
            pos_in_group = jnp.arange(T) - start[sorted_e]
            keep_sorted = pos_in_group < capacity
            keep = jnp.zeros((T,), bool).at[order].set(keep_sorted)
            return jnp.where(keep, top1_idx, 0).astype(jnp.int32)
        Lx, Bx, D = x.shape
        T = Lx * Bx
        E = router_w.shape[0]
        tokens = x.reshape(T, D)
        final_e = _route(tokens, router_w)
        out = jnp.zeros_like(tokens)
        for e in range(E):
            h = jax.nn.relu(tokens @ W1[e] + b1[e])
            y = h @ W2[e] + b2[e]
            out = out + jnp.where((final_e == e)[:, None], y, 0.0)
        return out.reshape(Lx, Bx, D)
    x = x + _L0_xattn_ref(_layernorm(x, axis=-1), ctx_1024, L0_xattn_Wq1, L0_xattn_Wk1, L0_xattn_Wv1, L0_xattn_Wq2, L0_xattn_Wk2, L0_xattn_Wv2, L0_xattn_alpha_attn, L0_xattn_Wout, L0_xattn_bout)
    x = x + _L0_ffn_ref(_layernorm(x, axis=-1), L0_ffn_Wg, L0_ffn_We, L0_ffn_be)
    x = x + _L1_xattn_ref(_layernorm(x, axis=-1), ctx_1024, L1_xattn_Wq, L1_xattn_Wk, L1_xattn_Wv, L1_xattn_Wo, L1_xattn_bo)
    x = x + _L1_ffn_ref(_layernorm(x, axis=-1), L1_ffn_router_w, L1_ffn_W1, L1_ffn_b1, L1_ffn_W2, L1_ffn_b2)
    return x

_drawn_inputs = setup_inputs


def setup_inputs(seed=0):
    import zlib

    import numpy as np

    out = dict(_drawn_inputs(seed))
    spreads = {'L0_xattn_bout': (0.0, 0.1)}
    factors = {'L0_ffn_be': 8.0, 'L1_xattn_bo': 2.782, 'L1_ffn_b1': 3.391, 'L1_ffn_b2': 2.706}
    for name, (base, spread) in spreads.items():
        noise = np.random.default_rng([zlib.crc32(name.encode()), seed]).standard_normal(out[name].shape)
        drawn = base * np.exp(spread * noise) if base else spread * noise
        out[name] = jnp.asarray(drawn.astype(out[name].dtype))
    for name, factor in factors.items():
        out[name] = (out[name] * factor).astype(out[name].dtype)
    return out
```

```python
from contextlib import ExitStack

import concourse.bass as bass
from concourse import mybir

ALU = mybir.AluOpType
ACT = mybir.ActivationFunctionType
AX = mybir.AxisListType
F32 = mybir.dt.float32
BF16 = mybir.dt.bfloat16
I32 = mybir.dt.int32
U32 = mybir.dt.uint32

EPS = 1e-5


def two_layers(nc, x, ctx_1024, L0_xattn_Wq1, L0_xattn_Wk1, L0_xattn_Wv1, L0_xattn_Wq2, L0_xattn_Wk2,
               L0_xattn_Wv2, L0_xattn_alpha_attn, L0_xattn_Wout, L0_xattn_bout, L0_ffn_Wg, L0_ffn_We,
               L0_ffn_be, L1_xattn_Wq, L1_xattn_Wk, L1_xattn_Wv, L1_xattn_Wo, L1_xattn_bo,
               L1_ffn_router_w, L1_ffn_W1, L1_ffn_b1, L1_ffn_W2, L1_ffn_b2, out):
    NT, P, D = x.shape
    INNER = L0_xattn_Wq1.shape[1]
    DH = 64
    H = INNER // DH
    C = INNER // P
    E = L0_ffn_Wg.shape[1]
    FF = L1_ffn_W1.shape[2]
    FC = FF // P
    T = NT * P
    SCALE = float(DH) ** -0.5
    CAP0 = T // E
    CAP1 = -(-(T * 5) // (E * 4))
    SLOTS = (E - 1) * CAP1
    ST = -(-SLOTS // P)
    FAR = 8192.0
    HALF = T // 2
    assert P == 128 and D == 128 and C == 4 and H == 8 and E == 8

    ctx = ExitStack()
    with ctx:
        def sb(name, shape, dt=F32):
            return ctx.enter_context(nc.sbuf_tensor(name, shape, dt))

        def sems(names):
            return [ctx.enter_context(nc.semaphore(n)) for n in names.split()]

        m0, m1, s_even, s_odd, t_even, t_odd, o_even, o_odd = [
            ctx.enter_context(nc.psum_tensor(n, [P, 512], F32))
            for n in ("m0", "m1", "s_even", "s_odd", "t_even", "t_odd", "o_even", "o_odd")]
        s_bank, t_bank, o_bank = (s_even, s_odd), (t_even, t_odd), (o_even, o_odd)

        def chunks(bank):
            return bank[:, :].rearrange("p (c n) -> p c n", c=C)

        def heads_out(bank):
            return bank[:, 0:C * (DH + 1)].rearrange("p (c n) -> p c n", c=C)

        ident = sb("ident", [P, P])
        ones = sb("ones", [P, P], BF16)
        before = sb("before", [P, P], BF16)
        first_first = sb("first_first", [P, E])
        place_base = sb("place_base", [P, E])
        minus_half = sb("minus_half", [P, 1])
        eps_col = sb("eps_col", [P, 1])
        carrier = sb("carrier", [P, 1])
        zeros = sb("zeros", [P, ST * D])
        wq1, wk1, wv1, wq2, wk2, wv2, wq, wk, wv = [
            sb(n, [D, INNER]) for n in "wq1 wk1 wv1 wq2 wk2 wv2 wq wk wv".split()]
        wout = sb("wout", [P, C, D])
        wo = sb("wo", [P, C, D])
        we_wg = sb("we_wg", [D, D + E])
        rw_rows = sb("rw_rows", [E, D])
        rw_t = sb("rw_t", [D, E])
        w1 = sb("w1", [D, E, FF])
        w2 = sb("w2", [P, E, FC, D])
        b1_rows = sb("b1_rows", [E * FC, P])
        b1_t = sb("b1_t", [P, E * FC])
        b2_rows = sb("b2_rows", [E, D])
        b2_t = sb("b2_t", [D, E])
        bout_b, be_b, bo_b, b20_b = [sb(n, [P, D]) for n in "bout_b be_b bo_b b20_b".split()]
        alpha = sb("alpha", [P, 4])
        x_in = sb("x_in", [P, D])
        ctx_in = sb("ctx_in", [P, D])
        stat_n, mv_n, rstd_n = sb("stat_n", [P, 6]), sb("mv_n", [P, 2]), sb("rstd_n", [P, 2])
        xn = sb("xn", [P, D])
        xc_t = sb("xc_t", [D, 2, P])
        xb = sb("xb", [P, D])
        q1, k1, q2, k2 = [sb(n, [P, C, P]) for n in "q1 k1 q2 k2".split()]
        v1, v2 = [sb(n, [P, H, DH + 1]) for n in "v1 v2".split()]
        shifted = sb("shifted", [P, 2, C, P])
        probs = sb("probs", [P, 2, C, P])
        probs_t = sb("probs_t", [P, 2, C, P])
        top = sb("top", [P, 2, C])
        rsum = sb("rsum", [P, 2, C])
        att_a = sb("att_a", [P, C, 2, DH])
        att_a2 = sb("att_a2", [P, C, 2, DH])
        att_at = sb("att_at", [P, C, P])
        x1 = sb("x1", [P, D])
        stat_b, mv_b, rstd_b = sb("stat_b", [P, 6]), sb("mv_b", [P, 2]), sb("rstd_b", [P, 2])
        h_b = sb("h_b", [P, D])
        h_bt = sb("h_bt", [D, P])
        ybe = sb("ybe", [P, D])
        gate = sb("gate", [P, 8])
        lg = sb("lg", [P, 3, E])
        pick = sb("pick", [P, E], BF16)
        pick_sum = sb("pick_sum", [P, E], BF16)
        kept = sb("kept", [P, E])
        x2 = sb("x2", [P, D])
        stat_2, mv_2, rstd_2 = sb("stat_2", [P, 6]), sb("mv_2", [P, 2]), sb("rstd_2", [P, 2])
        h_2 = sb("h_2", [P, D])
        h_2t = sb("h_2t", [D, P])
        xb2 = sb("xb2", [P, D])
        ql, kl = sb("ql", [P, C, P]), sb("kl", [P, C, P])
        vl = sb("vl", [P, H, DH + 1])
        att_b = sb("att_b", [P, C, 2, DH])
        att_bt = sb("att_bt", [P, C, P])
        x3 = sb("x3", [P, D])
        stat_c, mv_c, rstd_c = sb("stat_c", [P, 6]), sb("mv_c", [P, 2]), sb("rstd_c", [P, 2])
        h_c = sb("h_c", [P, D])
        h_ct = sb("h_ct", [D, P])
        x3_all = sb("x3_all", [P, NT, D])
        h_all = sb("h_all", [P, NT, D])
        ht_all = sb("ht_all", [D, T])
        lg_all = sb("lg_all", [P, NT, E])
        r_max, r_sum, r_prob, r_first, r_base, r_pos, r_out, r_slot = [
            sb(n, [P, NT]) for n in "r_max r_sum r_prob r_first r_base r_pos r_out r_slot".split()]
        r_less, r_exp, r_mark, r_tmp, r_tmp2 = [
            sb(n, [P, NT, E]) for n in "r_less r_exp r_mark r_tmp r_tmp2".split()]
        r_pick = sb("r_pick", [P, NT, E], BF16)
        r_idx = sb("r_idx", [P, NT], U32)
        prob_row = sb("prob_row", [P, T])
        ahead = sb("ahead", [P, NT, T], BF16)
        ties = sb("ties", [P, NT, P], BF16)
        hid0 = sb("hid0", [P, FC, T])
        acc = sb("acc", [P, NT, D])
        xg = sb("xg", [P, ST, D])
        xg_t = sb("xg_t", [D, ST * P])
        hid = sb("hid", [P, 2, FC, CAP1])
        y_t = sb("y_t", [D, SLOTS])
        y_rows = sb("y_rows", [P, ST, D])
        y_back = sb("y_back", [P, NT, D])
        res = sb("res", [P, NT, D])
        xg_dram = nc.dram_tensor("xg_dram", [ST * P, D], F32, kind="Internal").ap()
        y_dram = nc.dram_tensor("y_dram", [ST * P, D], F32, kind="Internal").ap()

        x_in_s, ctx_in_s, alpha_in, wq2_in, wk1_in, wv1_in, wq1_in, wk2_in, wv2_in = sems(
            "x_in_s ctx_in_s alpha_in wq2_in wk1_in wv1_in wq1_in wk2_in wv2_in")
        bout_in, small_in, late_a_in, stage_b_in, w1_in, w2_in = sems(
            "bout_in small_in late_a_in stage_b_in w1_in w2_in")
        const_s, xg_zero_in, alpha_exp, alpha_s, rw_mm, small_s = sems(
            "const_s xg_zero_in alpha_exp alpha_s rw_mm small_s")
        n_mv, n_rstd, n_xn, n_mm, n_sb, xb_s = sems(
            "n_mv n_rstd n_xn n_mm n_sb xb_s")
        q2_mm, q2_sb, k1_mm, k1_sb, v1_mm, v1_sb, q1_mm, q1_sb, k2_mm, k2_sb, v2_mm, v2_sb = sems(
            "q2_mm q2_sb k1_mm k1_sb v1_mm v1_sb q1_mm q1_sb k2_mm k2_sb v2_mm v2_sb")
        kl_mm, kl_sb, vl_mm, vl_sb = sems("kl_mm kl_sb vl_mm vl_sb")
        (d1_mm, d2_mm, dl_mm) = sems("d1_mm d2_mm dl_mm")
        d1_max, d2_max, dl_max = sems("d1_max d2_max dl_max")
        d1_sub, d2_sub, dl_sub = sems("d1_sub d2_sub dl_sub")
        d1_exp, d2_exp, dl_exp = sems("d1_exp d2_exp dl_exp")
        d1_tmm, d2_tmm, dl_tmm = sems("d1_tmm d2_tmm dl_tmm")
        d1_tsb, d2_tsb, dl_tsb = sems("d1_tsb d2_tsb dl_tsb")
        d1_omm, d2_omm, dl_omm = sems("d1_omm d2_omm dl_omm")
        d1_rec, d2_rec, dl_rec = sems("d1_rec d2_rec dl_rec")
        d1_out, d2_out, dl_out = sems("d1_out d2_out dl_out")

        def half(n, par):
            return 2 * n - 1 + par

        def both(n):
            return 2 * n
        att_s, aot_mm, aot_sb, x1_mm, x1_s = sems("att_s aot_mm aot_sb x1_mm x1_s")
        b_mv, b_rstd, b_h, bt_mm, bt_sb, y_mm, g_max, g_less, y_s, g_mark, g_exp = sems(
            "b_mv b_rstd b_h bt_mm bt_sb y_mm g_max g_less y_s g_mark g_exp")
        g_first, g_pick, loc_mm, g_gate, g_kept, g_kgate, pick_sum_s, x2_s = sems(
            "g_first g_pick loc_mm g_gate g_kept g_kgate pick_sum_s x2_s")
        b2_mv, b2_rstd, b2_h, b2t_mm, b2t_sb, xb2_s, ql_mm, ql_sb = sems(
            "b2_mv b2_rstd b2_h b2t_mm b2t_sb xb2_s ql_mm ql_sb")
        bot_mm, bot_sb, x3_mm, x3_s = sems("bot_mm bot_sb x3_mm x3_s")
        c_mv, c_rstd, c_h, ct_mm, ct_sb, cl_mm, cl_s, x3_all_s, h_all_s, ht_all_s = sems(
            "c_mv c_rstd c_h ct_mm ct_sb cl_mm cl_s x3_all_s h_all_s ht_all_s")
        f_dve, f_less, f_exp, f_prob, f_pick, row_mm, row_sb, ahead_s, rank_mm, f_out, f_idx = sems(
            "f_dve f_less f_exp f_prob f_pick row_mm row_sb ahead_s rank_mm f_out f_idx")
        hid0_mm, hid0_sb, y0_mm, y0_s, acc_s, scat_s, xg_in, xgt_mm, xgt_sb = sems(
            "hid0_mm hid0_sb y0_mm y0_s acc_s scat_s xg_in xgt_mm xgt_sb")
        hid_mm, hid_sb_act, hid_sb_dve, yt_mm, yt_sb, yr_mm, yr_sb, y_out, gath_s, res_s, out_s = sems(
            "hid_mm hid_sb_act hid_sb_dve yt_mm yt_sb yr_mm yr_sb y_out gath_s res_s out_s")

        block = ctx.enter_context(nc.Block())

        def before_d1(k, b, d2_s, dl_s):
            if isinstance(k, int) and k < 2:
                return d2_s, k
            return dl_s, k - 1

        def rows_after(e):
            full = [j for j in range(ST) if min((j + 1) * P, SLOTS) <= e * CAP1]
            return [j for j in full if min((j + 1) * P, SLOTS) > (e - 1) * CAP1]

        def tile_of(w, n):
            return w[:, bass.ds(n, 1), :].rearrange("p a d -> p (a d)")

        @block.sync
        def _(sp):
            sp.dma_start(x_in[:, :], x[0]).then_inc(x_in_s, 16)
            sp.dma_start(wq2[:, :], L0_xattn_Wq2).then_inc(wq2_in, 16)
            sp.dma_start(wk1[:, :], L0_xattn_Wk1).then_inc(wk1_in, 16)
            sp.dma_start(wv1[:, :], L0_xattn_Wv1).then_inc(wv1_in, 16)
            sp.dma_start(wq1[:, :], L0_xattn_Wq1).then_inc(wq1_in, 16)
            sp.dma_start(wk2[:, :], L0_xattn_Wk2).then_inc(wk2_in, 16)
            sp.dma_start(wv2[:, :], L0_xattn_Wv2).then_inc(wv2_in, 16)
            sp.dma_start(wk[:, :], L1_xattn_Wk).then_inc(late_a_in, 16)
            sp.dma_start(wout[:, :, :], L0_xattn_Wout.rearrange("(c p) n -> p c n", p=P)).then_inc(late_a_in, 16)
            sp.dma_start(wv[:, :], L1_xattn_Wv).then_inc(late_a_in, 16)
            sp.dma_start(be_b[:, :], L0_ffn_be.rearrange("(a d) -> a d", a=1).broadcast_to([P, D])).then_inc(stage_b_in, 16)
            sp.dma_start(we_wg[:, 0:D], L0_ffn_We).then_inc(stage_b_in, 16)
            sp.dma_start(we_wg[:, D:D + E], L0_ffn_Wg).then_inc(stage_b_in, 16)
            sp.dma_start(bo_b[:, :], L1_xattn_bo.rearrange("(a d) -> a d", a=1).broadcast_to([P, D])).then_inc(stage_b_in, 16)
            sp.dma_start(wq[:, :], L1_xattn_Wq).then_inc(stage_b_in, 16)
            sp.dma_start(wo[:, :, :], L1_xattn_Wo.rearrange("(c p) n -> p c n", p=P)).then_inc(stage_b_in, 16)
            sp.dma_start(b20_b[:, :], L1_ffn_b2[0:1, :].broadcast_to([P, D])).then_inc(w2_in, 16)
            w1_d = L1_ffn_W1.rearrange("e p f -> p e f")
            w2_d = L1_ffn_W2.rearrange("e (c p) n -> p e c n", p=P)
            sp.dma_start(w1[:, 0, :], w1_d[:, 0, :]).then_inc(w1_in, 16)
            sp.dma_start(w2[:, 0, :, :], w2_d[:, 0, :, :]).then_inc(w2_in, 16)
            with sp.Fori(1, NT) as n:
                sp.wait_ge(n_xn, n)
                sp.wait_ge(xb_s, n)
                sp.dma_start(x_in[:, :], x[bass.ds(n, 1)].rearrange("a p d -> (a p) d")).then_inc(x_in_s, 16)
                sp.wait_ge(n_mm, n)
                sp.dma_start(ctx_in[:, :], ctx_1024[bass.ds(n, 1)].rearrange("a p d -> (a p) d")).then_inc(ctx_in_s, 16)
                sp.dma_start(w1[:, bass.ds(n, 1), :].rearrange("p a f -> p (a f)"),
                             w1_d[:, bass.ds(n, 1), :].rearrange("p a f -> p (a f)")).then_inc(w1_in, 16)
                sp.dma_start(w2[:, bass.ds(n, 1), :, :].rearrange("p a c n -> p (a c) n"),
                             w2_d[:, bass.ds(n, 1), :, :].rearrange("p a c n -> p (a c) n")).then_inc(w2_in, 16)
            sp.wait_ge(scat_s, 16 * NT)
            for j in range(3):
                sp.dma_start(xg[:, 3 * j:3 * j + 3, :],
                             xg_dram.rearrange("(j p) d -> p j d", p=P)[:, 3 * j:3 * j + 3, :]).then_inc(xg_in, 16)
            y_v = y_dram.rearrange("(j p) d -> p j d", p=P)
            for j in range(3):
                sp.wait_ge(yr_sb, 3 * j + 3)
                sp.dma_start(y_v[:, 3 * j:3 * j + 3, :], y_rows[:, 3 * j:3 * j + 3, :]).then_inc(y_out, 16)
            for g in range(2):
                sp.wait_ge(res_s, g + 1)
                sp.dma_start(out.rearrange("t p d -> p t d")[:, 4 * g:4 * g + 4, :],
                             res[:, 4 * g:4 * g + 4, :]).then_inc(out_s, 16)
            sp.wait_ge(out_s, 32)

        @block.gpsimd
        def _(pool):
            nc.gpsimd.memset(ident[:, :], 0.0).then_inc(const_s, 1)
            nc.gpsimd.memset(ones[:, :], 1.0).then_inc(const_s, 1)
            nc.gpsimd.memset(minus_half[:, :], -0.5).then_inc(const_s, 1)
            nc.gpsimd.memset(eps_col[:, :], EPS).then_inc(const_s, 1)
            pool.wait_ge(const_s, 4)
            nc.gpsimd.affine_select(out=ident[:, :], in_=ident[:, :], compare_op=ALU.not_equal, fill=1.0, base=0,
                                    pattern=[[-1, P]], channel_multiplier=1).then_inc(const_s, 1)

            def rstd(mv, r, mv_s, r_s, n):
                pool.wait_ge(mv_s, both(n))
                nc.gpsimd.tensor_tensor(r[:, 0:1], mv[:, 1:2], eps_col[:, :], ALU.add).then_inc(r_s, 1)
                pool.wait_ge(r_s, both(n) - 1)
                nc.gpsimd.tensor_tensor(r[:, 1:2], r[:, 0:1], minus_half[:, :], ALU.pow).then_inc(r_s, 1)

            def residual(k):
                pool.wait_ge(x_in_s, 16 * (k + 1))
                nc.gpsimd.tensor_tensor(xb[:, :], x_in[:, :], bout_b[:, :], ALU.add).then_inc(xb_s, 1)

            rstd(mv_n, rstd_n, n_mv, n_rstd, 1)
            pool.dma_start(alpha[:, 0:1], L0_xattn_alpha_attn.rearrange("(a b) -> a b", a=1).broadcast_to([P, 1])).then_inc(alpha_in, 16)
            for w in (v1, v2, vl):
                last = nc.gpsimd.memset(w[:, :, DH:DH + 1], 1.0)
                last.then_inc(const_s, 1)
            nc.gpsimd.affine_select(out=before[:, :], in_=ones[:, :], compare_op=ALU.is_gt, fill=0.0, base=0,
                                    pattern=[[1, P]], channel_multiplier=-1).then_inc(const_s, 1)
            nc.gpsimd.memset(pick_sum[:, :], 0.0).then_inc(const_s, 1)
            for e in range(E):
                nc.gpsimd.memset(first_first[:, e:e + 1], float(E - e)).then_inc(const_s, 1)
                nc.gpsimd.memset(place_base[:, e:e + 1], float((e - 1) * CAP1)).then_inc(const_s, 1)
            pool.wait_ge(bout_in, 16)
            residual(0)

            def step(k, a, b, c, nxt):
                nA, nB, nC = k + 1, k, k - 1
                if c:
                    rstd(mv_c, rstd_c, c_mv, c_rstd, nC)
                    pool.wait_ge(x3_s, nC)
                    nc.gpsimd.tensor_copy(tile_of(x3_all, k - 2), x3[:, :]).then_inc(x3_all_s, 1)
                if nxt:
                    rstd(mv_n, rstd_n, n_mv, n_rstd, k + 2)
                if c:
                    pool.wait_ge(c_h, nC)
                    nc.gpsimd.tensor_copy(tile_of(h_all, k - 2), h_c[:, :]).then_inc(h_all_s, 1)
                if b:
                    pool.wait_ge(loc_mm, nB)
                    nc.gpsimd.tensor_tensor(pick_sum[:, :], pick_sum[:, :], pick[:, :], ALU.add).then_inc(pick_sum_s, 1)
                    rstd(mv_2, rstd_2, b2_mv, b2_rstd, nB)
                    pool.wait_ge(x2_s, nB)
                    nc.gpsimd.tensor_tensor(xb2[:, :], x2[:, :], bo_b[:, :], ALU.add).then_inc(xb2_s, 1)
                if c:
                    pool.wait_ge(ct_sb, nC)
                    nc.gpsimd.tensor_copy(ht_all[:, bass.ts(k - 2, P)], h_ct[:, :]).then_inc(ht_all_s, 1)
                if a:
                    rstd(mv_b, rstd_b, b_mv, b_rstd, nA)
                if nxt:
                    pool.wait_ge(x1_s, nA)
                    residual(k + 1)

            step(0, True, False, False, True)
            nc.gpsimd.memset(zeros[:, :], 0.0).then_inc(const_s, 1)
            nc.gpsimd.memset(y_back[:, :, :], 0.0).then_inc(const_s, 1)
            pool.wait_ge(const_s, 11 + 2 * E)
            pool.dma_start(xg_dram.rearrange("(p j) d -> p (j d)", p=P), zeros[:, :]).then_inc(xg_zero_in, 16)
            pool.wait_ge(stage_b_in, 96)
            step(1, True, True, False, True)
            with pool.Fori(2, NT - 1) as k:
                step(k, True, True, True, True)
            step(NT - 1, True, True, True, False)
            step(NT, False, True, True, False)
            step(NT + 1, False, False, True, False)

            pool.wait_ge(f_idx, 1)
            pool.wait_ge(xg_zero_in, 16)
            pool.wait_ge(h_all_s, NT)
            for t in range(NT):
                nc.gpsimd.indirect_dma_start(
                    out=xg_dram, out_offset=bass.IndirectOffsetOnAxis(ap=r_idx[:, t:t + 1], axis=0),
                    in_=h_all[:, t, :], in_offset=None, bounds_check=SLOTS - 1, oob_is_err=False).then_inc(scat_s, 16)
            pool.wait_ge(y_out, 48)
            pool.wait_ge(const_s, 12 + 2 * E)
            for t in range(NT):
                nc.gpsimd.indirect_dma_start(
                    out=y_back[:, t, :], out_offset=None, in_=y_dram,
                    in_offset=bass.IndirectOffsetOnAxis(ap=r_idx[:, t:t + 1], axis=0),
                    bounds_check=SLOTS - 1, oob_is_err=False).then_inc(gath_s, 16)
            pool.wait_ge(gath_s, 16 * NT)

        @block.scalar
        def _(act):
            act.dma_start(ctx_in[:, :], ctx_1024[0]).then_inc(ctx_in_s, 16)
            act.dma_start(bout_b[:, :], L0_xattn_bout.rearrange("(a d) -> a d", a=1).broadcast_to([P, D])).then_inc(bout_in, 16)
            act.dma_start(rw_rows[:, :], L1_ffn_router_w).then_inc(small_in, 16)
            act.dma_start(b1_rows[:, :], L1_ffn_b1.rearrange("e (c p) -> (e c) p", p=P)).then_inc(small_in, 16)
            act.dma_start(b2_rows[:, :], L1_ffn_b2).then_inc(small_in, 16)

            def out_of_psum(dst, src, mm, done, n):
                act.wait_ge(mm, n)
                nc.scalar.copy(dst, src).then_inc(done, 1)

            def exp_half(par, sub, tmm_before, n_before, done, n):
                act.wait_ge(sub, half(n, par))
                if not (isinstance(n_before, int) and n_before == 0):
                    act.wait_ge(tmm_before, half(n_before, par))
                nc.scalar.activation(probs[:, par, :, :], shifted[:, par, :, :], ACT.Exp, scale=SCALE).then_inc(done, 1)

            out_of_psum(xc_t[:, :, :], chunks(t_odd)[:, 0:2, :], n_mm, n_sb, 1)
            act.wait_ge(alpha_in, 16)
            nc.scalar.activation(alpha[:, 1:2], alpha[:, 0:1], ACT.Exp, scale=-1.0).then_inc(alpha_exp, 1)

            def step(k, a, b, c, nxt):
                nA, nB, nC = k + 1, k, k - 1
                if a:
                    out_of_psum(q2[:, :, :], chunks(m1), q2_mm, q2_sb, nA)
                if b:
                    out_of_psum(h_bt[:, :], t_even[:, 0:P], bt_mm, bt_sb, nB)
                if a:
                    out_of_psum(k1[:, :, :], chunks(m0), k1_mm, k1_sb, nA)
                if b:
                    act.wait_ge(g_less, nB)
                    nc.scalar.activation(lg[:, 1, :], lg[:, 0, :], ACT.Exp, accum_out=gate[:, 1:2]).then_inc(g_exp, 1)
                if c:
                    out_of_psum(h_ct[:, :], t_even[:, 0:P], ct_mm, ct_sb, nC)
                if a:
                    out_of_psum(v1[:, :, 0:DH], m1[:, :].rearrange("p (h d) -> p h d", h=H), v1_mm, v1_sb, nA)
                    exp_half(0, d1_sub, *before_d1(k, b, d2_tmm, dl_tmm), d1_exp, nA)
                    out_of_psum(q1[:, :, :], chunks(m0), q1_mm, q1_sb, nA)
                if c:
                    out_of_psum(lg_all[:, bass.ds(k - 2, 1), :].rearrange("p a e -> p (a e)"), o_even[:, 0:E], cl_mm, cl_s, nC)
                if a:
                    exp_half(1, d1_sub, *before_d1(k, b, d2_tmm, dl_tmm), d1_exp, nA)
                    out_of_psum(k2[:, :, :], chunks(m1), k2_mm, k2_sb, nA)
                    out_of_psum(v2[:, :, 0:DH], m0[:, :].rearrange("p (h d) -> p h d", h=H), v2_mm, v2_sb, nA)
                if b:
                    out_of_psum(h_2t[:, :], m1[:, 0:P], b2t_mm, b2t_sb, nB)
                if a:
                    for par in range(2):
                        out_of_psum(probs_t[:, par, :, :], chunks(t_bank[par]), d1_tmm, d1_tsb, half(nA, par))
                    exp_half(0, d2_sub, d1_tmm, nA, d2_exp, nA)
                if b:
                    out_of_psum(ql[:, :, :], chunks(m0), ql_mm, ql_sb, nB)
                if a:
                    exp_half(1, d2_sub, d1_tmm, nA, d2_exp, nA)
                    for par in range(2):
                        out_of_psum(probs_t[:, par, :, :], chunks(t_bank[par]), d2_tmm, d2_tsb, half(nA, par))
                if b:
                    for par in range(2):
                        exp_half(par, dl_sub, *((d2_tmm, nA) if a else (dl_tmm, nB - 1)), dl_exp, nB)
                if a:
                    out_of_psum(kl[:, :, :], chunks(m1), kl_mm, kl_sb, nA)
                if b:
                    for par in range(2):
                        out_of_psum(probs_t[:, par, :, :], chunks(t_bank[par]), dl_tmm, dl_tsb, half(nB, par))
                if a:
                    out_of_psum(att_at[:, :, :], chunks(m0), aot_mm, aot_sb, nA)
                    out_of_psum(vl[:, :, 0:DH], m0[:, :].rearrange("p (h d) -> p h d", h=H), vl_mm, vl_sb, nA)
                if b:
                    out_of_psum(att_bt[:, :, :], chunks(m1), bot_mm, bot_sb, nB)
                if nxt:
                    out_of_psum(xc_t[:, :, :], chunks(t_odd)[:, 0:2, :], n_mm, n_sb, k + 2)

            act.wait_ge(const_s, 8)
            step(0, True, False, False, True)
            step(1, True, True, False, True)
            with act.Fori(2, NT - 1) as k:
                step(k, True, True, True, True)
            step(NT - 1, True, True, True, False)
            step(NT, False, True, True, False)
            step(NT + 1, False, False, True, False)

            def hidden0(u):
                c, g = u // 2, u % 2
                act.wait_ge(hid0_mm, u + 1)
                nc.scalar.activation(hid0[:, c, g * HALF:(g + 1) * HALF], (m0, m1)[u % 2][:, :], ACT.Relu,
                                     bias=b1_t[:, c:c + 1]).then_inc(hid0_sb, 1)

            act.wait_ge(f_less, 1)
            nc.scalar.activation(r_exp[:, :, :], r_less[:, :, :], ACT.Exp).then_inc(f_exp, 1)
            hidden0(0)
            hidden0(1)
            for g in range(2):
                act.wait_ge(row_mm, g + 1)
                nc.scalar.copy(prob_row[:, g * HALF:(g + 1) * HALF], (t_even, t_odd)[g][:, :]).then_inc(row_sb, 1)
            for u in range(2, 2 * FC):
                hidden0(u)
            for j in range(3):
                act.wait_ge(xgt_mm, j + 1)
                w = min(512, ST * P - 384 * j, 384)
                nc.scalar.copy(xg_t[:, 384 * j:384 * j + w], (t_even, t_odd, o_even)[j][:, 0:w]).then_inc(xgt_sb, 1)

            def hidden(e):
                act.wait_ge(hid_mm, 2 * (e - 1) + 1)
                for c in range(2):
                    last = nc.scalar.activation(hid[:, e % 2, c, :], (m0, s_even)[e % 2][:, c * CAP1:(c + 1) * CAP1],
                                                ACT.Relu, bias=b1_t[:, e * FC + c:e * FC + c + 1])
                last.then_inc(hid_sb_act, 1)

            def expert_out(e):
                act.wait_ge(yt_mm, e)
                nc.scalar.activation(y_t[:, (e - 1) * CAP1:e * CAP1], (t_even, t_odd)[e % 2][:, 0:CAP1], ACT.Identity,
                                     bias=b2_t[:, e:e + 1]).then_inc(yt_sb, 1)

            for e in range(1, E):
                hidden(e)
                if e > 1:
                    expert_out(e - 1)
            expert_out(E - 1)

        @block.vector
        def _(dve):
            V = nc.vector

            def stats(src, stat, mv, mv_s, n):
                V.bn_stats(stat[:, :], src).then_inc(mv_s, 1)
                dve.wait_ge(mv_s, both(n) - 1)
                V.tensor_copy(carrier[:, :], stat[:, 0:1])
                V.bn_aggr(mv[:, :], stat[:, :]).then_inc(mv_s, 1)

            def normed(dst, src, mv, r, r_s, done, n):
                dve.wait_ge(r_s, both(n))
                V.tensor_scalar(dst, src, mv[:, 0:1], r[:, 1:2], ALU.subtract, ALU.mult).then_inc(done, 1)

            def shift(mm, mx, sub, exp_before, n_before, n):
                dve.wait_ge(mm, n)
                for par in range(2):
                    s = chunks(s_bank[par])
                    V.tensor_reduce(top[:, par, :], s, AX.X, ALU.max).then_inc(mx, 1)
                    dve.wait_ge(mx, half(n, par))
                    if not (isinstance(n_before, int) and n_before == 0):
                        dve.wait_ge(exp_before, half(n_before, par))
                    V.tensor_tensor(shifted[:, par, :, :], s, top[:, par, :].unsqueeze(2).broadcast_to([P, C, P]),
                                    ALU.subtract).then_inc(sub, 1)

            def scaled(par, dst, omm, rec, done, n, by):
                o = heads_out(o_bank[par])
                dve.wait_ge(omm, half(n, par))
                V.reciprocal(rsum[:, par, :], o[:, :, DH]).then_inc(rec, 1)
                dve.wait_ge(rec, half(n, par))
                V.scalar_tensor_tensor(out=dst[:, :, par, :], in0=o[:, :, 0:DH], scalar=by,
                                       in1=rsum[:, par, :].unsqueeze(2).broadcast_to([P, C, DH]),
                                       op0=ALU.mult, op1=ALU.mult).then_inc(done, 1)

            dve.wait_ge(x_in_s, 16)
            stats(x_in[:, :], stat_n, mv_n, n_mv, 1)
            normed(xn[:, :], x_in[:, :], mv_n, rstd_n, n_rstd, n_xn, 1)
            dve.wait_ge(alpha_exp, 1)
            V.tensor_scalar(alpha[:, 1:2], alpha[:, 1:2], 1.0, None, ALU.add).then_inc(alpha_s, 1)
            dve.wait_ge(alpha_s, 1)
            V.reciprocal(alpha[:, 2:3], alpha[:, 1:2]).then_inc(alpha_s, 1)
            dve.wait_ge(alpha_s, 2)
            V.tensor_scalar(alpha[:, 3:4], alpha[:, 2:3], -1.0, 1.0, ALU.mult, ALU.add).then_inc(alpha_s, 1)
            dve.wait_ge(rw_mm, 1)
            V.tensor_copy(rw_t[:, :], o_even[:, 0:E]).then_inc(small_s, 1)
            V.tensor_copy(b1_t[:, :], o_even[:, 64:64 + E * FC]).then_inc(small_s, 1)
            V.tensor_copy(b2_t[:, :], o_even[:, 128:128 + E]).then_inc(small_s, 1)

            def step(k, a, b, c, nxt):
                nA, nB, nC = k + 1, k, k - 1
                if c:
                    normed(h_c[:, :], x3[:, :], mv_c, rstd_c, c_rstd, c_h, nC)
                if b:
                    dve.wait_ge(y_mm, nB)
                    V.tensor_reduce(gate[:, 0:1], t_odd[:, D:D + E], AX.X, ALU.max).then_inc(g_max, 1)
                    dve.wait_ge(g_max, nB)
                    V.tensor_scalar(lg[:, 0, :], t_odd[:, D:D + E], gate[:, 0:1], None, ALU.subtract).then_inc(g_less, 1)
                    V.tensor_tensor(ybe[:, :], t_odd[:, 0:D], be_b[:, :], ALU.add).then_inc(y_s, 1)
                    dve.wait_ge(g_less, nB)
                    V.scalar_tensor_tensor(out=lg[:, 2, :], in0=lg[:, 0, :], scalar=0.0, in1=first_first[:, :],
                                           op0=ALU.is_ge, op1=ALU.mult).then_inc(g_mark, 1)
                    dve.wait_ge(g_mark, nB)
                    V.tensor_reduce(gate[:, 3:4], lg[:, 2, :], AX.X, ALU.max).then_inc(g_first, 1)
                    dve.wait_ge(g_first, nB)
                    dve.wait_ge(pick_sum_s, nB - 1)
                    V.tensor_scalar(pick[:, :], lg[:, 2, :], gate[:, 3:4], None, ALU.is_equal).then_inc(g_pick, 1)
                if nxt:
                    dve.wait_ge(x_in_s, 16 * (k + 2))
                    stats(x_in[:, :], stat_n, mv_n, n_mv, k + 2)
                if a:
                    shift(d1_mm, d1_max, d1_sub, *before_d1(k, b, d2_exp, dl_exp), nA)
                if b:
                    dve.wait_ge(g_exp, nB)
                    V.reciprocal(gate[:, 2:3], gate[:, 1:2]).then_inc(g_gate, 1)
                    dve.wait_ge(loc_mm, nB)
                    dve.wait_ge(g_pick, nB)
                    V.scalar_tensor_tensor(out=kept[:, :], in0=o_odd[:, 0:E], scalar=float(CAP0), in1=pick[:, :],
                                           op0=ALU.is_lt, op1=ALU.mult, accum_out=gate[:, 4:5]).then_inc(g_kept, 1)
                    dve.wait_ge(g_kept, nB)
                    dve.wait_ge(g_gate, nB)
                    V.tensor_tensor(gate[:, 5:6], gate[:, 4:5], gate[:, 2:3], ALU.mult).then_inc(g_kgate, 1)
                    dve.wait_ge(g_kgate, nB)
                    dve.wait_ge(y_s, nB)
                    V.scalar_tensor_tensor(out=x2[:, :], in0=ybe[:, :], scalar=gate[:, 5:6], in1=x1[:, :],
                                           op0=ALU.mult, op1=ALU.add).then_inc(x2_s, 1)
                    dve.wait_ge(x2_s, nB)
                    stats(x2[:, :], stat_2, mv_2, b2_mv, nB)
                if nxt:
                    normed(xn[:, :], x_in[:, :], mv_n, rstd_n, n_rstd, n_xn, k + 2)
                if b:
                    normed(h_2[:, :], x2[:, :], mv_2, rstd_2, b2_rstd, b2_h, nB)
                if a:
                    shift(d2_mm, d2_max, d2_sub, d1_exp, nA, nA)
                    for par in range(2):
                        scaled(par, att_a, d1_omm, d1_rec, d1_out, nA, alpha[:, 2:3])
                if b:
                    shift(dl_mm, dl_max, dl_sub, *((d2_exp, nA) if a else (dl_exp, nB - 1)), nB)
                if a:
                    for par in range(2):
                        scaled(par, att_a2, d2_omm, d2_rec, d2_out, nA, alpha[:, 3:4])
                    dve.wait_ge(d2_out, both(nA))
                    V.tensor_tensor(att_a[:, :, :, :].rearrange("p c a d -> p (c a d)"),
                                    att_a[:, :, :, :].rearrange("p c a d -> p (c a d)"),
                                    att_a2[:, :, :, :].rearrange("p c a d -> p (c a d)"), ALU.add).then_inc(att_s, 1)
                if b:
                    for par in range(2):
                        scaled(par, att_b, dl_omm, dl_rec, dl_out, nB, 1.0)
                if a:
                    dve.wait_ge(x1_mm, nA)
                    dve.wait_ge(xb_s, nA)
                    V.tensor_tensor(x1[:, :], m1[:, 0:D], xb[:, :], ALU.add).then_inc(x1_s, 1)
                    dve.wait_ge(x1_s, nA)
                    stats(x1[:, :], stat_b, mv_b, b_mv, nA)
                    normed(h_b[:, :], x1[:, :], mv_b, rstd_b, b_rstd, b_h, nA)
                if b:
                    dve.wait_ge(x3_mm, nB)
                    dve.wait_ge(xb2_s, nB)
                    if c:
                        dve.wait_ge(x3_all_s, nC)
                    V.tensor_tensor(x3[:, :], m0[:, 0:D], xb2[:, :], ALU.add).then_inc(x3_s, 1)
                    dve.wait_ge(x3_s, nB)
                    stats(x3[:, :], stat_c, mv_c, c_mv, nB)

            dve.wait_ge(const_s, 10 + 2 * E)
            step(0, True, False, False, True)
            dve.wait_ge(stage_b_in, 96)
            step(1, True, True, False, True)
            with dve.Fori(2, NT - 1) as k:
                step(k, True, True, True, True)
            step(NT - 1, True, True, True, False)
            step(NT, False, True, True, False)
            step(NT + 1, False, False, True, False)

            def per_tile(w):
                return w[:, :].unsqueeze(2).broadcast_to([P, NT, E])

            def per_expert(w):
                return w[:, :].unsqueeze(1).broadcast_to([P, NT, E])

            chain = [0]

            def done(ins):
                chain[0] += 1
                ins.then_inc(f_dve, 1)
                dve.wait_ge(f_dve, chain[0])

            dve.wait_ge(cl_s, NT)
            done(V.tensor_reduce(r_max[:, :], lg_all[:, :, :], AX.X, ALU.max))
            V.tensor_tensor(r_less[:, :, :], lg_all[:, :, :], per_tile(r_max), ALU.subtract).then_inc(f_less, 1)
            dve.wait_ge(f_exp, 1)
            done(V.tensor_reduce(r_sum[:, :], r_exp[:, :, :], AX.X, ALU.add))
            V.reciprocal(r_prob[:, :], r_sum[:, :]).then_inc(f_prob, 1)
            done(V.tensor_scalar(r_tmp[:, :, :], r_less[:, :, :], 0.0, None, ALU.is_ge))
            done(V.tensor_tensor(r_mark[:, :, :], r_tmp[:, :, :], per_expert(first_first), ALU.mult))
            done(V.tensor_reduce(r_first[:, :], r_mark[:, :, :], AX.X, ALU.max))
            V.tensor_tensor(r_pick[:, :, :], r_mark[:, :, :], per_tile(r_first), ALU.is_equal).then_inc(f_pick, 1)
            dve.wait_ge(f_pick, 1)
            done(V.tensor_tensor(r_tmp2[:, :, :], r_pick[:, :, :], per_expert(place_base), ALU.mult))
            done(V.tensor_reduce(r_base[:, :], r_tmp2[:, :, :], AX.X, ALU.add))
            dve.wait_ge(row_sb, 2)
            dve.wait_ge(f_prob, 1)
            dve.wait_ge(const_s, 9)
            for t in range(NT):
                w = (t + 1) * P
                V.tensor_scalar(ahead[:, t, 0:w], prob_row[:, 0:w], r_prob[:, t:t + 1], None, ALU.is_lt)
                if w < T:
                    V.tensor_scalar(ahead[:, t, w:T], prob_row[:, w:T], r_prob[:, t:t + 1], None, ALU.is_le)
                V.scalar_tensor_tensor(out=ties[:, t, :], in0=prob_row[:, t * P:w], scalar=r_prob[:, t:t + 1],
                                       in1=before[:, :], op0=ALU.is_equal, op1=ALU.mult).then_inc(ahead_s, 1)
            dve.wait_ge(rank_mm, 1)
            done(V.tensor_tensor(r_tmp[:, :, :], s_even[:, 0:NT * E].rearrange("p (t e) -> p t e", t=NT),
                                 r_pick[:, :, :], ALU.mult))
            done(V.tensor_reduce(r_pos[:, :], r_tmp[:, :, :], AX.X, ALU.add))
            V.tensor_tensor(r_slot[:, :], r_pos[:, :], r_base[:, :], ALU.add)
            done(V.tensor_scalar(r_pos[:, :], r_pos[:, :], float(CAP1), None, ALU.is_ge))
            V.tensor_tensor(r_out[:, :], r_pos[:, :], r_pick[:, :, 0], ALU.max).then_inc(f_out, 1)
            dve.wait_ge(f_out, 1)
            V.scalar_tensor_tensor(out=r_idx[:, :], in0=r_out[:, :], scalar=FAR, in1=r_slot[:, :],
                                   op0=ALU.mult, op1=ALU.add).then_inc(f_idx, 1)
            dve.wait_ge(w2_in, 16 * (NT + 1))
            dve.wait_ge(x3_all_s, NT)
            for g in range(2):
                dve.wait_ge(y0_mm, g + 1)
                a = acc[:, 4 * g:4 * g + 4, :]
                V.tensor_tensor(a, chunks((s_odd, o_odd)[g]), b20_b[:, :].unsqueeze(1).broadcast_to([P, 4, D]),
                                ALU.add).then_inc(y0_s, 1)
                dve.wait_ge(y0_s, g + 1)
                done(V.tensor_tensor(a, a, r_out[:, 4 * g:4 * g + 4].unsqueeze(2).broadcast_to([P, 4, D]), ALU.mult))
                V.tensor_tensor(a, a, x3_all[:, 4 * g:4 * g + 4, :], ALU.add).then_inc(acc_s, 1)

            def hidden(e):
                dve.wait_ge(hid_mm, 2 * (e - 1) + 2)
                for c in range(2):
                    last = V.tensor_scalar(hid[:, e % 2, 2 + c, :], (m1, s_odd)[e % 2][:, c * CAP1:(c + 1) * CAP1],
                                           b1_t[:, e * FC + 2 + c:e * FC + 3 + c], 0.0, ALU.add, ALU.max)
                last.then_inc(hid_sb_dve, 1)

            def rows_out(j):
                dve.wait_ge(yr_mm, j + 1)
                V.tensor_copy(y_rows[:, j, :], (o_even, o_odd)[j % 2][:, 0:D]).then_inc(yr_sb, 1)

            for e in range(1, E):
                hidden(e)
                for j in rows_after(e - 2):
                    rows_out(j)
            for e in (E - 2, E - 1):
                for j in rows_after(e):
                    rows_out(j)
            dve.wait_ge(gath_s, 16 * NT)
            dve.wait_ge(acc_s, 2)
            for g in range(2):
                V.tensor_tensor(res[:, 4 * g:4 * g + 4, :], acc[:, 4 * g:4 * g + 4, :], y_back[:, 4 * g:4 * g + 4, :],
                                ALU.add).then_inc(res_s, 1)

        @block.tensor
        def _(pe):
            mm = nc.tensor.matmul
            turn = nc.tensor.transpose
            xn_t, c_t = xc_t[:, 0, :], xc_t[:, 1, :]

            def project(bank, w, src, done):
                for c in range(C):
                    last = mm(chunks(bank)[:, c, :], w[:, c * P:(c + 1) * P], src, start=True, stop=True)
                last.then_inc(done, 1)

            def project_rows(bank, w, src, done):
                mm(bank[:, :], src, w[:, :], start=True, stop=True).then_inc(done, 1)

            def scores(q, kk, done):
                for c in range(C):
                    for par in range(2):
                        rows = slice(par * DH, (par + 1) * DH)
                        last = mm(chunks(s_bank[par])[:, c, :], q[rows, c, :], kk[rows, c, :], start=True, stop=True)
                last.then_inc(done, 1)

            def turn_probs(exp_s, tsb_before, n_before, done, n):
                for par in range(2):
                    pe.wait_ge(exp_s, half(n, par))
                    if not (isinstance(n_before, int) and n_before == 0):
                        pe.wait_ge(tsb_before, half(n_before, par))
                    for c in range(C):
                        last = turn(chunks(t_bank[par])[:, c, :], probs[:, par, c, :], ident[:, :])
                    last.then_inc(done, 1)

            def weigh(v, tsb, out_before, n_before, done, n):
                for par in range(2):
                    pe.wait_ge(tsb, half(n, par))
                    if not (isinstance(n_before, int) and n_before == 0):
                        pe.wait_ge(out_before, half(n_before, par))
                    for c in range(C):
                        last = mm(heads_out(o_bank[par])[:, c, :], probs_t[:, par, c, :], v[:, 2 * c + par, :],
                                  start=True, stop=True)
                    last.then_inc(done, 1)

            def turn_heads(bank, att, done):
                for c in range(C):
                    last = turn(chunks(bank)[:, c, :], att[:, c, :, :].rearrange("p a d -> p (a d)"), ident[:, :])
                last.then_inc(done, 1)

            def join_heads(bank, att_t, w, done):
                for c in range(C):
                    last = mm(bank[:, 0:D], att_t[:, c, :], w[:, c, :], start=(c == 0), stop=(c == C - 1))
                last.then_inc(done, 1)

            def turn_next(n):
                pe.wait_ge(ctx_in_s, 16 * n)
                turn(chunks(t_odd)[:, 1, :], ctx_in[:, :], ident[:, :])
                pe.wait_ge(n_xn, n)
                turn(chunks(t_odd)[:, 0, :], xn[:, :], ident[:, :]).then_inc(n_mm, 1)

            pe.wait_ge(const_s, 5)
            turn_next(1)
            pe.wait_ge(small_in, 48)
            turn(o_even[:, 0:E], rw_rows[:, :], ident[0:E, 0:E])
            turn(o_even[:, 64:64 + E * FC], b1_rows[:, :], ident[0:E * FC, 0:E * FC])
            turn(o_even[:, 128:128 + E], b2_rows[:, :], ident[0:E, 0:E]).then_inc(rw_mm, 1)

            def loaded(k, at, s, n=16):
                if isinstance(k, int) and k == at:
                    pe.wait_ge(s, n)

            def step(k, a, b, c, nxt):
                nA, nB, nC = k + 1, k, k - 1
                first, second = (isinstance(k, int) and k == n for n in (0, 1))
                if a:
                    loaded(k, 0, wq2_in)
                    if second:
                        pe.wait_ge(x1_s, 1)
                    pe.wait_ge(n_sb, nA)
                    project(m1, wq2, c_t, q2_mm)
                if b:
                    pe.wait_ge(b_h, nB)
                    if second:
                        pe.wait_ge(d2_tsb, both(1))
                    else:
                        pe.wait_ge(dl_tsb, both(nB - 1))
                    turn(t_even[:, 0:P], h_b[:, :], ident[:, :]).then_inc(bt_mm, 1)
                if a:
                    loaded(k, 0, wk1_in)
                    if second:
                        pe.wait_ge(vl_sb, 1)
                    elif not first:
                        pe.wait_ge(x3_s, nB - 1)
                    project(m0, wk1, xn_t, k1_mm)
                if b:
                    loaded(k, 1, stage_b_in, 96)
                    pe.wait_ge(bt_sb, nB)
                    mm(t_odd[:, 0:D + E], h_bt[:, :], we_wg[:, :], start=True, stop=True).then_inc(y_mm, 1)
                if a:
                    pe.wait_ge(q2_sb, nA)
                    pe.wait_ge(k1_sb, nA)
                    if second:
                        pe.wait_ge(d2_sub, both(1))
                    elif not first:
                        pe.wait_ge(dl_sub, both(nB - 1))
                    scores(q2, k1, d1_mm)
                if c:
                    pe.wait_ge(c_h, nC)
                    if b:
                        pe.wait_ge(bt_sb, nB)
                    else:
                        pe.wait_ge(dl_tsb, both(nB - 1))
                    turn(t_even[:, 0:P], h_c[:, :], ident[:, :]).then_inc(ct_mm, 1)
                if a:
                    loaded(k, 0, wv1_in)
                    pe.wait_ge(q2_sb, nA)
                    project_rows(m1, wv1, xn_t, v1_mm)
                    loaded(k, 0, wq1_in)
                    pe.wait_ge(k1_sb, nA)
                    project(m0, wq1, xn_t, q1_mm)
                if b:
                    pe.wait_ge(g_pick, nB)
                    if second:
                        pe.wait_ge(const_s, 10)
                        pe.wait_ge(d2_out, both(1))
                    else:
                        pe.wait_ge(dl_out, both(nB - 1))
                    mm(o_odd[:, 0:E], before[:, :], pick[:, :], start=True, stop=False)
                    pe.wait_ge(pick_sum_s, nB - 1)
                    mm(o_odd[:, 0:E], ones[:, :], pick_sum[:, :], start=False, stop=True).then_inc(loc_mm, 1)
                if c:
                    pe.wait_ge(ct_sb, nC)
                    pe.wait_ge(dl_out, both(nB - 1))
                    mm(o_even[:, 0:E], h_ct[:, :], rw_t[:, :], start=True, stop=True).then_inc(cl_mm, 1)
                if a:
                    loaded(k, 0, wk2_in)
                    pe.wait_ge(v1_sb, nA)
                    project(m1, wk2, c_t, k2_mm)
                    loaded(k, 0, wv2_in)
                    pe.wait_ge(q1_sb, nA)
                    project_rows(m0, wv2, c_t, v2_mm)
                    pe.wait_ge(k2_sb, nA)
                    pe.wait_ge(d1_sub, both(nA))
                    scores(q1, k2, d2_mm)
                if b:
                    pe.wait_ge(b2_h, nB)
                    if a:
                        pe.wait_ge(k2_sb, nA)
                    turn(m1[:, 0:P], h_2[:, :], ident[:, :]).then_inc(b2t_mm, 1)
                if b:
                    pe.wait_ge(y_s, nB)
                if c:
                    pe.wait_ge(ct_sb, nC)
                if a:
                    turn_probs(d1_exp, d1_exp, 0, d1_tmm, nA)
                if b:
                    pe.wait_ge(b2t_sb, nB)
                    if a:
                        pe.wait_ge(v2_sb, nA)
                    else:
                        pe.wait_ge(x3_s, nB - 1)
                    project(m0, wq, h_2t[:, :], ql_mm)
                if first:
                    pe.wait_ge(small_s, 3)
                if b:
                    pe.wait_ge(g_kept, nB)
                if c:
                    pe.wait_ge(cl_s, nC)
                if a:
                    weigh(v1, d1_tsb, d1_tsb, 0, d1_omm, nA)
                if b:
                    pe.wait_ge(ql_sb, nB)
                    if a:
                        pe.wait_ge(d2_sub, both(nA))
                    else:
                        pe.wait_ge(dl_sub, both(nB - 1))
                    scores(ql, kl, dl_mm)
                if a:
                    turn_probs(d2_exp, d1_tsb, nA, d2_tmm, nA)
                    weigh(v2, d2_tsb, d1_out, nA, d2_omm, nA)
                    loaded(k, 0, late_a_in, 48)
                    if b:
                        pe.wait_ge(b2t_sb, nB)
                    else:
                        pe.wait_ge(k2_sb, nA)
                    project(m1, wk, c_t, kl_mm)
                if b:
                    turn_probs(dl_exp, d2_tsb, nA if a else 0, dl_tmm, nB)
                if a:
                    pe.wait_ge(att_s, nA)
                    if b:
                        pe.wait_ge(ql_sb, nB)
                    else:
                        pe.wait_ge(v2_sb, nA)
                    turn_heads(m0, att_a, aot_mm)
                if b:
                    weigh(vl, dl_tsb, d2_out, nA if a else 0, dl_omm, nB)
                if a:
                    pe.wait_ge(aot_sb, nA)
                    pe.wait_ge(kl_sb, nA)
                    join_heads(m1, att_at, wout, x1_mm)
                    project_rows(m0, wv, c_t, vl_mm)
                if b:
                    pe.wait_ge(dl_out, both(nB))
                    if a:
                        pe.wait_ge(x1_s, nA)
                    turn_heads(m1, att_b, bot_mm)
                if nxt:
                    if b:
                        pe.wait_ge(dl_tsb, both(nB))
                    else:
                        pe.wait_ge(d2_tsb, both(nA))
                    turn_next(k + 2)
                if b:
                    pe.wait_ge(bot_sb, nB)
                    if a:
                        pe.wait_ge(vl_sb, nA)
                    join_heads(m0, att_bt, wo, x3_mm)

            step(0, True, False, False, True)
            step(1, True, True, False, True)
            with pe.Fori(2, NT - 1) as k:
                step(k, True, True, True, True)
            step(NT - 1, True, True, True, False)
            step(NT, False, True, True, False)
            step(NT + 1, False, False, True, False)

            def hidden0(u):
                c, g = u // 2, u % 2
                if u >= 2:
                    pe.wait_ge(hid0_sb, u - 1)
                mm((m0, m1)[u % 2][:, :], w1[:, 0, c * P:(c + 1) * P], ht_all[:, g * HALF:(g + 1) * HALF],
                   start=True, stop=True).then_inc(hid0_mm, 1)

            pe.wait_ge(w1_in, 16 * NT)
            pe.wait_ge(ht_all_s, NT)
            pe.wait_ge(cl_s, NT)
            pe.wait_ge(x3_s, NT)
            hidden0(0)
            hidden0(1)
            pe.wait_ge(f_prob, 1)
            pe.wait_ge(dl_tsb, both(NT))
            for t in range(NT):
                last = turn(chunks((t_even, t_odd)[t // 4])[:, t % 4, :], r_prob[:, t:t + 1].broadcast_to([P, P]), ident[:, :])
                if t % 4 == 3:
                    last.then_inc(row_mm, 1)
            for u in range(2, 2 * FC):
                hidden0(u)
            pe.wait_ge(f_pick, 1)
            pe.wait_ge(dl_sub, both(NT))
            for t in range(NT):
                pe.wait_ge(ahead_s, t + 1)
                for n in range(NT):
                    mm(s_even[:, n * E:(n + 1) * E], ahead[:, t, n * P:(n + 1) * P], r_pick[:, t, :],
                       start=(t == 0 and n == 0), stop=(t == NT - 1 and n != t), skip_group_check=True)
                last = mm(s_even[:, t * E:(t + 1) * E], ties[:, t, :], r_pick[:, t, :],
                          start=False, stop=True, skip_group_check=True)
            last.then_inc(rank_mm, 1)
            pe.wait_ge(w2_in, 16 * (NT + 1))
            pe.wait_ge(hid0_sb, 2 * FC)
            pe.wait_ge(dl_out, both(NT))
            for t in range(NT):
                for c in range(FC):
                    last = mm(chunks((s_odd, o_odd)[t // 4])[:, t % 4, :], hid0[:, c, t * P:(t + 1) * P], w2[:, 0, c, :],
                              start=(c == 0), stop=(c == FC - 1))
                if t % 4 == 3:
                    last.then_inc(y0_mm, 1)
            pe.wait_ge(row_sb, 2)
            for j in range(3):
                pe.wait_ge(xg_in, 48)
                for i in range(3):
                    last = turn(chunks((t_even, t_odd, o_even)[j])[:, i, :], xg[:, 3 * j + i, :], ident[:, :])
                last.then_inc(xgt_mm, 1)

            def hidden(e):
                for g in range(2):
                    if e > 2:
                        pe.wait_ge((hid_sb_act, hid_sb_dve)[g], e - 2)
                    bank = ((m0, m1), (s_even, s_odd))[e % 2][g]
                    for c in range(2):
                        f = 2 * g + c
                        last = mm(bank[:, c * CAP1:(c + 1) * CAP1], w1[:, e, f * P:(f + 1) * P],
                                  xg_t[:, (e - 1) * CAP1:e * CAP1], start=True, stop=True)
                    last.then_inc(hid_mm, 1)

            def expert_out(e):
                pe.wait_ge(hid_sb_act, e)
                pe.wait_ge(hid_sb_dve, e)
                if e > 2:
                    pe.wait_ge(yt_sb, e - 2)
                for c in range(FC):
                    last = mm((t_even, t_odd)[e % 2][:, 0:CAP1], w2[:, e, c, :], hid[:, e % 2, c, :],
                              start=(c == 0), stop=(c == FC - 1))
                last.then_inc(yt_mm, 1)

            def rows(e):
                for j in rows_after(e):
                    pe.wait_ge(yt_sb, e)
                    if j >= 2:
                        pe.wait_ge(yr_sb, j - 1)
                    w = min(P, SLOTS - j * P)
                    turn((o_even, o_odd)[j % 2][0:w, 0:D], y_t[:, j * P:j * P + w], ident[:, :]).then_inc(yr_mm, 1)

            pe.wait_ge(xgt_sb, 3)
            pe.wait_ge(f_idx, 1)
            pe.wait_ge(y0_s, 2)
            hidden(1)
            for e in range(2, E):
                hidden(e)
                expert_out(e - 1)
                if e > 2:
                    rows(e - 2)
            expert_out(E - 1)
            rows(E - 2)
            rows(E - 1)


_INS = ['x', 'ctx_1024', 'L0_xattn_Wq1', 'L0_xattn_Wk1', 'L0_xattn_Wv1', 'L0_xattn_Wq2', 'L0_xattn_Wk2', 'L0_xattn_Wv2',
        'L0_xattn_alpha_attn', 'L0_xattn_Wout', 'L0_xattn_bout', 'L0_ffn_Wg', 'L0_ffn_We', 'L0_ffn_be', 'L1_xattn_Wq',
        'L1_xattn_Wk', 'L1_xattn_Wv', 'L1_xattn_Wo', 'L1_xattn_bo', 'L1_ffn_router_w', 'L1_ffn_W1', 'L1_ffn_b1',
        'L1_ffn_W2', 'L1_ffn_b2']
_OUTS = [((8, 128, 128), 'float32')]


def kernel(**inputs):
    import numpy as _np
    import concourse.bacc as _bacc
    from concourse import mybir as _mybir
    from concourse.bass_utils import run_bass_kernel_spmd as _run

    nc = _bacc.Bacc("TRN2", target_bir_lowering=False, num_devices=1)
    arrays, args = {}, []
    for name in _INS:
        a = _np.ascontiguousarray(inputs[name])
        if a.ndim == 0:
            a = a.reshape(1)
        arrays[f"in_{name}_dram"] = a
        args.append(nc.dram_tensor(f"in_{name}_dram", a.shape, _mybir.dt.from_np(a.dtype), kind="ExternalInput").ap())
    for i, (shape, dtype) in enumerate(_OUTS):
        dt = _mybir.dt.from_np(_np.dtype(dtype))
        args.append(nc.dram_tensor(f"out_{i}_dram", shape, dt, kind="ExternalOutput").ap())
    two_layers(nc, *args)
    r = _run(nc, [arrays], core_ids=[0])
    got = tuple(r.results[0][f"out_{i}_dram"] for i in range(len(_OUTS)))
    return got[0]
```

```python
from contextlib import ExitStack

import concourse.bass as bass
from concourse import mybir

ALU = mybir.AluOpType
ACT = mybir.ActivationFunctionType
AX = mybir.AxisListType
F32 = mybir.dt.float32
BF16 = mybir.dt.bfloat16
I32 = mybir.dt.int32
U32 = mybir.dt.uint32

EPS = 1e-5


def two_layers(nc, x, ctx_1024, L0_xattn_Wq1, L0_xattn_Wk1, L0_xattn_Wv1, L0_xattn_Wq2, L0_xattn_Wk2,
               L0_xattn_Wv2, L0_xattn_alpha_attn, L0_xattn_Wout, L0_xattn_bout, L0_ffn_Wg, L0_ffn_We,
               L0_ffn_be, L1_xattn_Wq, L1_xattn_Wk, L1_xattn_Wv, L1_xattn_Wo, L1_xattn_bo,
               L1_ffn_router_w, L1_ffn_W1, L1_ffn_b1, L1_ffn_W2, L1_ffn_b2, out):
    NT, P, D = x.shape
    INNER = L0_xattn_Wq1.shape[1]
    DH = 64
    H = INNER // DH
    C = INNER // P
    E = L0_ffn_Wg.shape[1]
    FF = L1_ffn_W1.shape[2]
    FC = FF // P
    T = NT * P
    SCALE = float(DH) ** -0.5
    CAP0 = T // E
    CAP1 = -(-(T * 5) // (E * 4))
    SLOTS = (E - 1) * CAP1
    ST = -(-SLOTS // P)
    FAR = 8192.0
    ROW = 2 * D + 1
    HALF = T // 2
    assert P == 128 and D == 128 and C == 4 and H == 8 and E == 8

    ctx = ExitStack()
    with ctx:
        def sb(name, shape, dt=F32):
            return ctx.enter_context(nc.sbuf_tensor(name, shape, dt))

        def sems(names):
            return [ctx.enter_context(nc.semaphore(n)) for n in names.split()]

        m0, m1, s_even, s_odd, t_even, t_odd, o_a, o_b = [
            ctx.enter_context(nc.psum_tensor(n, [P, 512], F32))
            for n in ("m0", "m1", "s_even", "s_odd", "t_even", "t_odd", "o_a", "o_b")]
        s_bank, t_bank = (s_even, s_odd), (t_even, t_odd)

        def chunks(bank):
            return bank[:, :].rearrange("p (c n) -> p c n", c=C)

        ident = sb("ident", [P, P])
        ones = sb("ones", [P, P], BF16)
        before = sb("before", [P, P], BF16)
        first_first = sb("first_first", [P, E])
        place_base = sb("place_base", [P, E])
        minus_half = sb("minus_half", [P, 1])
        eps_col = sb("eps_col", [P, 1])
        carrier = sb("carrier", [P, 1])
        pool_carrier = sb("pool_carrier", [P, 1])
        token = sb("token", [P, NT])
        b20_x = sb("b20_x", [P, NT, D])
        no_rows = sb("no_rows", [P, ST, ROW])
        wq1, wk1, wv1, wq2, wk2, wv2, wq, wk, wv = [
            sb(n, [D, INNER]) for n in "wq1 wk1 wv1 wq2 wk2 wv2 wq wk wv".split()]
        wout = sb("wout", [P, C, D])
        wo = sb("wo", [P, C, D])
        we_wg = sb("we_wg", [D, D + E])
        rw_rows = sb("rw_rows", [E, D])
        rw_t = sb("rw_t", [D, E])
        w1 = sb("w1", [D, E, FF])
        w2 = sb("w2", [P, E, FC, D])
        b1_rows = sb("b1_rows", [E * FC, P])
        b1_t = sb("b1_t", [P, E * FC])
        b2_rows = sb("b2_rows", [E, D])
        b2_t = sb("b2_t", [D, E])
        bout_b, be_b, bo_b, b20_b = [sb(n, [P, D]) for n in "bout_b be_b bo_b b20_b".split()]
        alpha = sb("alpha", [P, 4])
        x_in = sb("x_in", [P, D])
        ctx_in = sb("ctx_in", [P, D])
        stat_n, mv_n, rstd_n = sb("stat_n", [P, 6]), sb("mv_n", [P, 2]), sb("rstd_n", [P, 2])
        xn = sb("xn", [P, D])
        xc_t = sb("xc_t", [D, 2, P])
        xb = sb("xb", [P, D])
        q1, k1, q2, k2 = [sb(n, [P, C, P]) for n in "q1 k1 q2 k2".split()]
        v1, v2 = [sb(n, [P, H, DH]) for n in "v1 v2".split()]
        probs = sb("probs", [P, 2, C, P])
        probs_t = sb("probs_t", [P, 2, C, P])
        low = sb("low", [P, 2, C])
        wsum = sb("wsum", [P, 2, C])
        rsum = sb("rsum", [P, 2, C])
        att_at = sb("att_at", [P, C, P])
        x1 = sb("x1", [P, D])
        stat_b, mv_b, rstd_b = sb("stat_b", [P, 6]), sb("mv_b", [P, 2]), sb("rstd_b", [P, 2])
        h_b = sb("h_b", [P, D])
        h_bt = sb("h_bt", [D, P])
        ybe = sb("ybe", [P, D])
        gate = sb("gate", [P, 8])
        lg = sb("lg", [P, 3, E])
        pick = sb("pick", [P, E], BF16)
        pick_sum = sb("pick_sum", [P, E], BF16)
        kept = sb("kept", [P, E])
        x2 = sb("x2", [P, D])
        stat_2, mv_2, rstd_2 = sb("stat_2", [P, 6]), sb("mv_2", [P, 2]), sb("rstd_2", [P, 2])
        h_2 = sb("h_2", [P, D])
        h_2t = sb("h_2t", [D, P])
        xb2 = sb("xb2", [P, D])
        ql, kl = sb("ql", [P, C, P]), sb("kl", [P, C, P])
        vl_next = sb("vl_next", [P, H, DH])
        vl = sb("vl", [P, H, DH])
        att_bt = sb("att_bt", [P, C, P])
        x3 = sb("x3", [P, D])
        stat_c, mv_c, rstd_c = sb("stat_c", [P, 6]), sb("mv_c", [P, 2]), sb("rstd_c", [P, 2])
        h_c = sb("h_c", [P, D])
        h_ct = sb("h_ct", [D, P])
        rows_all = sb("rows_all", [P, NT, ROW])
        ht_all = sb("ht_all", [D, T])
        lg_all = sb("lg_all", [P, NT, E])
        r_max, r_sum, r_prob, r_first, r_base, r_pos, r_out, r_slot = [
            sb(n, [P, NT]) for n in "r_max r_sum r_prob r_first r_base r_pos r_out r_slot".split()]
        r_less, r_exp, r_mark, r_tmp, r_tmp2 = [
            sb(n, [P, NT, E]) for n in "r_less r_exp r_mark r_tmp r_tmp2".split()]
        r_pick = sb("r_pick", [P, NT, E], BF16)
        r_idx = sb("r_idx", [P, NT], U32)
        prob_row = sb("prob_row", [P, T])
        ahead = sb("ahead", [P, NT, T], BF16)
        ties = sb("ties", [P, NT, P], BF16)
        hid0 = sb("hid0", [P, FC, T])
        acc = sb("acc", [P, NT, D])
        xg = sb("xg", [P, ST, ROW])
        xg_tok = sb("xg_tok", [P, ST], U32)
        xg_t = sb("xg_t", [D, ST * P])
        hid = sb("hid", [P, 2, FC, CAP1])
        y_t = sb("y_t", [D, SLOTS])
        y_rows = sb("y_rows", [P, ST, D])
        xg_dram = nc.dram_tensor("xg_dram", [ST * P, ROW], F32, kind="Internal").ap()

        x_in_s, ctx_in_s, alpha_in, wq2_in, wk1_in, wv1_in, wq1_in, wk2_in, wv2_in = sems(
            "x_in_s ctx_in_s alpha_in wq2_in wk1_in wv1_in wq1_in wk2_in wv2_in")
        bout_in, small_in, late_a_in, stage_b_in, w1_in, w2_in = sems(
            "bout_in small_in late_a_in stage_b_in w1_in w2_in")
        const_s, xg_zero_in, alpha_exp, alpha_s, rw_mm, small_s = sems(
            "const_s xg_zero_in alpha_exp alpha_s rw_mm small_s")
        n_mv, n_rstd, n_xn, n_mm, n_sb, xb_s = sems(
            "n_mv n_rstd n_xn n_mm n_sb xb_s")
        q2_mm, q2_sb, k1_mm, k1_sb, v1_mm, v1_sb, q1_mm, q1_sb, k2_mm, k2_sb, v2_mm, v2_sb = sems(
            "q2_mm q2_sb k1_mm k1_sb v1_mm v1_sb q1_mm q1_sb k2_mm k2_sb v2_mm v2_sb")
        kl_mm, kl_sb, vl_mm, vl_sb, vl_moved = sems("kl_mm kl_sb vl_mm vl_sb vl_moved")
        d1_mm, d2_mm, dl_mm, d1_low, d2_low, dl_low, d1_exp, d2_exp, dl_exp = sems(
            "d1_mm d2_mm dl_mm d1_low d2_low dl_low d1_exp d2_exp dl_exp")
        d1_rec, d2_rec, dl_rec, d1_w, d2_w, dl_w = sems("d1_rec d2_rec dl_rec d1_w d2_w dl_w")
        d1_tmm, d2_tmm, dl_tmm, d1_tsb_even, d1_tsb_odd, d2_tsb, dl_tsb = sems(
            "d1_tmm d2_tmm dl_tmm d1_tsb_even d1_tsb_odd d2_tsb dl_tsb")
        oa_mm, oa_sb, x1_mm, x1_s = sems("oa_mm oa_sb x1_mm x1_s")

        def half(n, par):
            return 2 * n - 1 + par

        def both(n):
            return 2 * n
        b_mv, b_rstd, b_h, bt_mm, bt_sb, y_mm, g_max, g_less, y_s, g_mark, g_exp = sems(
            "b_mv b_rstd b_h bt_mm bt_sb y_mm g_max g_less y_s g_mark g_exp")
        g_first, g_pick, loc_mm, g_gate, g_kept, g_kgate, pick_sum_s, x2_s = sems(
            "g_first g_pick loc_mm g_gate g_kept g_kgate pick_sum_s x2_s")
        b2_mv, b2_rstd, b2_h, b2t_mm, b2t_sb, xb2_s, ql_mm, ql_sb = sems(
            "b2_mv b2_rstd b2_h b2t_mm b2t_sb xb2_s ql_mm ql_sb")
        ob_mm, ob_sb, x3_mm, x3_s = sems("ob_mm ob_sb x3_mm x3_s")
        c_mv, c_rstd, c_h, ct_mm, ct_sb, cl_mm, cl_s, x3_all_s, h_all_s, ht_all_s = sems(
            "c_mv c_rstd c_h ct_mm ct_sb cl_mm cl_s x3_all_s h_all_s ht_all_s")
        f_dve, f_less, f_exp, f_prob, f_pick, row_mm, row_sb, ahead_s, rank_mm, f_out, f_idx = sems(
            "f_dve f_less f_exp f_prob f_pick row_mm row_sb ahead_s rank_mm f_out f_idx")
        hid0_mm, hid0_sb, y0_mm, b20_x_s, acc_s, acc_out, scat_s, xg_in, tok_s, xgt_mm, xgt_sb = sems(
            "hid0_mm hid0_sb y0_mm b20_x_s acc_s acc_out scat_s xg_in tok_s xgt_mm xgt_sb")
        hid_mm, hid_sb_act, hid_sb_dve, yt_mm, yt_sb, yr_mm, yr_sb, out_s = sems(
            "hid_mm hid_sb_act hid_sb_dve yt_mm yt_sb yr_mm yr_sb out_s")

        block = ctx.enter_context(nc.Block())

        def before_d1(k, c, d2_s, dl_s):
            return (dl_s, k - 1) if c else (d2_s, k)

        HID0 = ([(c, 0, 4, b) for c, b in enumerate((m1, s_even, s_odd, o_a))]
                + [(c, 4, NT - 1, b) for c, b in enumerate((m1, o_a, m1, o_a))]
                + [(c, NT - 1, NT, m1) for c in range(FC)])

        def rows_after(e):
            full = [j for j in range(ST) if min((j + 1) * P, SLOTS) <= e * CAP1]
            return [j for j in full if min((j + 1) * P, SLOTS) > (e - 1) * CAP1]

        def tile_of(w, n):
            return w[:, bass.ds(n, 1), :].rearrange("p a d -> p (a d)")

        @block.sync
        def _(sp):
            sp.dma_start(x_in[:, :], x[0]).then_inc(x_in_s, 16)
            sp.dma_start(wq2[:, :], L0_xattn_Wq2).then_inc(wq2_in, 16)
            sp.dma_start(wk1[:, :], L0_xattn_Wk1).then_inc(wk1_in, 16)
            sp.dma_start(wv1[:, :], L0_xattn_Wv1).then_inc(wv1_in, 16)
            sp.dma_start(wq1[:, :], L0_xattn_Wq1).then_inc(wq1_in, 16)
            sp.dma_start(wk2[:, :], L0_xattn_Wk2).then_inc(wk2_in, 16)
            sp.dma_start(wv2[:, :], L0_xattn_Wv2).then_inc(wv2_in, 16)
            sp.dma_start(wk[:, :], L1_xattn_Wk).then_inc(late_a_in, 16)
            sp.dma_start(wout[:, :, :], L0_xattn_Wout.rearrange("(c p) n -> p c n", p=P)).then_inc(late_a_in, 16)
            sp.dma_start(wv[:, :], L1_xattn_Wv).then_inc(late_a_in, 16)
            sp.dma_start(be_b[:, :], L0_ffn_be.rearrange("(a d) -> a d", a=1).broadcast_to([P, D])).then_inc(stage_b_in, 16)
            sp.dma_start(we_wg[:, 0:D], L0_ffn_We).then_inc(stage_b_in, 16)
            sp.dma_start(we_wg[:, D:D + E], L0_ffn_Wg).then_inc(stage_b_in, 16)
            sp.dma_start(bo_b[:, :], L1_xattn_bo.rearrange("(a d) -> a d", a=1).broadcast_to([P, D])).then_inc(stage_b_in, 16)
            sp.dma_start(wq[:, :], L1_xattn_Wq).then_inc(stage_b_in, 16)
            sp.dma_start(wo[:, :, :], L1_xattn_Wo.rearrange("(c p) n -> p c n", p=P)).then_inc(stage_b_in, 16)
            sp.dma_start(b20_b[:, :], L1_ffn_b2[0:1, :].broadcast_to([P, D])).then_inc(w2_in, 16)
            w1_d = L1_ffn_W1.rearrange("e p f -> p e f")
            w2_d = L1_ffn_W2.rearrange("e (c p) n -> p e c n", p=P)
            sp.dma_start(w1[:, 0, :], w1_d[:, 0, :]).then_inc(w1_in, 16)
            sp.dma_start(w2[:, 0, :, :], w2_d[:, 0, :, :]).then_inc(w2_in, 16)
            with sp.Fori(1, NT) as n:
                sp.wait_ge(n_xn, n)
                sp.wait_ge(xb_s, n)
                sp.dma_start(x_in[:, :], x[bass.ds(n, 1)].rearrange("a p d -> (a p) d")).then_inc(x_in_s, 16)
                sp.wait_ge(n_mm, n)
                sp.dma_start(ctx_in[:, :], ctx_1024[bass.ds(n, 1)].rearrange("a p d -> (a p) d")).then_inc(ctx_in_s, 16)
                sp.dma_start(w1[:, bass.ds(n, 1), :].rearrange("p a f -> p (a f)"),
                             w1_d[:, bass.ds(n, 1), :].rearrange("p a f -> p (a f)")).then_inc(w1_in, 16)
                sp.dma_start(w2[:, bass.ds(n, 1), :, :].rearrange("p a c n -> p (a c) n"),
                             w2_d[:, bass.ds(n, 1), :, :].rearrange("p a c n -> p (a c) n")).then_inc(w2_in, 16)
            for g in range(2):
                sp.wait_ge(acc_s, g + 1)
                sp.dma_start(out.rearrange("t p d -> p t d")[:, 4 * g:4 * g + 4, :],
                             acc[:, 4 * g:4 * g + 4, :]).then_inc(acc_out, 16)
            sp.wait_ge(scat_s, 16 * NT)
            for j in range(3):
                sp.dma_start(xg[:, 3 * j:3 * j + 3, :],
                             xg_dram.rearrange("(j p) d -> p j d", p=P)[:, 3 * j:3 * j + 3, :]).then_inc(xg_in, 16)
            sp.wait_ge(acc_out, 32)

        @block.gpsimd
        def _(pool):
            nc.gpsimd.memset(ident[:, :], 0.0).then_inc(const_s, 1)
            nc.gpsimd.memset(ones[:, :], 1.0).then_inc(const_s, 1)
            nc.gpsimd.memset(minus_half[:, :], -0.5).then_inc(const_s, 1)
            nc.gpsimd.memset(eps_col[:, :], EPS).then_inc(const_s, 1)
            pool.wait_ge(const_s, 4)
            nc.gpsimd.affine_select(out=ident[:, :], in_=ident[:, :], compare_op=ALU.not_equal, fill=1.0, base=0,
                                    pattern=[[-1, P]], channel_multiplier=1).then_inc(const_s, 1)

            def rstd(mv, r, mv_s, r_s, n):
                pool.wait_ge(mv_s, both(n))
                nc.gpsimd.tensor_tensor(r[:, 0:1], mv[:, 1:2], eps_col[:, :], ALU.add).then_inc(r_s, 1)
                pool.wait_ge(r_s, both(n) - 1)
                nc.gpsimd.tensor_tensor(r[:, 1:2], r[:, 0:1], minus_half[:, :], ALU.pow).then_inc(r_s, 1)

            def residual(k):
                pool.wait_ge(x_in_s, 16 * (k + 1))
                nc.gpsimd.tensor_tensor(xb[:, :], x_in[:, :], bout_b[:, :], ALU.add).then_inc(xb_s, 1)

            rstd(mv_n, rstd_n, n_mv, n_rstd, 1)
            pool.dma_start(alpha[:, 0:1], L0_xattn_alpha_attn.rearrange("(a b) -> a b", a=1).broadcast_to([P, 1])).then_inc(alpha_in, 16)
            nc.gpsimd.affine_select(out=before[:, :], in_=ones[:, :], compare_op=ALU.is_gt, fill=0.0, base=0,
                                    pattern=[[1, P]], channel_multiplier=-1).then_inc(const_s, 1)
            nc.gpsimd.memset(pick_sum[:, :], 0.0).then_inc(const_s, 1)
            for e in range(E):
                nc.gpsimd.memset(first_first[:, e:e + 1], float(E - e)).then_inc(const_s, 1)
                nc.gpsimd.memset(place_base[:, e:e + 1], float((e - 1) * CAP1)).then_inc(const_s, 1)
            pool.wait_ge(bout_in, 16)
            residual(0)

            def count_choice(n):
                pool.wait_ge(loc_mm, n)
                nc.gpsimd.tensor_tensor(pick_sum[:, :], pick_sum[:, :], pick[:, :], ALU.add).then_inc(pick_sum_s, 1)

            def x2_and_bias(n, c):
                pool.wait_ge(x2_s, n)
                if c:
                    pool.wait_ge(x3_s, n - 1)
                nc.gpsimd.tensor_tensor(xb2[:, :], x2[:, :], bo_b[:, :], ALU.add).then_inc(xb2_s, 1)

            def move_vl(n, c):
                pool.wait_ge(vl_sb, n)
                if c:
                    pool.wait_ge(ob_mm, n - 1)
                nc.gpsimd.tensor_tensor(pool_carrier[:, :], eps_col[:, :], eps_col[:, :], ALU.add)
                nc.gpsimd.tensor_copy(vl[:, :, :], vl_next[:, :, :]).then_inc(vl_moved, 1)

            def step(k, b, c, nxt):
                nA, nB, nC = k + 1, k, k - 1
                if nxt:
                    rstd(mv_n, rstd_n, n_mv, n_rstd, k + 2)
                if b:
                    count_choice(nB)
                    rstd(mv_2, rstd_2, b2_mv, b2_rstd, nB)
                if c:
                    rstd(mv_c, rstd_c, c_mv, c_rstd, nC)
                if b:
                    x2_and_bias(nB, c)
                if c:
                    pool.wait_ge(x3_s, nC)
                    nc.gpsimd.tensor_copy(rows_all[:, bass.ds(k - 2, 1), D:2 * D].rearrange("p a d -> p (a d)"),
                                          x3[:, :]).then_inc(x3_all_s, 1)
                if b:
                    move_vl(nB, c)
                if c:
                    pool.wait_ge(c_h, nC)
                    nc.gpsimd.tensor_copy(rows_all[:, bass.ds(k - 2, 1), 0:D].rearrange("p a d -> p (a d)"),
                                          h_c[:, :]).then_inc(h_all_s, 1)
                    pool.wait_ge(ct_sb, nC)
                    nc.gpsimd.tensor_copy(ht_all[:, bass.ts(k - 2, P)], h_ct[:, :]).then_inc(ht_all_s, 1)
                rstd(mv_b, rstd_b, b_mv, b_rstd, nA)
                if nxt:
                    pool.wait_ge(x1_s, nA)
                    residual(k + 1)

            step(0, False, False, True)
            nc.gpsimd.iota(token[:, :], [[P, NT]], base=0, channel_multiplier=1,
                           allow_small_or_imprecise_dtypes=True).then_inc(const_s, 1)
            nc.gpsimd.memset(no_rows[:, :, :], 0.0).then_inc(const_s, 1)
            pool.wait_ge(const_s, 9 + 2 * E)
            nc.gpsimd.tensor_copy(rows_all[:, :, 2 * D], token[:, :]).then_inc(const_s, 1)
            nc.gpsimd.memset(no_rows[:, :, 2 * D:ROW], FAR).then_inc(const_s, 1)
            pool.wait_ge(const_s, 11 + 2 * E)
            pool.dma_start(xg_dram.rearrange("(p j) d -> p j d", p=P), no_rows[:, :, :]).then_inc(xg_zero_in, 16)
            pool.wait_ge(stage_b_in, 96)
            step(1, True, False, True)
            with pool.Fori(2, NT - 1) as k:
                step(k, True, True, True)
            step(NT - 1, True, True, False)

            move_vl(NT, True)
            rstd(mv_c, rstd_c, c_mv, c_rstd, NT - 1)
            rstd(mv_2, rstd_2, b2_mv, b2_rstd, NT)
            x2_and_bias(NT, True)
            pool.wait_ge(w2_in, 16 * (NT + 1))
            pool.wait_ge(x3_all_s, NT - 2)
            for t in range(NT - 1):
                nc.gpsimd.tensor_tensor(b20_x[:, t, :], rows_all[:, t, D:2 * D], b20_b[:, :], ALU.add).then_inc(b20_x_s, 1)
            rstd(mv_c, rstd_c, c_mv, c_rstd, NT)
            pool.wait_ge(x3_s, NT)
            nc.gpsimd.tensor_tensor(b20_x[:, NT - 1, :], rows_all[:, NT - 1, D:2 * D], b20_b[:, :], ALU.add).then_inc(b20_x_s, 1)

            pool.wait_ge(f_idx, 1)
            pool.wait_ge(xg_zero_in, 16)
            pool.wait_ge(h_all_s, NT - 2)
            pool.wait_ge(c_h, NT)
            for t in range(NT):
                nc.gpsimd.indirect_dma_start(
                    out=xg_dram, out_offset=bass.IndirectOffsetOnAxis(ap=r_idx[:, t:t + 1], axis=0),
                    in_=rows_all[:, t, :], in_offset=None, bounds_check=SLOTS - 1, oob_is_err=False).then_inc(scat_s, 16)
            pool.wait_ge(acc_out, 32)
            pool.wait_ge(tok_s, 1)
            for j in range(ST):
                w = min(P, SLOTS - j * P)
                pool.wait_ge(yr_sb, j + 1)
                nc.gpsimd.indirect_dma_start(
                    out=out.rearrange("t p d -> (t p) d"),
                    out_offset=bass.IndirectOffsetOnAxis(ap=xg_tok[0:w, j:j + 1], axis=0),
                    in_=y_rows[0:w, j, :], in_offset=None, bounds_check=T - 1, oob_is_err=False).then_inc(out_s, 16)
            pool.wait_ge(out_s, 16 * ST)

        @block.scalar
        def _(act):
            act.dma_start(ctx_in[:, :], ctx_1024[0]).then_inc(ctx_in_s, 16)
            act.dma_start(bout_b[:, :], L0_xattn_bout.rearrange("(a d) -> a d", a=1).broadcast_to([P, D])).then_inc(bout_in, 16)
            act.dma_start(rw_rows[:, :], L1_ffn_router_w).then_inc(small_in, 16)
            act.dma_start(b1_rows[:, :], L1_ffn_b1.rearrange("e (c p) -> (e c) p", p=P)).then_inc(small_in, 16)
            act.dma_start(b2_rows[:, :], L1_ffn_b2).then_inc(small_in, 16)

            def out_of_psum(dst, src, mm, done, n):
                act.wait_ge(mm, n)
                nc.scalar.copy(dst, src).then_inc(done, 1)

            def queries(dst, src, mm, done, n):
                act.wait_ge(mm, n)
                nc.scalar.activation(dst, src, ACT.Copy, scale=-SCALE).then_inc(done, 1)

            def exp_half(par, low_s, tmm_before, n_before, done, n):
                act.wait_ge(low_s, half(n, par))
                if not (isinstance(n_before, int) and n_before == 0):
                    act.wait_ge(tmm_before, half(n_before, par))
                for c in range(C):
                    last = nc.scalar.activation(probs[:, par, c, :], chunks(s_bank[par])[:, c, :], ACT.Exp,
                                                bias=low[:, par, c:c + 1], scale=-1.0, accum_out=wsum[:, par, c:c + 1])
                last.then_inc(done, 1)

            def turned(par, tmm, tsb, n):
                out_of_psum(probs_t[:, par, :, :], chunks(t_bank[par]), tmm, tsb, half(n, par))

            def by_head(bank):
                return bank[:, :].rearrange("p (h d) -> p h d", h=H)

            out_of_psum(xc_t[:, :, :], chunks(t_odd)[:, 0:2, :], n_mm, n_sb, 1)
            act.wait_ge(alpha_in, 16)
            nc.scalar.activation(alpha[:, 1:2], alpha[:, 0:1], ACT.Exp, scale=-1.0).then_inc(alpha_exp, 1)

            def gate_exp(n):
                act.wait_ge(g_less, n)
                nc.scalar.activation(lg[:, 1, :], lg[:, 0, :], ACT.Exp, accum_out=gate[:, 1:2]).then_inc(g_exp, 1)

            def step(k, b, c, nxt):
                nA, nB, nC = k + 1, k, k - 1
                if c:
                    turned(0, dl_tmm, dl_tsb, nC)
                if b:
                    out_of_psum(h_bt[:, :], o_b[:, 0:P], bt_mm, bt_sb, nB)
                if c:
                    turned(1, dl_tmm, dl_tsb, nC)
                exp_half(0, d1_low, *before_d1(k, c, d2_tmm, dl_tmm), d1_exp, nA)
                queries(q1[:, :, :], chunks(m1), q1_mm, q1_sb, nA)
                if b:
                    gate_exp(nB)
                out_of_psum(k2[:, :, :], chunks(m0), k2_mm, k2_sb, nA)
                if c:
                    out_of_psum(att_bt[:, :, :], chunks(o_b), ob_mm, ob_sb, nC)
                exp_half(1, d1_low, *before_d1(k, c, d2_tmm, dl_tmm), d1_exp, nA)
                out_of_psum(v1[:, :, :], by_head(m1), v1_mm, v1_sb, nA)
                out_of_psum(probs_t[:, 0, :, :], chunks(t_even), d1_tmm, d1_tsb_even, half(nA, 0))
                exp_half(0, d2_low, d1_tmm, nA, d2_exp, nA)
                if b:
                    out_of_psum(h_2t[:, :], m0[:, 0:P], b2t_mm, b2t_sb, nB)
                exp_half(1, d2_low, d1_tmm, nA, d2_exp, nA)
                if b:
                    queries(ql[:, :, :], chunks(m1), ql_mm, ql_sb, nB)
                if c:
                    out_of_psum(h_ct[:, :], o_b[:, 0:P], ct_mm, ct_sb, nC)
                turned(0, d2_tmm, d2_tsb, nA)
                turned(1, d2_tmm, d2_tsb, nA)
                if c:
                    out_of_psum(lg_all[:, bass.ds(k - 2, 1), :].rearrange("p a e -> p (a e)"), o_b[:, P:P + E], cl_mm, cl_s, nC)
                if nxt:
                    out_of_psum(xc_t[:, :, :], chunks(t_odd)[:, 0:2, :], n_mm, n_sb, k + 2)
                if b:
                    exp_half(0, dl_low, d2_tmm, nA, dl_exp, nB)
                out_of_psum(att_at[:, :, :], chunks(o_a), oa_mm, oa_sb, nA)
                if nxt:
                    queries(q2[:, :, :], chunks(m0), q2_mm, q2_sb, k + 2)
                if b:
                    exp_half(1, dl_low, d2_tmm, nA, dl_exp, nB)

            queries(q2[:, :, :], chunks(m0), q2_mm, q2_sb, 1)
            step(0, False, False, True)
            step(1, True, False, True)
            with act.Fori(2, NT - 1) as k:
                step(k, True, True, True)
            step(NT - 1, True, True, False)

            def hidden0(u):
                c, t0, t1, bank = HID0[u]
                w = (t1 - t0) * P
                at = c * P if bank is m1 and t0 == NT - 1 else 0
                act.wait_ge(hid0_mm, u + 1 if t0 < NT - 1 else len(HID0))
                nc.scalar.activation(hid0[:, c, t0 * P:t1 * P], bank[:, at:at + w], ACT.Relu,
                                     bias=b1_t[:, c:c + 1]).then_inc(hid0_sb, 1)

            def probability_row(r, bank, t0, t1):
                act.wait_ge(row_mm, r)
                nc.scalar.copy(prob_row[:, t0 * P:t1 * P], bank[:, 0:(t1 - t0) * P]).then_inc(row_sb, 1)

            turned(0, dl_tmm, dl_tsb, NT - 1)
            turned(1, dl_tmm, dl_tsb, NT - 1)
            hidden0(0)
            out_of_psum(h_bt[:, :], t_even[:, 0:P], bt_mm, bt_sb, NT)
            out_of_psum(att_bt[:, :, :], chunks(o_b), ob_mm, ob_sb, NT - 1)
            gate_exp(NT)
            hidden0(1)
            hidden0(2)
            out_of_psum(ht_all[:, (NT - 2) * P:(NT - 1) * P], t_even[:, 0:P], ct_mm, ct_sb, NT - 1)
            hidden0(3)
            out_of_psum(lg_all[:, NT - 2, :], t_odd[:, 0:E], cl_mm, cl_s, NT - 1)
            out_of_psum(h_2t[:, :], t_even[:, 0:P], b2t_mm, b2t_sb, NT)
            queries(ql[:, :, :], chunks(m0), ql_mm, ql_sb, NT)
            act.wait_ge(f_less, 1)
            nc.scalar.activation(r_exp[:, 0:NT - 1, :], r_less[:, 0:NT - 1, :], ACT.Exp).then_inc(f_exp, 1)
            hidden0(4)
            exp_half(0, dl_low, dl_tmm, NT - 1, dl_exp, NT)
            probability_row(1, o_a, 0, 4)
            exp_half(1, dl_low, dl_tmm, NT - 1, dl_exp, NT)
            probability_row(2, m1, 4, NT - 1)
            turned(0, dl_tmm, dl_tsb, NT)
            turned(1, dl_tmm, dl_tsb, NT)
            hidden0(5)
            out_of_psum(att_bt[:, :, :], chunks(o_b), ob_mm, ob_sb, NT)
            hidden0(6)
            hidden0(7)
            out_of_psum(ht_all[:, (NT - 1) * P:T], t_even[:, 0:P], ct_mm, ct_sb, NT)
            out_of_psum(lg_all[:, NT - 1, :], t_odd[:, 0:E], cl_mm, cl_s, NT)
            act.wait_ge(f_less, 2)
            nc.scalar.activation(r_exp[:, NT - 1, :], r_less[:, NT - 1, :], ACT.Exp).then_inc(f_exp, 1)
            probability_row(3, t_even, NT - 1, NT)
            for u in range(8, 12):
                hidden0(u)

            for j in range(3):
                act.wait_ge(xgt_mm, j + 1)
                nc.scalar.copy(xg_t[:, 384 * j:384 * (j + 1)], (t_even, t_odd, o_a)[j][:, 0:384]).then_inc(xgt_sb, 1)

            def hidden(e):
                act.wait_ge(hid_mm, 2 * (e - 1) + 1)
                for c in range(2):
                    last = nc.scalar.activation(hid[:, e % 2, c, :], (m0, s_even)[e % 2][:, c * CAP1:(c + 1) * CAP1],
                                                ACT.Relu, bias=b1_t[:, e * FC + c:e * FC + c + 1])
                last.then_inc(hid_sb_act, 1)

            def expert_out(e):
                act.wait_ge(yt_mm, e)
                nc.scalar.activation(y_t[:, (e - 1) * CAP1:e * CAP1], (t_even, t_odd)[e % 2][:, 0:CAP1], ACT.Identity,
                                     bias=b2_t[:, e:e + 1]).then_inc(yt_sb, 1)

            for e in range(1, E):
                hidden(e)
                if e > 1:
                    expert_out(e - 1)
            expert_out(E - 1)

        @block.vector
        def _(dve):
            V = nc.vector

            def stats(src, stat, mv, mv_s, n):
                V.bn_stats(stat[:, :], src).then_inc(mv_s, 1)
                dve.wait_ge(mv_s, both(n) - 1)
                V.tensor_copy(carrier[:, :], stat[:, 0:1])
                V.bn_aggr(mv[:, :], stat[:, :]).then_inc(mv_s, 1)

            def normed(dst, src, mv, r, r_s, done, n):
                dve.wait_ge(r_s, both(n))
                V.tensor_scalar(dst, src, mv[:, 0:1], r[:, 1:2], ALU.subtract, ALU.mult).then_inc(done, 1)

            def lowest(mm, low_s, exp_before, n_before, n):
                dve.wait_ge(mm, n)
                for par in range(2):
                    if not (isinstance(n_before, int) and n_before == 0):
                        dve.wait_ge(exp_before, half(n_before, par))
                    V.tensor_reduce(low[:, par, :], chunks(s_bank[par]), AX.X, ALU.min).then_inc(low_s, 1)

            def divide(par, exp_s, rec, done, n, by):
                dve.wait_ge(exp_s, half(n, par))
                V.reciprocal(rsum[:, par, :], wsum[:, par, :]).then_inc(rec, 1)
                dve.wait_ge(rec, half(n, par))
                V.scalar_tensor_tensor(out=probs[:, par, :, :], in0=probs[:, par, :, :], scalar=by,
                                       in1=rsum[:, par, :].unsqueeze(2).broadcast_to([P, C, P]),
                                       op0=ALU.mult, op1=ALU.mult).then_inc(done, 1)

            dve.wait_ge(x_in_s, 16)
            stats(x_in[:, :], stat_n, mv_n, n_mv, 1)
            normed(xn[:, :], x_in[:, :], mv_n, rstd_n, n_rstd, n_xn, 1)
            dve.wait_ge(alpha_exp, 1)
            V.tensor_scalar(alpha[:, 1:2], alpha[:, 1:2], 1.0, None, ALU.add).then_inc(alpha_s, 1)
            dve.wait_ge(alpha_s, 1)
            V.reciprocal(alpha[:, 2:3], alpha[:, 1:2]).then_inc(alpha_s, 1)
            dve.wait_ge(alpha_s, 2)
            V.tensor_scalar(alpha[:, 3:4], alpha[:, 2:3], -1.0, 1.0, ALU.mult, ALU.add).then_inc(alpha_s, 1)
            dve.wait_ge(rw_mm, 1)
            V.tensor_copy(rw_t[:, :], o_a[:, 0:E]).then_inc(small_s, 1)
            V.tensor_copy(b1_t[:, :], o_a[:, 64:64 + E * FC]).then_inc(small_s, 1)
            V.tensor_copy(b2_t[:, :], o_a[:, 128:128 + E]).then_inc(small_s, 1)

            def copy(dst, src, mm, done, n):
                dve.wait_ge(mm, n)
                V.tensor_copy(dst, src).then_inc(done, 1)

            def by_head(bank):
                return bank[:, :].rearrange("p (h d) -> p h d", h=H)

            def gate_choice(n, y):
                dve.wait_ge(y_mm, n)
                V.tensor_reduce(gate[:, 0:1], y[:, D:D + E], AX.X, ALU.max).then_inc(g_max, 1)
                dve.wait_ge(g_max, n)
                V.tensor_scalar(lg[:, 0, :], y[:, D:D + E], gate[:, 0:1], None, ALU.subtract).then_inc(g_less, 1)
                V.tensor_tensor(ybe[:, :], y[:, 0:D], be_b[:, :], ALU.add).then_inc(y_s, 1)
                dve.wait_ge(g_less, n)
                V.scalar_tensor_tensor(out=lg[:, 2, :], in0=lg[:, 0, :], scalar=0.0, in1=first_first[:, :],
                                       op0=ALU.is_ge, op1=ALU.mult).then_inc(g_mark, 1)
                dve.wait_ge(g_mark, n)
                V.tensor_reduce(gate[:, 3:4], lg[:, 2, :], AX.X, ALU.max).then_inc(g_first, 1)
                dve.wait_ge(g_first, n)
                dve.wait_ge(pick_sum_s, n - 1)
                V.tensor_scalar(pick[:, :], lg[:, 2, :], gate[:, 3:4], None, ALU.is_equal).then_inc(g_pick, 1)

            def gate_result(n):
                dve.wait_ge(g_exp, n)
                V.reciprocal(gate[:, 2:3], gate[:, 1:2]).then_inc(g_gate, 1)
                dve.wait_ge(loc_mm, n)
                dve.wait_ge(g_pick, n)
                V.scalar_tensor_tensor(out=kept[:, :], in0=o_b[:, 0:E], scalar=float(CAP0), in1=pick[:, :],
                                       op0=ALU.is_lt, op1=ALU.mult, accum_out=gate[:, 4:5]).then_inc(g_kept, 1)
                dve.wait_ge(g_kept, n)
                dve.wait_ge(g_gate, n)
                V.tensor_tensor(gate[:, 5:6], gate[:, 4:5], gate[:, 2:3], ALU.mult).then_inc(g_kgate, 1)
                dve.wait_ge(g_kgate, n)
                dve.wait_ge(y_s, n)
                V.scalar_tensor_tensor(out=x2[:, :], in0=ybe[:, :], scalar=gate[:, 5:6], in1=x1[:, :],
                                       op0=ALU.mult, op1=ALU.add).then_inc(x2_s, 1)
                dve.wait_ge(x2_s, n)
                stats(x2[:, :], stat_2, mv_2, b2_mv, n)

            def step(k, b, c, nxt):
                nA, nB, nC = k + 1, k, k - 1
                if b:
                    normed(h_b[:, :], x1[:, :], mv_b, rstd_b, b_rstd, b_h, nB)
                lowest(d1_mm, d1_low, *before_d1(k, c, d2_exp, dl_exp), nA)
                if b:
                    gate_choice(nB, o_b[:, P:P + D + E])
                divide(0, d1_exp, d1_rec, d1_w, nA, alpha[:, 2:3])
                if nxt:
                    dve.wait_ge(x_in_s, 16 * (k + 2))
                    stats(x_in[:, :], stat_n, mv_n, n_mv, k + 2)
                divide(1, d1_exp, d1_rec, d1_w, nA, alpha[:, 2:3])
                if b:
                    gate_result(nB)
                if c:
                    dve.wait_ge(x3_mm, nC)
                    dve.wait_ge(xb2_s, nC)
                    V.tensor_tensor(x3[:, :], m0[:, 0:D], xb2[:, :], ALU.add).then_inc(x3_s, 1)
                    dve.wait_ge(x3_s, nC)
                    stats(x3[:, :], stat_c, mv_c, c_mv, nC)
                if b:
                    normed(h_2[:, :], x2[:, :], mv_2, rstd_2, b2_rstd, b2_h, nB)
                if nxt:
                    normed(xn[:, :], x_in[:, :], mv_n, rstd_n, n_rstd, n_xn, k + 2)
                lowest(d2_mm, d2_low, d1_exp, nA, nA)
                dve.wait_ge(d1_tmm, both(nA))
                V.tensor_copy(probs_t[:, 1, :, :], chunks(t_odd)).then_inc(d1_tsb_odd, 1)
                copy(v2[:, :, :], by_head(m1), v2_mm, v2_sb, nA)
                if c:
                    normed(h_c[:, :], x3[:, :], mv_c, rstd_c, c_rstd, c_h, nC)
                divide(0, d2_exp, d2_rec, d2_w, nA, alpha[:, 3:4])
                if b:
                    dve.wait_ge(vl_moved, nB)
                copy(vl_next[:, :, :], by_head(m0), vl_mm, vl_sb, nA)
                divide(1, d2_exp, d2_rec, d2_w, nA, alpha[:, 3:4])
                if b:
                    lowest(dl_mm, dl_low, d2_exp, nA, nB)
                copy(kl[:, :, :], chunks(m1), kl_mm, kl_sb, nA)
                if b:
                    divide(0, dl_exp, dl_rec, dl_w, nB, 1.0)
                if nxt:
                    copy(k1[:, :, :], chunks(m1), k1_mm, k1_sb, k + 2)
                if c:
                    dve.wait_ge(x3_all_s, nC)
                dve.wait_ge(x1_mm, nA)
                dve.wait_ge(xb_s, nA)
                V.tensor_tensor(x1[:, :], m0[:, 0:D], xb[:, :], ALU.add).then_inc(x1_s, 1)
                dve.wait_ge(x1_s, nA)
                stats(x1[:, :], stat_b, mv_b, b_mv, nA)
                if b:
                    divide(1, dl_exp, dl_rec, dl_w, nB, 1.0)

            copy(k1[:, :, :], chunks(m1), k1_mm, k1_sb, 1)
            dve.wait_ge(const_s, 7 + 2 * E)
            step(0, False, False, True)
            dve.wait_ge(stage_b_in, 96)
            step(1, True, False, True)
            with dve.Fori(2, NT - 1) as k:
                step(k, True, True, True)
            step(NT - 1, True, True, False)

            def per_tile(w, t0, t1):
                return w[:, t0:t1].unsqueeze(2).broadcast_to([P, t1 - t0, E])

            def per_expert(w, t0, t1):
                return w[:, :].unsqueeze(1).broadcast_to([P, t1 - t0, E])

            chain = [0]

            def done(ins):
                chain[0] += 1
                ins.then_inc(f_dve, 1)
                dve.wait_ge(f_dve, chain[0])

            def choices(r, t0, t1):
                dve.wait_ge(cl_s, t1)
                done(V.tensor_reduce(r_max[:, t0:t1], lg_all[:, t0:t1, :], AX.X, ALU.max))
                V.tensor_tensor(r_less[:, t0:t1, :], lg_all[:, t0:t1, :], per_tile(r_max, t0, t1), ALU.subtract).then_inc(f_less, 1)
                dve.wait_ge(f_less, r)
                done(V.tensor_scalar(r_tmp[:, t0:t1, :], r_less[:, t0:t1, :], 0.0, None, ALU.is_ge))
                dve.wait_ge(f_exp, r)
                done(V.tensor_reduce(r_sum[:, t0:t1], r_exp[:, t0:t1, :], AX.X, ALU.add))
                V.reciprocal(r_prob[:, t0:t1], r_sum[:, t0:t1]).then_inc(f_prob, 1)
                done(V.tensor_tensor(r_mark[:, t0:t1, :], r_tmp[:, t0:t1, :], per_expert(first_first, t0, t1), ALU.mult))
                done(V.tensor_reduce(r_first[:, t0:t1], r_mark[:, t0:t1, :], AX.X, ALU.max))
                V.tensor_tensor(r_pick[:, t0:t1, :], r_mark[:, t0:t1, :], per_tile(r_first, t0, t1), ALU.is_equal).then_inc(f_pick, 1)
                dve.wait_ge(f_pick, r)
                done(V.tensor_tensor(r_tmp2[:, t0:t1, :], r_pick[:, t0:t1, :], per_expert(place_base, t0, t1), ALU.mult))
                done(V.tensor_reduce(r_base[:, t0:t1], r_tmp2[:, t0:t1, :], AX.X, ALU.add))

            def ranks_before(t):
                w = (t + 1) * P
                V.tensor_scalar(ahead[:, t, 0:w], prob_row[:, 0:w], r_prob[:, t:t + 1], None, ALU.is_lt)
                if t < NT - 2:
                    V.tensor_scalar(ahead[:, t, w:T - P], prob_row[:, w:T - P], r_prob[:, t:t + 1], None, ALU.is_le)
                tied(t)

            def tied(t):
                V.scalar_tensor_tensor(out=ties[:, t, :], in0=prob_row[:, t * P:(t + 1) * P], scalar=r_prob[:, t:t + 1],
                                       in1=before[:, :], op0=ALU.is_equal, op1=ALU.mult).then_inc(ahead_s, 1)

            normed(h_b[:, :], x1[:, :], mv_b, rstd_b, b_rstd, b_h, NT)
            dve.wait_ge(x3_mm, NT - 1)
            dve.wait_ge(xb2_s, NT - 1)
            V.tensor_tensor(rows_all[:, NT - 2, D:2 * D], m0[:, 0:D], xb2[:, :], ALU.add).then_inc(x3_s, 1)
            dve.wait_ge(x3_s, NT - 1)
            stats(rows_all[:, NT - 2, D:2 * D], stat_c, mv_c, c_mv, NT - 1)
            gate_choice(NT, t_odd[:, 0:D + E])
            normed(rows_all[:, NT - 2, 0:D], rows_all[:, NT - 2, D:2 * D], mv_c, rstd_c, c_rstd, c_h, NT - 1)
            gate_result(NT)
            normed(h_2[:, :], x2[:, :], mv_2, rstd_2, b2_rstd, b2_h, NT)
            choices(1, 0, NT - 1)
            lowest(dl_mm, dl_low, dl_exp, NT - 1, NT)
            divide(0, dl_exp, dl_rec, dl_w, NT, 1.0)
            divide(1, dl_exp, dl_rec, dl_w, NT, 1.0)
            dve.wait_ge(row_sb, 2)
            dve.wait_ge(f_prob, 1)
            for t in range(3):
                ranks_before(t)
            dve.wait_ge(x3_mm, NT)
            dve.wait_ge(xb2_s, NT)
            V.tensor_tensor(rows_all[:, NT - 1, D:2 * D], m0[:, 0:D], xb2[:, :], ALU.add).then_inc(x3_s, 1)
            dve.wait_ge(x3_s, NT)
            stats(rows_all[:, NT - 1, D:2 * D], stat_c, mv_c, c_mv, NT)
            ranks_before(3)
            normed(rows_all[:, NT - 1, 0:D], rows_all[:, NT - 1, D:2 * D], mv_c, rstd_c, c_rstd, c_h, NT)
            ranks_before(4)
            ranks_before(5)
            ranks_before(6)
            choices(2, NT - 1, NT)
            dve.wait_ge(row_sb, 3)
            dve.wait_ge(f_prob, 2)
            V.tensor_scalar(ahead[:, NT - 1, :], prob_row[:, :], r_prob[:, NT - 1:NT], None, ALU.is_lt)
            tied(NT - 1)
            V.tensor_tensor(ahead[:, 0:NT - 1, T - P:T], prob_row[:, T - P:T].unsqueeze(1).broadcast_to([P, NT - 1, P]),
                            r_prob[:, 0:NT - 1].unsqueeze(2).broadcast_to([P, NT - 1, P]), ALU.is_le).then_inc(ahead_s, 1)
            dve.wait_ge(rank_mm, 1)
            done(V.tensor_tensor(r_tmp[:, :, :], o_a[:, 0:NT * E].rearrange("p (t e) -> p t e", t=NT),
                                 r_pick[:, :, :], ALU.mult))
            done(V.tensor_reduce(r_pos[:, :], r_tmp[:, :, :], AX.X, ALU.add))
            V.tensor_tensor(r_slot[:, :], r_pos[:, :], r_base[:, :], ALU.add)
            done(V.tensor_scalar(r_pos[:, :], r_pos[:, :], float(CAP1), None, ALU.is_ge))
            V.tensor_tensor(r_out[:, :], r_pos[:, :], r_pick[:, :, 0], ALU.max).then_inc(f_out, 1)
            dve.wait_ge(f_out, 1)
            V.scalar_tensor_tensor(out=r_idx[:, :], in0=r_out[:, :], scalar=FAR, in1=r_slot[:, :],
                                   op0=ALU.mult, op1=ALU.add).then_inc(f_idx, 1)
            dve.wait_ge(b20_x_s, NT)
            for g in range(2):
                dve.wait_ge(y0_mm, g + 1)
                V.tensor_tensor(acc[:, 4 * g:4 * g + 4, :], chunks((s_even, s_odd)[g]), b20_x[:, 4 * g:4 * g + 4, :],
                                ALU.add).then_inc(acc_s, 1)

            dve.wait_ge(xg_in, 48)
            V.tensor_copy(xg_tok[:, :], xg[:, :, 2 * D]).then_inc(tok_s, 1)

            def hidden(e):
                dve.wait_ge(hid_mm, 2 * (e - 1) + 2)
                for c in range(2):
                    last = V.tensor_scalar(hid[:, e % 2, 2 + c, :], (m1, s_odd)[e % 2][:, c * CAP1:(c + 1) * CAP1],
                                           b1_t[:, e * FC + 2 + c:e * FC + 3 + c], 0.0, ALU.add, ALU.max)
                last.then_inc(hid_sb_dve, 1)

            def rows_out(j):
                dve.wait_ge(yr_mm, j + 1)
                w = min(P, SLOTS - j * P)
                V.tensor_tensor(y_rows[0:w, j, :], (o_a, o_b)[j % 2][0:w, 0:D], xg[0:w, j, D:2 * D], ALU.add).then_inc(yr_sb, 1)

            for e in range(1, E):
                hidden(e)
                for j in rows_after(e - 2):
                    rows_out(j)
            for e in (E - 2, E - 1):
                for j in rows_after(e):
                    rows_out(j)

        @block.tensor
        def _(pe):
            mm = nc.tensor.matmul
            turn = nc.tensor.transpose
            xn_t, c_t = xc_t[:, 0, :], xc_t[:, 1, :]

            def project(bank, w, src, done):
                for c in range(C):
                    last = mm(chunks(bank)[:, c, :], w[:, c * P:(c + 1) * P], src, start=True, stop=True)
                last.then_inc(done, 1)

            def project_rows(bank, w, src, done):
                mm(bank[:, :], src, w[:, :], start=True, stop=True).then_inc(done, 1)

            def scores(q, kk, done):
                for c in range(C):
                    for par in range(2):
                        rows = slice(par * DH, (par + 1) * DH)
                        last = mm(chunks(s_bank[par])[:, c, :], q[rows, c, :], kk[rows, c, :], start=True, stop=True)
                last.then_inc(done, 1)

            def turn_probs(w, copied_before, done, n):
                for par in range(2):
                    pe.wait_ge(w, half(n, par))
                    if copied_before is not None:
                        pe.wait_ge(*copied_before[par])
                    for c in range(C):
                        last = turn(chunks(t_bank[par])[:, c, :], probs[:, par, c, :], ident[:, :])
                    last.then_inc(done, 1)

            def weigh(bank, v, copied, fresh, done):
                for par in range(2):
                    pe.wait_ge(*copied[par])
                    for c in range(C):
                        last = mm(chunks(bank)[par * DH:(par + 1) * DH, c, :], v[:, 2 * c + par, :], probs_t[:, par, c, :],
                                  start=(fresh and c == 0), stop=(done is not None), skip_group_check=True)
                if done is not None:
                    last.then_inc(done, 1)

            def halves(s, n):
                return (s, half(n, 0)), (s, half(n, 1))

            def d1_copied(n):
                return (d1_tsb_even, n), (d1_tsb_odd, n)

            def join_heads(bank, att_t, w, done):
                for c in range(C):
                    last = mm(bank[:, 0:D], att_t[:, c, :], w[:, c, :], start=(c == 0), stop=(c == C - 1))
                last.then_inc(done, 1)

            def turn_next(n):
                pe.wait_ge(ctx_in_s, 16 * n)
                turn(chunks(t_odd)[:, 1, :], ctx_in[:, :], ident[:, :])
                pe.wait_ge(n_xn, n)
                turn(chunks(t_odd)[:, 0, :], xn[:, :], ident[:, :]).then_inc(n_mm, 1)

            pe.wait_ge(const_s, 5)
            turn_next(1)
            pe.wait_ge(small_in, 48)
            turn(o_a[:, 0:E], rw_rows[:, :], ident[0:E, 0:E])
            turn(o_a[:, 64:64 + E * FC], b1_rows[:, :], ident[0:E * FC, 0:E * FC])
            turn(o_a[:, 128:128 + E], b2_rows[:, :], ident[0:E, 0:E]).then_inc(rw_mm, 1)

            def loaded(k, at, s, n=16):
                if isinstance(k, int) and k == at:
                    pe.wait_ge(s, n)

            def step(k, b, c, nxt):
                nA, nB, nC = k + 1, k, k - 1
                first, second = (isinstance(k, int) and k == n for n in (0, 1))
                pe.wait_ge(q2_sb, nA)
                pe.wait_ge(k1_sb, nA)
                if b:
                    s, n = before_d1(k, c, d2_exp, dl_exp)
                    pe.wait_ge(s, both(n))
                scores(q2, k1, d1_mm)
                if c:
                    pe.wait_ge(n_sb, nA)
                    turn_probs(dl_w, halves(d2_tsb, nB), dl_tmm, nC)
                if b:
                    pe.wait_ge(b_h, nB)
                    if c:
                        pe.wait_ge(g_kept, nB - 1)
                    turn(o_b[:, 0:P], h_b[:, :], ident[:, :]).then_inc(bt_mm, 1)
                loaded(k, 0, wq1_in)
                project(m1, wq1, xn_t, q1_mm)
                if b:
                    loaded(k, 1, stage_b_in, 96)
                    pe.wait_ge(bt_sb, nB)
                    mm(o_b[:, P:P + D + E], h_bt[:, :], we_wg[:, :], start=True, stop=True).then_inc(y_mm, 1)
                    pe.wait_ge(x1_s, nB)
                loaded(k, 0, wk2_in)
                project(m0, wk2, c_t, k2_mm)
                if c:
                    pe.wait_ge(y_s, nB)
                    pe.wait_ge(vl_moved, nC)
                    weigh(o_b, vl, halves(dl_tsb, nC), True, ob_mm)
                loaded(k, 0, wv1_in)
                pe.wait_ge(q1_sb, nA)
                project_rows(m1, wv1, xn_t, v1_mm)
                if b:
                    if c:
                        pe.wait_ge(ob_sb, nC)
                    else:
                        pe.wait_ge(y_s, nB)
                        pe.wait_ge(const_s, 7)
                    count_choices(nB)
                pe.wait_ge(k2_sb, nA)
                if c:
                    join_heads(m0, att_bt, wo, x3_mm)
                pe.wait_ge(d1_exp, both(nA))
                scores(q1, k2, d2_mm)
                pe.wait_ge(n_sb, nA)
                if second:
                    pe.wait_ge(d2_tsb, both(1))
                turn_probs(d1_w, halves(dl_tsb, nC) if c else None, d1_tmm, nA)
                loaded(k, 0, wv2_in)
                pe.wait_ge(v1_sb, nA)
                project_rows(m1, wv2, c_t, v2_mm)
                if b:
                    pe.wait_ge(b2_h, nB)
                    if c:
                        pe.wait_ge(x3_s, nC)
                    turn(m0[:, 0:P], h_2[:, :], ident[:, :]).then_inc(b2t_mm, 1)
                    pe.wait_ge(oa_sb, nB)
                else:
                    pe.wait_ge(small_s, 3)
                weigh(o_a, v1, d1_copied(nA), True, None)
                if c:
                    pe.wait_ge(c_h, nC)
                    pe.wait_ge(g_kept, nB)
                    turn(o_b[:, 0:P], h_c[:, :], ident[:, :]).then_inc(ct_mm, 1)
                if b:
                    pe.wait_ge(b2t_sb, nB)
                    pe.wait_ge(v2_sb, nA)
                    project(m1, wq, h_2t[:, :], ql_mm)
                loaded(k, 0, late_a_in, 48)
                project_rows(m0, wv, c_t, vl_mm)
                if b:
                    pe.wait_ge(ql_sb, nB)
                    pe.wait_ge(kl_sb, nB)
                    pe.wait_ge(d2_exp, both(nA))
                    scores(ql, kl, dl_mm)
                turn_probs(d2_w, d1_copied(nA), d2_tmm, nA)
                if c:
                    pe.wait_ge(ct_sb, nC)
                    mm(o_b[:, P:P + E], h_ct[:, :], rw_t[:, :], start=True, stop=True).then_inc(cl_mm, 1)
                pe.wait_ge(v2_sb, nA)
                project(m1, wk, c_t, kl_mm)
                if nxt:
                    pe.wait_ge(d2_tsb, both(nA))
                    turn_next(k + 2)
                weigh(o_a, v2, halves(d2_tsb, nA), False, oa_mm)
                pe.wait_ge(vl_sb, nA)
                if nxt:
                    first_projections(k + 1)
                if c:
                    pe.wait_ge(cl_s, nC)
                pe.wait_ge(oa_sb, nA)
                if nxt:
                    pe.wait_ge(q2_sb, k + 2)
                join_heads(m0, att_at, wout, x1_mm)

            def first_projections(k):
                pe.wait_ge(n_sb, k + 1)
                loaded(k, 0, wq2_in)
                project(m0, wq2, c_t, q2_mm)
                loaded(k, 0, wk1_in)
                if not (isinstance(k, int) and k == 0):
                    pe.wait_ge(kl_sb, k)
                project(m1, wk1, xn_t, k1_mm)

            def count_choices(n):
                pe.wait_ge(g_pick, n)
                mm(o_b[:, 0:E], before[:, :], pick[:, :], start=True, stop=False)
                pe.wait_ge(pick_sum_s, n - 1)
                mm(o_b[:, 0:E], ones[:, :], pick_sum[:, :], start=False, stop=True).then_inc(loc_mm, 1)

            first_projections(0)
            step(0, False, False, True)
            step(1, True, False, True)
            with pe.Fori(2, NT - 1) as k:
                step(k, True, True, True)
            step(NT - 1, True, True, False)

            def hidden0(u):
                c, t0, t1, bank = HID0[u]
                w = (t1 - t0) * P
                at = c * P if bank is m1 and t0 == NT - 1 else 0
                mm(bank[:, at:at + w], w1[:, 0, c * P:(c + 1) * P], ht_all[:, t0 * P:t1 * P],
                   start=True, stop=True).then_inc(hid0_mm, 1)

            def probability_row(bank, t0, t1):
                for t in range(t0, t1):
                    last = turn(chunks(bank)[:, t - t0, :], r_prob[:, t:t + 1].broadcast_to([P, P]), ident[:, :])
                last.then_inc(row_mm, 1)

            def ranks(t, n, start=False, stop=False):
                return mm(o_a[:, n * E:(n + 1) * E], ahead[:, t, n * P:(n + 1) * P], r_pick[:, t, :],
                          start=start, stop=stop, skip_group_check=True)

            def tied(t, stop=False):
                return mm(o_a[:, t * E:(t + 1) * E], ties[:, t, :], r_pick[:, t, :],
                          start=False, stop=stop, skip_group_check=True)

            def out0(t, bank, done=None):
                for c in range(FC):
                    last = mm(chunks(bank)[:, t % 4, :], hid0[:, c, t * P:(t + 1) * P], w2[:, 0, c, :],
                              start=(c == 0), stop=(c == FC - 1))
                if done is not None:
                    last.then_inc(done, 1)

            turn_probs(dl_w, halves(d2_tsb, NT), dl_tmm, NT - 1)
            pe.wait_ge(w1_in, 16 * NT)
            pe.wait_ge(ht_all_s, NT - 2)
            pe.wait_ge(kl_sb, NT)
            hidden0(0)
            pe.wait_ge(g_kept, NT - 1)
            pe.wait_ge(vl_moved, NT - 1)
            weigh(o_b, vl, halves(dl_tsb, NT - 1), True, ob_mm)
            pe.wait_ge(b_h, NT)
            turn(t_even[:, 0:P], h_b[:, :], ident[:, :]).then_inc(bt_mm, 1)
            pe.wait_ge(ob_sb, NT - 1)
            pe.wait_ge(x1_s, NT)
            join_heads(m0, att_bt, wo, x3_mm)
            pe.wait_ge(bt_sb, NT)
            mm(t_odd[:, 0:D + E], h_bt[:, :], we_wg[:, :], start=True, stop=True).then_inc(y_mm, 1)
            pe.wait_ge(dl_exp, both(NT - 1))
            hidden0(1)
            count_choices(NT)
            hidden0(2)
            pe.wait_ge(c_h, NT - 1)
            turn(t_even[:, 0:P], rows_all[:, NT - 2, 0:D], ident[:, :]).then_inc(ct_mm, 1)
            pe.wait_ge(oa_sb, NT)
            hidden0(3)
            pe.wait_ge(ct_sb, NT - 1)
            pe.wait_ge(y_s, NT)
            mm(t_odd[:, 0:E], ht_all[:, (NT - 2) * P:(NT - 1) * P], rw_t[:, :], start=True, stop=True).then_inc(cl_mm, 1)
            pe.wait_ge(b2_h, NT)
            turn(t_even[:, 0:P], h_2[:, :], ident[:, :]).then_inc(b2t_mm, 1)
            pe.wait_ge(hid0_sb, 1)
            hidden0(4)
            pe.wait_ge(b2t_sb, NT)
            pe.wait_ge(x3_s, NT - 1)
            project(m0, wq, h_2t[:, :], ql_mm)
            pe.wait_ge(f_prob, 1)
            pe.wait_ge(hid0_sb, 4)
            probability_row(o_a, 0, 4)
            pe.wait_ge(ql_sb, NT)
            pe.wait_ge(kl_sb, NT)
            scores(ql, kl, dl_mm)
            pe.wait_ge(hid0_sb, 5)
            probability_row(m1, 4, NT - 1)
            pe.wait_ge(row_sb, 1)
            hidden0(5)
            pe.wait_ge(cl_s, NT - 1)
            turn_probs(dl_w, None, dl_tmm, NT)
            pe.wait_ge(row_sb, 2)
            hidden0(6)
            pe.wait_ge(g_kept, NT)
            pe.wait_ge(vl_moved, NT)
            weigh(o_b, vl, halves(dl_tsb, NT), True, ob_mm)
            pe.wait_ge(hid0_sb, 6)
            hidden0(7)
            pe.wait_ge(ob_sb, NT)
            pe.wait_ge(ql_sb, NT)
            join_heads(m0, att_bt, wo, x3_mm)
            pe.wait_ge(w2_in, 16 * (NT + 1))
            pe.wait_ge(dl_exp, both(NT))
            pe.wait_ge(hid0_sb, 8)
            out0(0, s_even)
            out0(1, s_even)
            pe.wait_ge(c_h, NT)
            pe.wait_ge(dl_tsb, both(NT))
            turn(t_even[:, 0:P], rows_all[:, NT - 1, 0:D], ident[:, :]).then_inc(ct_mm, 1)
            out0(2, s_even)
            pe.wait_ge(ct_sb, NT)
            mm(t_odd[:, 0:E], ht_all[:, (NT - 1) * P:T], rw_t[:, :], start=True, stop=True).then_inc(cl_mm, 1)
            pe.wait_ge(f_pick, 1)
            for t in range(NT - 1):
                pe.wait_ge(ahead_s, t + 1)
                for n in range(NT - 1):
                    ranks(t, n, start=(t == 0 and n == 0))
                tied(t)
            out0(3, s_even, y0_mm)
            pe.wait_ge(f_prob, 2)
            probability_row(t_even, NT - 1, NT)
            pe.wait_ge(hid0_sb, 7)
            for u in range(8, 12):
                hidden0(u)
            pe.wait_ge(f_pick, 2)
            pe.wait_ge(ahead_s, NT)
            for n in range(NT):
                ranks(NT - 1, n)
            tied(NT - 1)
            pe.wait_ge(ahead_s, NT + 1)
            for t in range(NT - 1):
                last = ranks(t, NT - 1, stop=(t == NT - 2))
            last.then_inc(rank_mm, 1)
            pe.wait_ge(hid0_sb, 12)
            for t in range(4, NT):
                out0(t, s_odd, y0_mm if t == NT - 1 else None)

            pe.wait_ge(row_sb, 3)
            pe.wait_ge(cl_s, NT)
            pe.wait_ge(f_idx, 1)
            pe.wait_ge(xg_in, 48)
            for j in range(3):
                for i in range(3):
                    last = turn(chunks((t_even, t_odd, o_a)[j])[:, i, :], xg[:, 3 * j + i, 0:D], ident[:, :])
                last.then_inc(xgt_mm, 1)

            def hidden(e):
                pe.wait_ge(xgt_sb, -(-e * CAP1 // 384))
                for g in range(2):
                    if e > 2:
                        pe.wait_ge((hid_sb_act, hid_sb_dve)[g], e - 2)
                    bank = ((m0, m1), (s_even, s_odd))[e % 2][g]
                    for c in range(2):
                        f = 2 * g + c
                        last = mm(bank[:, c * CAP1:(c + 1) * CAP1], w1[:, e, f * P:(f + 1) * P],
                                  xg_t[:, (e - 1) * CAP1:e * CAP1], start=True, stop=True)
                    last.then_inc(hid_mm, 1)

            def expert_out(e):
                pe.wait_ge(hid_sb_act, e)
                pe.wait_ge(hid_sb_dve, e)
                if e > 2:
                    pe.wait_ge(yt_sb, e - 2)
                else:
                    pe.wait_ge(xgt_sb, 3)
                for c in range(FC):
                    last = mm((t_even, t_odd)[e % 2][:, 0:CAP1], w2[:, e, c, :], hid[:, e % 2, c, :],
                              start=(c == 0), stop=(c == FC - 1))
                last.then_inc(yt_mm, 1)

            def rows(e):
                for j in rows_after(e):
                    pe.wait_ge(yt_sb, e)
                    if j >= 2:
                        pe.wait_ge(yr_sb, j - 1)
                    w = min(P, SLOTS - j * P)
                    turn((o_a, o_b)[j % 2][0:w, 0:D], y_t[:, j * P:j * P + w], ident[:, :]).then_inc(yr_mm, 1)

            pe.wait_ge(acc_s, 2)
            pe.wait_ge(ob_sb, NT)
            hidden(1)
            for e in range(2, E):
                hidden(e)
                expert_out(e - 1)
                if e > 2:
                    rows(e - 2)
            expert_out(E - 1)
            rows(E - 2)
            rows(E - 1)


_INS = ['x', 'ctx_1024', 'L0_xattn_Wq1', 'L0_xattn_Wk1', 'L0_xattn_Wv1', 'L0_xattn_Wq2', 'L0_xattn_Wk2', 'L0_xattn_Wv2',
        'L0_xattn_alpha_attn', 'L0_xattn_Wout', 'L0_xattn_bout', 'L0_ffn_Wg', 'L0_ffn_We', 'L0_ffn_be', 'L1_xattn_Wq',
        'L1_xattn_Wk', 'L1_xattn_Wv', 'L1_xattn_Wo', 'L1_xattn_bo', 'L1_ffn_router_w', 'L1_ffn_W1', 'L1_ffn_b1',
        'L1_ffn_W2', 'L1_ffn_b2']
_OUTS = [((8, 128, 128), 'float32')]


def kernel(**inputs):
    import numpy as _np
    import concourse.bacc as _bacc
    from concourse import mybir as _mybir
    from concourse.bass_utils import run_bass_kernel_spmd as _run

    nc = _bacc.Bacc("TRN2", target_bir_lowering=False, num_devices=1)
    arrays, args = {}, []
    for name in _INS:
        a = _np.ascontiguousarray(inputs[name])
        if a.ndim == 0:
            a = a.reshape(1)
        arrays[f"in_{name}_dram"] = a
        args.append(nc.dram_tensor(f"in_{name}_dram", a.shape, _mybir.dt.from_np(a.dtype), kind="ExternalInput").ap())
    for i, (shape, dtype) in enumerate(_OUTS):
        dt = _mybir.dt.from_np(_np.dtype(dtype))
        args.append(nc.dram_tensor(f"out_{i}_dram", shape, dt, kind="ExternalOutput").ap())
    two_layers(nc, *args)
    r = _run(nc, [arrays], core_ids=[0])
    got = tuple(r.results[0][f"out_{i}_dram"] for i in range(len(_OUTS)))
    return got[0]
```

```python
from contextlib import ExitStack

import concourse.bass as bass
from concourse import mybir

ALU = mybir.AluOpType
ACT = mybir.ActivationFunctionType
AX = mybir.AxisListType
F32 = mybir.dt.float32
BF16 = mybir.dt.bfloat16
I32 = mybir.dt.int32
U32 = mybir.dt.uint32

EPS = 1e-5


def two_layers(nc, x, ctx_1024, L0_xattn_Wq1, L0_xattn_Wk1, L0_xattn_Wv1, L0_xattn_Wq2, L0_xattn_Wk2,
               L0_xattn_Wv2, L0_xattn_alpha_attn, L0_xattn_Wout, L0_xattn_bout, L0_ffn_Wg, L0_ffn_We,
               L0_ffn_be, L1_xattn_Wq, L1_xattn_Wk, L1_xattn_Wv, L1_xattn_Wo, L1_xattn_bo,
               L1_ffn_router_w, L1_ffn_W1, L1_ffn_b1, L1_ffn_W2, L1_ffn_b2, out):
    NT, P, D = x.shape
    INNER = L0_xattn_Wq1.shape[1]
    DH = 64
    H = INNER // DH
    C = INNER // P
    E = L0_ffn_Wg.shape[1]
    FF = L1_ffn_W1.shape[2]
    FC = FF // P
    T = NT * P
    SCALE = float(DH) ** -0.5
    CAP0 = T // E
    CAP1 = -(-(T * 5) // (E * 4))
    SLOTS = (E - 1) * CAP1
    ST = -(-SLOTS // P)
    FAR = 8192.0
    ROW = 2 * D + 1
    assert P == 128 and D == 128 and C == 4 and H == 8 and E == 8

    ctx = ExitStack()
    with ctx:
        def sb(name, shape, dt=F32):
            return ctx.enter_context(nc.sbuf_tensor(name, shape, dt))

        def sems(names):
            return [ctx.enter_context(nc.semaphore(n)) for n in names.split()]

        m0, m1, s_even, s_odd, t_even, t_odd, o_a, o_b = [
            ctx.enter_context(nc.psum_tensor(n, [P, 512], F32))
            for n in ("m0", "m1", "s_even", "s_odd", "t_even", "t_odd", "o_a", "o_b")]
        s_bank, t_bank = (s_even, s_odd), (t_even, t_odd)

        def chunks(bank):
            return bank[:, :].rearrange("p (c n) -> p c n", c=C)

        ident = sb("ident", [P, P])
        ones = sb("ones", [P, P], BF16)
        before = sb("before", [P, P], BF16)
        first_first = sb("first_first", [P, E])
        place_base = sb("place_base", [P, E])
        minus_half = sb("minus_half", [P, 1])
        eps_col = sb("eps_col", [P, 1])
        carrier = sb("carrier", [P, 1])
        pool_carrier = sb("pool_carrier", [P, 1])
        token = sb("token", [P, NT])
        b20_x = sb("b20_x", [P, NT, D])
        no_rows = sb("no_rows", [P, ST, ROW])
        wq1, wk1, wv1, wq2, wk2, wv2, wq, wk, wv = [
            sb(n, [D, INNER]) for n in "wq1 wk1 wv1 wq2 wk2 wv2 wq wk wv".split()]
        wout = sb("wout", [P, C, D])
        wo = sb("wo", [P, C, D])
        we_wg = sb("we_wg", [D, D + E])
        rw_rows = sb("rw_rows", [E, D])
        rw_t = sb("rw_t", [D, E])
        w1 = sb("w1", [D, E, FF])
        w2 = sb("w2", [P, E, FC, D])
        b1_rows = sb("b1_rows", [E * FC, P])
        b1_t = sb("b1_t", [P, E * FC])
        b2_rows = sb("b2_rows", [E, D])
        b2_t = sb("b2_t", [D, E])
        bout_b, be_b, bo_b, b20_b = [sb(n, [P, D]) for n in "bout_b be_b bo_b b20_b".split()]
        alpha = sb("alpha", [P, 4])
        x_in = sb("x_in", [P, D])
        ctx_in = sb("ctx_in", [P, D])
        stat_n, mv_n, rstd_n = sb("stat_n", [P, 6]), sb("mv_n", [P, 2]), sb("rstd_n", [P, 2])
        xn = sb("xn", [P, D])
        xc_t = sb("xc_t", [D, 2, P])
        xb = sb("xb", [P, D])
        q1, k1, q2, k2 = [sb(n, [P, C, P]) for n in "q1 k1 q2 k2".split()]
        v1, v2 = [sb(n, [P, H, DH]) for n in "v1 v2".split()]
        probs = sb("probs", [P, 2, C, P])
        probs_t = sb("probs_t", [P, 2, C, P])
        low = sb("low", [P, 2, C])
        wsum = sb("wsum", [P, 2, C])
        rsum = sb("rsum", [P, 2, C])
        att_at = sb("att_at", [P, C, P])
        x1 = sb("x1", [P, D])
        stat_b, mv_b, rstd_b = sb("stat_b", [P, 6]), sb("mv_b", [P, 2]), sb("rstd_b", [P, 2])
        h_b = sb("h_b", [P, D])
        h_bt = sb("h_bt", [D, P])
        ybe = sb("ybe", [P, D])
        gate = sb("gate", [P, 8])
        lg = sb("lg", [P, 3, E])
        pick = sb("pick", [P, E], BF16)
        pick_sum = sb("pick_sum", [P, E], BF16)
        kept = sb("kept", [P, E])
        x2 = sb("x2", [P, D])
        stat_2, mv_2, rstd_2 = sb("stat_2", [P, 6]), sb("mv_2", [P, 2]), sb("rstd_2", [P, 2])
        h_2 = sb("h_2", [P, D])
        h_2t = sb("h_2t", [D, P])
        xb2 = sb("xb2", [P, D])
        ql, kl = sb("ql", [P, C, P]), sb("kl", [P, C, P])
        vl_next = sb("vl_next", [P, H, DH])
        vl = sb("vl", [P, H, DH])
        att_bt = sb("att_bt", [P, C, P])
        x3 = sb("x3", [P, D])
        stat_c, mv_c, rstd_c = sb("stat_c", [P, 6]), sb("mv_c", [P, 2]), sb("rstd_c", [P, 2])
        h_c = sb("h_c", [P, D])
        h_ct = sb("h_ct", [D, P])
        rows_all = sb("rows_all", [P, NT, ROW])
        ht_all = sb("ht_all", [D, T])
        lg_all = sb("lg_all", [P, NT, E])
        r_max, r_sum, r_prob, r_first, r_base, r_pos, r_out, r_slot = [
            sb(n, [P, NT]) for n in "r_max r_sum r_prob r_first r_base r_pos r_out r_slot".split()]
        r_less, r_exp, r_mark, r_tmp, r_tmp2 = [
            sb(n, [P, NT, E]) for n in "r_less r_exp r_mark r_tmp r_tmp2".split()]
        r_pick = sb("r_pick", [P, NT, E], BF16)
        r_idx = sb("r_idx", [P, NT], U32)
        prob_row = sb("prob_row", [P, T])
        ahead = sb("ahead", [P, NT, T], BF16)
        ties = sb("ties", [P, NT, P], BF16)
        hid0 = sb("hid0", [P, FC, T])
        acc = sb("acc", [P, NT, D])
        xg = sb("xg", [P, ST, ROW])
        xg_tok = sb("xg_tok", [P, ST], U32)
        xg_t = sb("xg_t", [D, ST * P])
        hid = sb("hid", [P, 2, FC, CAP1])
        y_t = sb("y_t", [D, SLOTS])
        y_rows = sb("y_rows", [P, ST, D])
        xg_dram = nc.dram_tensor("xg_dram", [ST * P, ROW], F32, kind="Internal").ap()

        x_in_s, ctx_in_s, alpha_in, wq2_in, wk1_in, wv1_in, wq1_in, wk2_in, wv2_in, wv_in = sems(
            "x_in_s ctx_in_s alpha_in wq2_in wk1_in wv1_in wq1_in wk2_in wv2_in wv_in")
        bout_in, small_in, late_a_in, stage_b_in, w1_in, w2_in = sems(
            "bout_in small_in late_a_in stage_b_in w1_in w2_in")
        const_s, xg_zero_in, alpha_exp, alpha_s, rw_mm, small_s = sems(
            "const_s xg_zero_in alpha_exp alpha_s rw_mm small_s")
        n_mv, n_rstd, n_xn, n_mm, n_sb, xb_s = sems(
            "n_mv n_rstd n_xn n_mm n_sb xb_s")
        q2_mm, q2_sb, k1_mm, k1_sb, v1_mm, v1_sb, q1_mm, q1_sb, k2_mm, k2_sb, v2_mm, v2_sb = sems(
            "q2_mm q2_sb k1_mm k1_sb v1_mm v1_sb q1_mm q1_sb k2_mm k2_sb v2_mm v2_sb")
        kl_mm, kl_sb, vl_mm, vl_sb, vl_moved = sems("kl_mm kl_sb vl_mm vl_sb vl_moved")
        d1_mm, d2_mm, dl_mm, d1_low, d2_low, dl_low, d1_exp, d2_exp, dl_exp = sems(
            "d1_mm d2_mm dl_mm d1_low d2_low dl_low d1_exp d2_exp dl_exp")
        d1_rec, d2_rec, dl_rec, d1_w, d2_w, dl_w = sems("d1_rec d2_rec dl_rec d1_w d2_w dl_w")
        d1_tmm, d2_tmm, dl_tmm = sems("d1_tmm d2_tmm dl_tmm")
        d1_tsb = sems("d1_tsb_even d1_tsb_odd")
        d2_tsb = sems("d2_tsb_even d2_tsb_odd")
        dl_tsb = sems("dl_tsb_even dl_tsb_odd")
        oa_mm, oa_sb, x1_mm, x1_s = sems("oa_mm oa_sb x1_mm x1_s")

        def half(n, par):
            return 2 * n - 1 + par

        def both(n):
            return 2 * n

        b_mv, b_rstd, b_h, bt_mm, bt_sb, y_mm, g_max, g_less, y_s, g_mark, g_exp = sems(
            "b_mv b_rstd b_h bt_mm bt_sb y_mm g_max g_less y_s g_mark g_exp")
        g_first, g_pick, loc_mm, g_gate, g_kept, g_kgate, pick_sum_s, x2_s = sems(
            "g_first g_pick loc_mm g_gate g_kept g_kgate pick_sum_s x2_s")
        b2_mv, b2_rstd, b2_h, b2t_mm, b2t_sb, xb2_s, ql_mm, ql_sb = sems(
            "b2_mv b2_rstd b2_h b2t_mm b2t_sb xb2_s ql_mm ql_sb")
        ob_mm, ob_sb, x3_mm, x3_s = sems("ob_mm ob_sb x3_mm x3_s")
        c_mv, c_rstd, c_h, ct_mm, ct_sb, cl_mm, cl_s, x3_all_s, h_all_s, ht_all_s = sems(
            "c_mv c_rstd c_h ct_mm ct_sb cl_mm cl_s x3_all_s h_all_s ht_all_s")
        f_dve, f_less, f_exp, f_prob, f_pick, row_mm, row_sb, ahead_s, rank_mm, f_out, f_idx = sems(
            "f_dve f_less f_exp f_prob f_pick row_mm row_sb ahead_s rank_mm f_out f_idx")
        hid0_mm, hid0_sb, y0_mm, b20_x_s, acc_s, acc_out, scat_s, xg_rest_in, tok_s, xgt_mm, xgt_sb = sems(
            "hid0_mm hid0_sb y0_mm b20_x_s acc_s acc_out scat_s xg_rest_in tok_s xgt_mm xgt_sb")
        xg_in = sems("xg0_in xg1_in xg2_in")
        hid_mm, hid_sb_act, hid_sb_dve, yt_mm, yt_sb, yr_mm, yr_sb, out_s = sems(
            "hid_mm hid_sb_act hid_sb_dve yt_mm yt_sb yr_mm yr_sb out_s")

        block = ctx.enter_context(nc.Block())

        def before_d1(k, c, d2_s, dl_s):
            return (dl_s, k - 1) if c else (d2_s, k)

        HID0 = ([(c, 0, 4, b) for c, b in enumerate((m1, s_even, s_odd, o_b))]
                + [(c, 4, NT - 1, b) for c, b in enumerate((m0, s_even, s_odd, m1))]
                + [(c, NT - 1, NT, m1) for c in range(FC)])

        def rows_after(e):
            full = [j for j in range(ST) if min((j + 1) * P, SLOTS) <= e * CAP1]
            return [j for j in full if min((j + 1) * P, SLOTS) > (e - 1) * CAP1]

        @block.sync
        def _(sp):
            sp.dma_start(x_in[:, :], x[0]).then_inc(x_in_s, 16)
            sp.dma_start(wq2[:, :], L0_xattn_Wq2).then_inc(wq2_in, 16)
            sp.dma_start(wk1[:, :], L0_xattn_Wk1).then_inc(wk1_in, 16)
            sp.dma_start(wv1[:, :], L0_xattn_Wv1).then_inc(wv1_in, 16)
            sp.dma_start(wq1[:, :], L0_xattn_Wq1).then_inc(wq1_in, 16)
            sp.dma_start(wk2[:, :], L0_xattn_Wk2).then_inc(wk2_in, 16)
            sp.dma_start(wv[:, :], L1_xattn_Wv).then_inc(wv_in, 16)
            sp.dma_start(wv2[:, :], L0_xattn_Wv2).then_inc(wv2_in, 16)
            sp.dma_start(wk[:, :], L1_xattn_Wk).then_inc(late_a_in, 16)
            sp.dma_start(wout[:, :, :], L0_xattn_Wout.rearrange("(c p) n -> p c n", p=P)).then_inc(late_a_in, 16)
            sp.dma_start(be_b[:, :], L0_ffn_be.rearrange("(a d) -> a d", a=1).broadcast_to([P, D])).then_inc(stage_b_in, 16)
            sp.dma_start(we_wg[:, 0:D], L0_ffn_We).then_inc(stage_b_in, 16)
            sp.dma_start(we_wg[:, D:D + E], L0_ffn_Wg).then_inc(stage_b_in, 16)
            sp.dma_start(bo_b[:, :], L1_xattn_bo.rearrange("(a d) -> a d", a=1).broadcast_to([P, D])).then_inc(stage_b_in, 16)
            sp.dma_start(wq[:, :], L1_xattn_Wq).then_inc(stage_b_in, 16)
            sp.dma_start(wo[:, :, :], L1_xattn_Wo.rearrange("(c p) n -> p c n", p=P)).then_inc(stage_b_in, 16)
            sp.dma_start(b20_b[:, :], L1_ffn_b2[0:1, :].broadcast_to([P, D])).then_inc(w2_in, 16)
            w1_d = L1_ffn_W1.rearrange("e p f -> p e f")
            w2_d = L1_ffn_W2.rearrange("e (c p) n -> p e c n", p=P)
            sp.dma_start(w1[:, 0, :], w1_d[:, 0, :]).then_inc(w1_in, 16)
            sp.dma_start(w2[:, 0, :, :], w2_d[:, 0, :, :]).then_inc(w2_in, 16)
            with sp.Fori(1, NT) as n:
                sp.wait_ge(n_xn, n)
                sp.wait_ge(xb_s, n)
                sp.dma_start(x_in[:, :], x[bass.ds(n, 1)].rearrange("a p d -> (a p) d")).then_inc(x_in_s, 16)
                sp.wait_ge(n_mm, n)
                sp.dma_start(ctx_in[:, :], ctx_1024[bass.ds(n, 1)].rearrange("a p d -> (a p) d")).then_inc(ctx_in_s, 16)
                sp.dma_start(w1[:, bass.ds(n, 1), :].rearrange("p a f -> p (a f)"),
                             w1_d[:, bass.ds(n, 1), :].rearrange("p a f -> p (a f)")).then_inc(w1_in, 16)
                sp.dma_start(w2[:, bass.ds(n, 1), :, :].rearrange("p a c n -> p (a c) n"),
                             w2_d[:, bass.ds(n, 1), :, :].rearrange("p a c n -> p (a c) n")).then_inc(w2_in, 16)
            for g in range(2):
                sp.wait_ge(acc_s, g + 1)
                sp.dma_start(out.rearrange("t p d -> p t d")[:, 4 * g:4 * g + 4, :],
                             acc[:, 4 * g:4 * g + 4, :]).then_inc(acc_out, 16)
            sp.wait_ge(scat_s, 16 * NT)
            xg_v = xg_dram.rearrange("(j p) d -> p j d", p=P)
            for j in range(3):
                sp.dma_start(xg[:, 3 * j:3 * j + 3, 0:D], xg_v[:, 3 * j:3 * j + 3, 0:D]).then_inc(xg_in[j], 16)
            sp.dma_start(xg[:, :, D:ROW], xg_v[:, :, D:ROW]).then_inc(xg_rest_in, 16)
            sp.wait_ge(acc_out, 32)

        @block.gpsimd
        def _(pool):
            nc.gpsimd.memset(ident[:, :], 0.0).then_inc(const_s, 1)
            nc.gpsimd.memset(ones[:, :], 1.0).then_inc(const_s, 1)
            nc.gpsimd.memset(minus_half[:, :], -0.5).then_inc(const_s, 1)
            nc.gpsimd.memset(eps_col[:, :], EPS).then_inc(const_s, 1)
            pool.wait_ge(const_s, 4)
            nc.gpsimd.affine_select(out=ident[:, :], in_=ident[:, :], compare_op=ALU.not_equal, fill=1.0, base=0,
                                    pattern=[[-1, P]], channel_multiplier=1).then_inc(const_s, 1)

            def rstd(mv, r, mv_s, r_s, n):
                pool.wait_ge(mv_s, both(n))
                nc.gpsimd.tensor_tensor(r[:, 0:1], mv[:, 1:2], eps_col[:, :], ALU.add).then_inc(r_s, 1)
                pool.wait_ge(r_s, both(n) - 1)
                nc.gpsimd.tensor_tensor(r[:, 1:2], r[:, 0:1], minus_half[:, :], ALU.pow).then_inc(r_s, 1)

            def residual(k):
                pool.wait_ge(x_in_s, 16 * (k + 1))
                nc.gpsimd.tensor_tensor(xb[:, :], x_in[:, :], bout_b[:, :], ALU.add).then_inc(xb_s, 1)

            rstd(mv_n, rstd_n, n_mv, n_rstd, 1)
            pool.dma_start(alpha[:, 0:1], L0_xattn_alpha_attn.rearrange("(a b) -> a b", a=1).broadcast_to([P, 1])).then_inc(alpha_in, 16)
            nc.gpsimd.affine_select(out=before[:, :], in_=ones[:, :], compare_op=ALU.is_gt, fill=0.0, base=0,
                                    pattern=[[1, P]], channel_multiplier=-1).then_inc(const_s, 1)
            nc.gpsimd.memset(pick_sum[:, :], 0.0).then_inc(const_s, 1)
            for e in range(E):
                nc.gpsimd.memset(first_first[:, e:e + 1], float(E - e)).then_inc(const_s, 1)
                nc.gpsimd.memset(place_base[:, e:e + 1], float((e - 1) * CAP1)).then_inc(const_s, 1)
            pool.wait_ge(bout_in, 16)
            residual(0)

            def count_choice(n):
                pool.wait_ge(loc_mm, n)
                nc.gpsimd.tensor_tensor(pick_sum[:, :], pick_sum[:, :], pick[:, :], ALU.add).then_inc(pick_sum_s, 1)

            def x2_and_bias(n, c):
                pool.wait_ge(x2_s, n)
                if c:
                    pool.wait_ge(x3_s, n - 1)
                nc.gpsimd.tensor_tensor(xb2[:, :], x2[:, :], bo_b[:, :], ALU.add).then_inc(xb2_s, 1)

            def move_vl(n, c):
                pool.wait_ge(vl_sb, n)
                if c:
                    pool.wait_ge(ob_mm, n - 1)
                nc.gpsimd.tensor_tensor(pool_carrier[:, :], eps_col[:, :], eps_col[:, :], ALU.add)
                nc.gpsimd.tensor_copy(vl[:, :, :], vl_next[:, :, :]).then_inc(vl_moved, 1)

            def step(k, b, c, nxt):
                nA, nB, nC = k + 1, k, k - 1
                if nxt:
                    rstd(mv_n, rstd_n, n_mv, n_rstd, k + 2)
                if b:
                    count_choice(nB)
                    rstd(mv_2, rstd_2, b2_mv, b2_rstd, nB)
                if c:
                    rstd(mv_c, rstd_c, c_mv, c_rstd, nC)
                if b:
                    x2_and_bias(nB, c)
                if c:
                    pool.wait_ge(x3_s, nC)
                    nc.gpsimd.tensor_copy(rows_all[:, bass.ds(k - 2, 1), D:2 * D].rearrange("p a d -> p (a d)"),
                                          x3[:, :]).then_inc(x3_all_s, 1)
                if b:
                    move_vl(nB, c)
                if c:
                    pool.wait_ge(c_h, nC)
                    nc.gpsimd.tensor_copy(rows_all[:, bass.ds(k - 2, 1), 0:D].rearrange("p a d -> p (a d)"),
                                          h_c[:, :]).then_inc(h_all_s, 1)
                    pool.wait_ge(ct_sb, nC)
                    nc.gpsimd.tensor_copy(ht_all[:, bass.ts(k - 2, P)], h_ct[:, :]).then_inc(ht_all_s, 1)
                rstd(mv_b, rstd_b, b_mv, b_rstd, nA)
                if nxt:
                    pool.wait_ge(x1_s, nA)
                    residual(k + 1)

            step(0, False, False, True)
            nc.gpsimd.iota(token[:, :], [[P, NT]], base=0, channel_multiplier=1,
                           allow_small_or_imprecise_dtypes=True).then_inc(const_s, 1)
            nc.gpsimd.memset(no_rows[:, :, :], 0.0).then_inc(const_s, 1)
            pool.wait_ge(const_s, 9 + 2 * E)
            nc.gpsimd.tensor_copy(rows_all[:, :, 2 * D], token[:, :]).then_inc(const_s, 1)
            nc.gpsimd.memset(no_rows[:, :, 2 * D:ROW], FAR).then_inc(const_s, 1)
            pool.wait_ge(const_s, 11 + 2 * E)
            pool.dma_start(xg_dram.rearrange("(p j) d -> p j d", p=P), no_rows[:, :, :]).then_inc(xg_zero_in, 16)
            pool.wait_ge(stage_b_in, 96)
            step(1, True, False, True)
            with pool.Fori(2, NT - 1) as k:
                step(k, True, True, True)
            step(NT - 1, True, True, False)

            rstd(mv_2, rstd_2, b2_mv, b2_rstd, NT)
            rstd(mv_c, rstd_c, c_mv, c_rstd, NT - 1)
            move_vl(NT, True)
            x2_and_bias(NT, True)
            pool.wait_ge(w2_in, 16 * (NT + 1))
            pool.wait_ge(x3_all_s, NT - 2)
            for t in range(NT - 1):
                nc.gpsimd.tensor_tensor(b20_x[:, t, :], rows_all[:, t, D:2 * D], b20_b[:, :], ALU.add).then_inc(b20_x_s, 1)
            rstd(mv_c, rstd_c, c_mv, c_rstd, NT)
            pool.wait_ge(x3_s, NT)
            nc.gpsimd.tensor_tensor(b20_x[:, NT - 1, :], rows_all[:, NT - 1, D:2 * D], b20_b[:, :], ALU.add).then_inc(b20_x_s, 1)

            pool.wait_ge(f_idx, 1)
            pool.wait_ge(xg_zero_in, 16)
            pool.wait_ge(h_all_s, NT - 2)
            pool.wait_ge(c_h, NT)
            for t in range(NT):
                nc.gpsimd.indirect_dma_start(
                    out=xg_dram, out_offset=bass.IndirectOffsetOnAxis(ap=r_idx[:, t:t + 1], axis=0),
                    in_=rows_all[:, t, :], in_offset=None, bounds_check=SLOTS - 1, oob_is_err=False).then_inc(scat_s, 16)
            pool.wait_ge(acc_out, 32)
            pool.wait_ge(tok_s, 1)
            for j in range(ST):
                w = min(P, SLOTS - j * P)
                pool.wait_ge(yr_sb, j + 1)
                nc.gpsimd.indirect_dma_start(
                    out=out.rearrange("t p d -> (t p) d"),
                    out_offset=bass.IndirectOffsetOnAxis(ap=xg_tok[0:w, j:j + 1], axis=0),
                    in_=y_rows[0:w, j, :], in_offset=None, bounds_check=T - 1, oob_is_err=False).then_inc(out_s, 16)
            pool.wait_ge(out_s, 16 * ST)

        @block.scalar
        def _(act):
            act.dma_start(ctx_in[:, :], ctx_1024[0]).then_inc(ctx_in_s, 16)
            act.dma_start(bout_b[:, :], L0_xattn_bout.rearrange("(a d) -> a d", a=1).broadcast_to([P, D])).then_inc(bout_in, 16)
            act.dma_start(rw_rows[:, :], L1_ffn_router_w).then_inc(small_in, 16)
            act.dma_start(b1_rows[:, :], L1_ffn_b1.rearrange("e (c p) -> (e c) p", p=P)).then_inc(small_in, 16)
            act.dma_start(b2_rows[:, :], L1_ffn_b2).then_inc(small_in, 16)

            def out_of_psum(dst, src, mm, done, n):
                act.wait_ge(mm, n)
                nc.scalar.copy(dst, src).then_inc(done, 1)

            def queries(dst, src, mm, done, n):
                act.wait_ge(mm, n)
                nc.scalar.activation(dst, src, ACT.Copy, scale=-SCALE).then_inc(done, 1)

            def exp_half(par, low_s, tmm_before, n_before, done, n):
                act.wait_ge(low_s, half(n, par))
                if not (isinstance(n_before, int) and n_before == 0):
                    act.wait_ge(tmm_before, half(n_before, par))
                for c in range(C):
                    last = nc.scalar.activation(probs[:, par, c, :], chunks(s_bank[par])[:, c, :], ACT.Exp,
                                                bias=low[:, par, c:c + 1], scale=-1.0, accum_out=wsum[:, par, c:c + 1])
                last.then_inc(done, 1)

            def turned(par, tmm, tsb, n):
                act.wait_ge(tmm, half(n, par))
                nc.scalar.copy(probs_t[:, par, :, :], chunks(t_bank[par])).then_inc(tsb[par], 1)

            def by_head(bank):
                return bank[:, :].rearrange("p (h d) -> p h d", h=H)

            act.wait_ge(alpha_in, 16)
            nc.scalar.activation(alpha[:, 1:2], alpha[:, 0:1], ACT.Exp, scale=-1.0).then_inc(alpha_exp, 1)

            def gate_exp(n):
                act.wait_ge(g_less, n)
                nc.scalar.activation(lg[:, 1, :], lg[:, 0, :], ACT.Exp, accum_out=gate[:, 1:2]).then_inc(g_exp, 1)

            def step(k, b, c, nxt):
                nA, nB, nC = k + 1, k, k - 1
                if c:
                    turned(0, dl_tmm, dl_tsb, nC)
                if b:
                    out_of_psum(h_bt[:, :], o_b[:, 0:P], bt_mm, bt_sb, nB)
                if not b:
                    queries(q1[:, :, :], chunks(m1), q1_mm, q1_sb, nA)
                exp_half(0, d1_low, *before_d1(k, c, d2_tmm, dl_tmm), d1_exp, nA)
                if b:
                    queries(q1[:, :, :], chunks(m1), q1_mm, q1_sb, nA)
                if b:
                    gate_exp(nB)
                exp_half(1, d1_low, *before_d1(k, c, d2_tmm, dl_tmm), d1_exp, nA)
                if c:
                    out_of_psum(att_bt[:, :, :], chunks(o_b), ob_mm, ob_sb, nC)
                out_of_psum(v1[:, :, :], by_head(m1), v1_mm, v1_sb, nA)
                turned(0, d1_tmm, d1_tsb, nA)
                if b:
                    out_of_psum(h_2t[:, :], o_b[:, 3 * P:4 * P], b2t_mm, b2t_sb, nB)
                turned(1, d1_tmm, d1_tsb, nA)
                exp_half(0, d2_low, d1_tmm, nA, d2_exp, nA)
                exp_half(1, d2_low, d1_tmm, nA, d2_exp, nA)
                if b:
                    act.wait_ge(vl_moved, nB)
                out_of_psum(vl_next[:, :, :], by_head(m0), vl_mm, vl_sb, nA)
                if c:
                    out_of_psum(h_ct[:, :], o_b[:, 0:P], ct_mm, ct_sb, nC)
                turned(0, d2_tmm, d2_tsb, nA)
                turned(1, d2_tmm, d2_tsb, nA)
                if c:
                    out_of_psum(lg_all[:, bass.ds(k - 2, 1), :].rearrange("p a e -> p (a e)"), o_b[:, P:P + E], cl_mm, cl_s, nC)
                if b:
                    exp_half(0, dl_low, d2_tmm, nA, dl_exp, nB)
                out_of_psum(att_at[:, :, :], chunks(o_a), oa_mm, oa_sb, nA)
                if b:
                    exp_half(1, dl_low, d2_tmm, nA, dl_exp, nB)

            queries(q2[:, :, :], chunks(m0), q2_mm, q2_sb, 1)
            step(0, False, False, True)
            step(1, True, False, True)
            with act.Fori(2, NT - 1) as k:
                step(k, True, True, True)
            step(NT - 1, True, True, False)

            def hidden0(u):
                c, t0, t1, bank = HID0[u]
                w = (t1 - t0) * P
                at = c * P if bank is m1 and t0 == NT - 1 else 0
                act.wait_ge(hid0_mm, u + 1 if t0 < NT - 1 else len(HID0))
                nc.scalar.activation(hid0[:, c, t0 * P:t1 * P], bank[:, at:at + w], ACT.Relu,
                                     bias=b1_t[:, c:c + 1]).then_inc(hid0_sb, 1)

            turned(0, dl_tmm, dl_tsb, NT - 1)
            hidden0(0)
            out_of_psum(h_bt[:, :], t_even[:, 0:P], bt_mm, bt_sb, NT)
            turned(1, dl_tmm, dl_tsb, NT - 1)
            hidden0(1)
            gate_exp(NT)
            out_of_psum(att_bt[:, :, :], chunks(o_b), ob_mm, ob_sb, NT - 1)
            out_of_psum(h_2t[:, :], t_even[:, 0:P], b2t_mm, b2t_sb, NT)
            hidden0(2)
            out_of_psum(ht_all[:, (NT - 2) * P:(NT - 1) * P], t_odd[:, 0:P], ct_mm, ct_sb, NT - 1)
            queries(ql[:, :, :], chunks(m0), ql_mm, ql_sb, NT)
            out_of_psum(lg_all[:, NT - 2, :], t_even[:, 0:E], cl_mm, cl_s, NT - 1)
            act.wait_ge(f_less, 1)
            nc.scalar.activation(r_exp[:, 0:NT - 1, :], r_less[:, 0:NT - 1, :], ACT.Exp).then_inc(f_exp, 1)
            exp_half(0, dl_low, dl_tmm, NT - 1, dl_exp, NT)
            exp_half(1, dl_low, dl_tmm, NT - 1, dl_exp, NT)
            hidden0(3)
            turned(0, dl_tmm, dl_tsb, NT)
            hidden0(4)
            turned(1, dl_tmm, dl_tsb, NT)
            hidden0(5)
            hidden0(6)
            out_of_psum(att_bt[:, :, :], chunks(o_b), ob_mm, ob_sb, NT)
            hidden0(7)
            out_of_psum(ht_all[:, (NT - 1) * P:T], t_even[:, 0:P], ct_mm, ct_sb, NT)
            out_of_psum(lg_all[:, NT - 1, :], t_odd[:, 0:E], cl_mm, cl_s, NT)
            act.wait_ge(f_less, 2)
            nc.scalar.activation(r_exp[:, NT - 1, :], r_less[:, NT - 1, :], ACT.Exp).then_inc(f_exp, 1)
            out_of_psum(prob_row[:, (NT - 1) * P:T], t_even[:, 0:P], row_mm, row_sb, 3)
            for u in range(8, 12):
                hidden0(u)

            for j in range(3):
                act.wait_ge(xgt_mm, j + 1)
                nc.scalar.copy(xg_t[:, 384 * j:384 * (j + 1)], (t_even, t_odd, o_a)[j][:, 0:384]).then_inc(xgt_sb, 1)

            def hidden(e):
                act.wait_ge(hid_mm, 2 * (e - 1) + 1)
                for c in range(2):
                    last = nc.scalar.activation(hid[:, e % 2, c, :], (m0, s_even)[e % 2][:, c * CAP1:(c + 1) * CAP1],
                                                ACT.Relu, bias=b1_t[:, e * FC + c:e * FC + c + 1])
                last.then_inc(hid_sb_act, 1)

            def expert_out(e):
                act.wait_ge(yt_mm, e)
                nc.scalar.activation(y_t[:, (e - 1) * CAP1:e * CAP1], (t_even, t_odd)[e % 2][:, 0:CAP1], ACT.Identity,
                                     bias=b2_t[:, e:e + 1]).then_inc(yt_sb, 1)

            for e in range(1, E):
                hidden(e)
                if e > 1:
                    expert_out(e - 1)
            expert_out(E - 1)

        @block.vector
        def _(dve):
            V = nc.vector

            def stats(src, stat, mv, mv_s, n):
                V.bn_stats(stat[:, :], src).then_inc(mv_s, 1)
                dve.wait_ge(mv_s, both(n) - 1)
                V.tensor_copy(carrier[:, :], stat[:, 0:1])
                V.bn_aggr(mv[:, :], stat[:, :]).then_inc(mv_s, 1)

            def normed(dst, src, mv, r, r_s, done, n):
                dve.wait_ge(r_s, both(n))
                V.tensor_scalar(dst, src, mv[:, 0:1], r[:, 1:2], ALU.subtract, ALU.mult).then_inc(done, 1)

            def copy(dst, src, mm, done, n):
                dve.wait_ge(mm, n)
                V.tensor_copy(dst, src).then_inc(done, 1)

            def lowest(mm, low_s, exp_before, n_before, n):
                dve.wait_ge(mm, n)
                for par in range(2):
                    if not (isinstance(n_before, int) and n_before == 0):
                        dve.wait_ge(exp_before, half(n_before, par))
                    V.tensor_reduce(low[:, par, :], chunks(s_bank[par]), AX.X, ALU.min).then_inc(low_s, 1)

            def divide(par, exp_s, rec, done, n, by):
                dve.wait_ge(exp_s, half(n, par))
                V.reciprocal(rsum[:, par, :], wsum[:, par, :]).then_inc(rec, 1)
                dve.wait_ge(rec, half(n, par))
                V.scalar_tensor_tensor(out=probs[:, par, :, :], in0=probs[:, par, :, :], scalar=by,
                                       in1=rsum[:, par, :].unsqueeze(2).broadcast_to([P, C, P]),
                                       op0=ALU.mult, op1=ALU.mult).then_inc(done, 1)

            dve.wait_ge(x_in_s, 16)
            stats(x_in[:, :], stat_n, mv_n, n_mv, 1)
            normed(xn[:, :], x_in[:, :], mv_n, rstd_n, n_rstd, n_xn, 1)
            copy(xc_t[:, :, :], chunks(t_odd)[:, 0:2, :], n_mm, n_sb, 1)
            dve.wait_ge(alpha_exp, 1)
            V.tensor_scalar(alpha[:, 1:2], alpha[:, 1:2], 1.0, None, ALU.add).then_inc(alpha_s, 1)
            dve.wait_ge(alpha_s, 1)
            V.reciprocal(alpha[:, 2:3], alpha[:, 1:2]).then_inc(alpha_s, 1)
            dve.wait_ge(alpha_s, 2)
            V.tensor_scalar(alpha[:, 3:4], alpha[:, 2:3], -1.0, 1.0, ALU.mult, ALU.add).then_inc(alpha_s, 1)
            copy(k1[:, :, :], chunks(m1), k1_mm, k1_sb, 1)
            dve.wait_ge(rw_mm, 1)
            V.tensor_copy(rw_t[:, :], o_a[:, 0:E]).then_inc(small_s, 1)
            V.tensor_copy(b1_t[:, :], o_a[:, 64:64 + E * FC]).then_inc(small_s, 1)
            V.tensor_copy(b2_t[:, :], o_a[:, 128:128 + E]).then_inc(small_s, 1)

            def turned_odd(tmm, tsb, n):
                dve.wait_ge(tmm, both(n))
                V.tensor_copy(probs_t[:, 1, :, :], chunks(t_odd)).then_inc(tsb[1], 1)

            def by_head(bank):
                return bank[:, :].rearrange("p (h d) -> p h d", h=H)

            def gate_choice(n, y):
                dve.wait_ge(y_mm, n)
                V.tensor_reduce(gate[:, 0:1], y[:, D:D + E], AX.X, ALU.max).then_inc(g_max, 1)
                dve.wait_ge(g_max, n)
                V.tensor_scalar(lg[:, 0, :], y[:, D:D + E], gate[:, 0:1], None, ALU.subtract).then_inc(g_less, 1)
                V.tensor_tensor(ybe[:, :], y[:, 0:D], be_b[:, :], ALU.add).then_inc(y_s, 1)
                dve.wait_ge(g_less, n)
                V.scalar_tensor_tensor(out=lg[:, 2, :], in0=lg[:, 0, :], scalar=0.0, in1=first_first[:, :],
                                       op0=ALU.is_ge, op1=ALU.mult).then_inc(g_mark, 1)
                dve.wait_ge(g_mark, n)
                V.tensor_reduce(gate[:, 3:4], lg[:, 2, :], AX.X, ALU.max).then_inc(g_first, 1)
                dve.wait_ge(g_first, n)
                dve.wait_ge(pick_sum_s, n - 1)
                V.tensor_scalar(pick[:, :], lg[:, 2, :], gate[:, 3:4], None, ALU.is_equal).then_inc(g_pick, 1)

            def gate_result(n, earlier):
                dve.wait_ge(g_exp, n)
                V.reciprocal(gate[:, 2:3], gate[:, 1:2]).then_inc(g_gate, 1)
                dve.wait_ge(loc_mm, n)
                dve.wait_ge(g_pick, n)
                V.scalar_tensor_tensor(out=kept[:, :], in0=earlier, scalar=float(CAP0), in1=pick[:, :],
                                       op0=ALU.is_lt, op1=ALU.mult, accum_out=gate[:, 4:5]).then_inc(g_kept, 1)
                dve.wait_ge(g_kept, n)
                dve.wait_ge(g_gate, n)
                V.tensor_tensor(gate[:, 5:6], gate[:, 4:5], gate[:, 2:3], ALU.mult).then_inc(g_kgate, 1)
                dve.wait_ge(g_kgate, n)
                dve.wait_ge(y_s, n)
                V.scalar_tensor_tensor(out=x2[:, :], in0=ybe[:, :], scalar=gate[:, 5:6], in1=x1[:, :],
                                       op0=ALU.mult, op1=ALU.add).then_inc(x2_s, 1)
                dve.wait_ge(x2_s, n)
                stats(x2[:, :], stat_2, mv_2, b2_mv, n)

            def step(k, b, c, nxt):
                nA, nB, nC = k + 1, k, k - 1
                if b:
                    normed(h_b[:, :], x1[:, :], mv_b, rstd_b, b_rstd, b_h, nB)
                lowest(d1_mm, d1_low, *before_d1(k, c, d2_exp, dl_exp), nA)
                if c:
                    turned_odd(dl_tmm, dl_tsb, nC)
                if b:
                    gate_choice(nB, o_b[:, P:P + D + E])
                if not b:
                    copy(k2[:, :, :], chunks(m0), k2_mm, k2_sb, nA)
                divide(0, d1_exp, d1_rec, d1_w, nA, alpha[:, 2:3])
                if b:
                    copy(k2[:, :, :], chunks(m0), k2_mm, k2_sb, nA)
                if nxt:
                    dve.wait_ge(x_in_s, 16 * (k + 2))
                    stats(x_in[:, :], stat_n, mv_n, n_mv, k + 2)
                if b:
                    gate_result(nB, o_a[:, 0:E])
                divide(1, d1_exp, d1_rec, d1_w, nA, alpha[:, 2:3])
                if b:
                    normed(h_2[:, :], x2[:, :], mv_2, rstd_2, b2_rstd, b2_h, nB)
                lowest(d2_mm, d2_low, d1_exp, nA, nA)
                if c:
                    dve.wait_ge(x3_mm, nC)
                    dve.wait_ge(xb2_s, nC)
                    V.tensor_tensor(x3[:, :], m0[:, 0:D], xb2[:, :], ALU.add).then_inc(x3_s, 1)
                    dve.wait_ge(x3_s, nC)
                    stats(x3[:, :], stat_c, mv_c, c_mv, nC)
                copy(v2[:, :, :], by_head(m1), v2_mm, v2_sb, nA)
                if c:
                    normed(h_c[:, :], x3[:, :], mv_c, rstd_c, c_rstd, c_h, nC)
                if nxt:
                    normed(xn[:, :], x_in[:, :], mv_n, rstd_n, n_rstd, n_xn, k + 2)
                divide(0, d2_exp, d2_rec, d2_w, nA, alpha[:, 3:4])
                if b:
                    dve.wait_ge(ql_mm, nB)
                    V.tensor_scalar(ql[:, :, :], chunks(m1), -SCALE, None, ALU.mult).then_inc(ql_sb, 1)
                divide(1, d2_exp, d2_rec, d2_w, nA, alpha[:, 3:4])
                if b:
                    lowest(dl_mm, dl_low, d2_exp, nA, nB)
                if nxt:
                    copy(xc_t[:, :, :], chunks(t_odd)[:, 0:2, :], n_mm, n_sb, k + 2)
                copy(kl[:, :, :], chunks(m1), kl_mm, kl_sb, nA)
                if b:
                    divide(0, dl_exp, dl_rec, dl_w, nB, 1.0)
                if nxt:
                    dve.wait_ge(q2_mm, k + 2)
                    V.tensor_scalar(q2[:, :, :], chunks(m0), -SCALE, None, ALU.mult).then_inc(q2_sb, 1)
                    copy(k1[:, :, :], chunks(m1), k1_mm, k1_sb, k + 2)
                if c:
                    dve.wait_ge(x3_all_s, nC)
                dve.wait_ge(x1_mm, nA)
                dve.wait_ge(xb_s, nA)
                V.tensor_tensor(x1[:, :], m0[:, 0:D], xb[:, :], ALU.add).then_inc(x1_s, 1)
                dve.wait_ge(x1_s, nA)
                stats(x1[:, :], stat_b, mv_b, b_mv, nA)
                if b:
                    divide(1, dl_exp, dl_rec, dl_w, nB, 1.0)

            dve.wait_ge(const_s, 7 + 2 * E)
            step(0, False, False, True)
            dve.wait_ge(stage_b_in, 96)
            step(1, True, False, True)
            with dve.Fori(2, NT - 1) as k:
                step(k, True, True, True)
            step(NT - 1, True, True, False)

            def per_tile(w, t0, t1):
                return w[:, t0:t1].unsqueeze(2).broadcast_to([P, t1 - t0, E])

            def per_expert(w, t0, t1):
                return w[:, :].unsqueeze(1).broadcast_to([P, t1 - t0, E])

            chain = [0]

            def done(ins, meanwhile=None, t=None):
                chain[0] += 1
                ins.then_inc(f_dve, 1)
                if t is not None:
                    meanwhile(t)
                dve.wait_ge(f_dve, chain[0])

            def probabilities(r, t0, t1, rank=None):
                dve.wait_ge(cl_s, t1)
                done(V.tensor_reduce(r_max[:, t0:t1], lg_all[:, t0:t1, :], AX.X, ALU.max))
                V.tensor_tensor(r_less[:, t0:t1, :], lg_all[:, t0:t1, :], per_tile(r_max, t0, t1), ALU.subtract).then_inc(f_less, 1)
                if rank is not None:
                    before_earlier(rank)
                dve.wait_ge(f_exp, r)
                done(V.tensor_reduce(r_sum[:, t0:t1], r_exp[:, t0:t1, :], AX.X, ALU.add))
                V.reciprocal(r_prob[:, t0:t1], r_sum[:, t0:t1]).then_inc(f_prob, 1)

            def choices(r, t0, t1, rank=None):
                dve.wait_ge(f_less, r)
                done(V.tensor_scalar(r_tmp[:, t0:t1, :], r_less[:, t0:t1, :], 0.0, None, ALU.is_ge), before_later, rank)
                done(V.tensor_tensor(r_mark[:, t0:t1, :], r_tmp[:, t0:t1, :], per_expert(first_first, t0, t1), ALU.mult), tied, rank)
                done(V.tensor_reduce(r_first[:, t0:t1], r_mark[:, t0:t1, :], AX.X, ALU.max))
                V.tensor_tensor(r_pick[:, t0:t1, :], r_mark[:, t0:t1, :], per_tile(r_first, t0, t1), ALU.is_equal).then_inc(f_pick, 1)
                dve.wait_ge(f_pick, r)
                done(V.tensor_tensor(r_tmp2[:, t0:t1, :], r_pick[:, t0:t1, :], per_expert(place_base, t0, t1), ALU.mult))
                done(V.tensor_reduce(r_base[:, t0:t1], r_tmp2[:, t0:t1, :], AX.X, ALU.add))

            def before_earlier(t):
                w = (t + 1) * P
                V.tensor_scalar(ahead[:, t, 0:w], prob_row[:, 0:w], r_prob[:, t:t + 1], None, ALU.is_lt)

            def before_later(t):
                if t < NT - 2:
                    w = (t + 1) * P
                    V.tensor_scalar(ahead[:, t, w:T - P], prob_row[:, w:T - P], r_prob[:, t:t + 1], None, ALU.is_le)

            def tied(t):
                V.scalar_tensor_tensor(out=ties[:, t, :], in0=prob_row[:, t * P:(t + 1) * P], scalar=r_prob[:, t:t + 1],
                                       in1=before[:, :], op0=ALU.is_equal, op1=ALU.mult).then_inc(ahead_s, 1)

            def ranks_before(t):
                before_earlier(t)
                before_later(t)
                tied(t)

            normed(h_b[:, :], x1[:, :], mv_b, rstd_b, b_rstd, b_h, NT)
            gate_choice(NT, o_a[:, 0:D + E])
            gate_result(NT, o_a[:, 256:256 + E])
            dve.wait_ge(x3_mm, NT - 1)
            dve.wait_ge(xb2_s, NT - 1)
            V.tensor_tensor(rows_all[:, NT - 2, D:2 * D], m0[:, 0:D], xb2[:, :], ALU.add).then_inc(x3_s, 1)
            normed(h_2[:, :], x2[:, :], mv_2, rstd_2, b2_rstd, b2_h, NT)
            dve.wait_ge(x3_s, NT - 1)
            stats(rows_all[:, NT - 2, D:2 * D], stat_c, mv_c, c_mv, NT - 1)
            normed(rows_all[:, NT - 2, 0:D], rows_all[:, NT - 2, D:2 * D], mv_c, rstd_c, c_rstd, c_h, NT - 1)
            probabilities(1, 0, NT - 1)
            lowest(dl_mm, dl_low, dl_exp, NT - 1, NT)
            copy(prob_row[:, 0:4 * P], o_a[:, :], row_mm, row_sb, 1)
            divide(0, dl_exp, dl_rec, dl_w, NT, 1.0)
            copy(prob_row[:, 4 * P:(NT - 1) * P], m1[:, 0:(NT - 5) * P], row_mm, row_sb, 2)
            divide(1, dl_exp, dl_rec, dl_w, NT, 1.0)
            choices(1, 0, NT - 1)
            dve.wait_ge(row_sb, 2)
            dve.wait_ge(f_prob, 1)
            ranks_before(0)
            ranks_before(1)
            ranks_before(2)
            dve.wait_ge(x3_mm, NT)
            dve.wait_ge(xb2_s, NT)
            V.tensor_tensor(rows_all[:, NT - 1, D:2 * D], m0[:, 0:D], xb2[:, :], ALU.add).then_inc(x3_s, 1)
            dve.wait_ge(x3_s, NT)
            stats(rows_all[:, NT - 1, D:2 * D], stat_c, mv_c, c_mv, NT)
            ranks_before(3)
            normed(rows_all[:, NT - 1, 0:D], rows_all[:, NT - 1, D:2 * D], mv_c, rstd_c, c_rstd, c_h, NT)
            ranks_before(4)
            probabilities(2, NT - 1, NT, rank=5)
            choices(2, NT - 1, NT, rank=5)
            ranks_before(6)
            dve.wait_ge(row_sb, 3)
            dve.wait_ge(f_prob, 2)
            V.tensor_scalar(ahead[:, NT - 1, :], prob_row[:, :], r_prob[:, NT - 1:NT], None, ALU.is_lt)
            tied(NT - 1)
            V.tensor_tensor(ahead[:, 0:NT - 1, T - P:T], prob_row[:, T - P:T].unsqueeze(1).broadcast_to([P, NT - 1, P]),
                            r_prob[:, 0:NT - 1].unsqueeze(2).broadcast_to([P, NT - 1, P]), ALU.is_le).then_inc(ahead_s, 1)
            dve.wait_ge(rank_mm, 1)
            done(V.tensor_tensor(r_tmp[:, :, :], o_a[:, 0:NT * E].rearrange("p (t e) -> p t e", t=NT),
                                 r_pick[:, :, :], ALU.mult))
            done(V.tensor_reduce(r_pos[:, :], r_tmp[:, :, :], AX.X, ALU.add))
            V.tensor_tensor(r_slot[:, :], r_pos[:, :], r_base[:, :], ALU.add)
            done(V.tensor_scalar(r_pos[:, :], r_pos[:, :], float(CAP1), None, ALU.is_ge))
            V.tensor_tensor(r_out[:, :], r_pos[:, :], r_pick[:, :, 0], ALU.max).then_inc(f_out, 1)
            dve.wait_ge(f_out, 1)
            V.scalar_tensor_tensor(out=r_idx[:, :], in0=r_out[:, :], scalar=FAR, in1=r_slot[:, :],
                                   op0=ALU.mult, op1=ALU.add).then_inc(f_idx, 1)
            dve.wait_ge(b20_x_s, NT)
            for g in range(2):
                dve.wait_ge(y0_mm, g + 1)
                V.tensor_tensor(acc[:, 4 * g:4 * g + 4, :], chunks((s_even, s_odd)[g]), b20_x[:, 4 * g:4 * g + 4, :],
                                ALU.add).then_inc(acc_s, 1)

            dve.wait_ge(xg_rest_in, 16)
            V.tensor_copy(xg_tok[:, :], xg[:, :, 2 * D]).then_inc(tok_s, 1)

            def hidden(e):
                dve.wait_ge(hid_mm, 2 * (e - 1) + 2)
                for c in range(2):
                    last = V.tensor_scalar(hid[:, e % 2, 2 + c, :], (m1, s_odd)[e % 2][:, c * CAP1:(c + 1) * CAP1],
                                           b1_t[:, e * FC + 2 + c:e * FC + 3 + c], 0.0, ALU.add, ALU.max)
                last.then_inc(hid_sb_dve, 1)

            def rows_out(j):
                dve.wait_ge(yr_mm, j + 1)
                w = min(P, SLOTS - j * P)
                V.tensor_tensor(y_rows[0:w, j, :], (o_a, o_b)[j % 2][0:w, 0:D], xg[0:w, j, D:2 * D], ALU.add).then_inc(yr_sb, 1)

            for e in range(1, E):
                hidden(e)
                for j in rows_after(e - 2):
                    rows_out(j)
            for e in (E - 2, E - 1):
                for j in rows_after(e):
                    rows_out(j)

        @block.tensor
        def _(pe):
            mm = nc.tensor.matmul
            turn = nc.tensor.transpose
            xn_t, c_t = xc_t[:, 0, :], xc_t[:, 1, :]

            def project(bank, w, src, done):
                for c in range(C):
                    last = mm(chunks(bank)[:, c, :], w[:, c * P:(c + 1) * P], src, start=True, stop=True)
                last.then_inc(done, 1)

            def project_rows(bank, w, src, done):
                mm(bank[:, :], src, w[:, :], start=True, stop=True).then_inc(done, 1)

            def scores(q, kk, done):
                for c in range(C):
                    for par in range(2):
                        rows = slice(par * DH, (par + 1) * DH)
                        last = mm(chunks(s_bank[par])[:, c, :], q[rows, c, :], kk[rows, c, :], start=True, stop=True)
                last.then_inc(done, 1)

            def turn_half(par, w, done, n):
                pe.wait_ge(w, half(n, par))
                for c in range(C):
                    last = turn(chunks(t_bank[par])[:, c, :], probs[:, par, c, :], ident[:, :])
                last.then_inc(done, 1)

            def turn_probs(w, copied_before, n_before, done, n):
                for par in range(2):
                    if copied_before is not None:
                        pe.wait_ge(copied_before[par], n_before)
                    turn_half(par, w, done, n)

            def weigh(bank, v, copied, n, fresh, done):
                for par in range(2):
                    pe.wait_ge(copied[par], n)
                for c in range(C):
                    for par in range(2):
                        last = mm(chunks(bank)[par * DH:(par + 1) * DH, c, :], v[:, 2 * c + par, :], probs_t[:, par, c, :],
                                  start=(fresh and c == 0), stop=(done is not None), skip_group_check=True)
                if done is not None:
                    last.then_inc(done, 1)

            def both_copied(tsb, n):
                pe.wait_ge(tsb[0], n)
                pe.wait_ge(tsb[1], n)

            def join_heads(bank, att_t, w, done):
                for c in range(C):
                    last = mm(bank[:, 0:D], att_t[:, c, :], w[:, c, :], start=(c == 0), stop=(c == C - 1))
                last.then_inc(done, 1)

            def turn_next(n):
                pe.wait_ge(ctx_in_s, 16 * n)
                turn(chunks(t_odd)[:, 1, :], ctx_in[:, :], ident[:, :])
                pe.wait_ge(n_xn, n)
                turn(chunks(t_odd)[:, 0, :], xn[:, :], ident[:, :]).then_inc(n_mm, 1)

            def keep_awake(bank, times):
                for _ in range(times):
                    mm(bank[:, :], ones[:, :], ones[:, :].unsqueeze(1).broadcast_to([P, 4, P]), start=True, stop=True)

            pe.wait_ge(const_s, 2)
            keep_awake(s_even, 6)
            pe.wait_ge(const_s, 5)
            turn_next(1)

            def loaded(k, at, s, n=16):
                if isinstance(k, int) and k == at:
                    pe.wait_ge(s, n)

            def step(k, b, c, nxt):
                nA, nB, nC = k + 1, k, k - 1
                second = isinstance(k, int) and k == 1
                pe.wait_ge(q2_sb, nA)
                pe.wait_ge(k1_sb, nA)
                if b:
                    s, n = before_d1(k, c, d2_exp, dl_exp)
                    pe.wait_ge(s, both(n))
                scores(q2, k1, d1_mm)
                if c:
                    pe.wait_ge(n_sb, nA)
                    turn_probs(dl_w, d2_tsb, nB, dl_tmm, nC)
                if b:
                    pe.wait_ge(b_h, nB)
                    turn(o_b[:, 0:P], h_b[:, :], ident[:, :]).then_inc(bt_mm, 1)
                loaded(k, 0, wq1_in)
                project(m1, wq1, xn_t, q1_mm)
                if b:
                    loaded(k, 1, stage_b_in, 96)
                    pe.wait_ge(bt_sb, nB)
                    mm(o_b[:, P:P + D + E], h_bt[:, :], we_wg[:, :], start=True, stop=True).then_inc(y_mm, 1)
                    pe.wait_ge(x1_s, nB)
                loaded(k, 0, wk2_in)
                project(m0, wk2, c_t, k2_mm)
                if c:
                    pe.wait_ge(y_s, nB)
                    pe.wait_ge(vl_moved, nC)
                    weigh(o_b, vl, dl_tsb, nC, True, ob_mm)
                loaded(k, 0, wv1_in)
                pe.wait_ge(q1_sb, nA)
                project_rows(m1, wv1, xn_t, v1_mm)
                if b:
                    if not c:
                        pe.wait_ge(const_s, 7)
                    count_choices(nB)
                pe.wait_ge(k2_sb, nA)
                if not b:
                    loaded(k, 0, wv_in)
                    project_rows(m0, wv, c_t, vl_mm)
                pe.wait_ge(d1_exp, both(nA))
                scores(q1, k2, d2_mm)
                if c:
                    pe.wait_ge(ob_sb, nC)
                    join_heads(m0, att_bt, wo, x3_mm)
                pe.wait_ge(n_sb, nA)
                if second:
                    both_copied(d2_tsb, 1)
                turn_probs(d1_w, dl_tsb if c else None, nC, d1_tmm, nA)
                if b:
                    pe.wait_ge(b2_h, nB)
                    turn(o_b[:, 3 * P:4 * P], h_2[:, :], ident[:, :]).then_inc(b2t_mm, 1)
                loaded(k, 0, wv2_in)
                pe.wait_ge(v1_sb, nA)
                project_rows(m1, wv2, c_t, v2_mm)
                if b:
                    pe.wait_ge(g_kept, nB)
                else:
                    pe.wait_ge(small_s, 3)
                weigh(o_a, v1, d1_tsb, nA, True, None)
                if b:
                    pe.wait_ge(b2t_sb, nB)
                    pe.wait_ge(v2_sb, nA)
                    project(m1, wq, h_2t[:, :], ql_mm)
                if c:
                    pe.wait_ge(c_h, nC)
                    turn(o_b[:, 0:P], h_c[:, :], ident[:, :]).then_inc(ct_mm, 1)
                if b:
                    if c:
                        pe.wait_ge(x3_s, nC)
                    project_rows(m0, wv, c_t, vl_mm)
                if b:
                    pe.wait_ge(ql_sb, nB)
                    pe.wait_ge(kl_sb, nB)
                    pe.wait_ge(d2_exp, both(nA))
                    scores(ql, kl, dl_mm)
                if not b:
                    loaded(k, 0, late_a_in, 32)
                    pe.wait_ge(v2_sb, nA)
                    project(m1, wk, c_t, kl_mm)
                turn_probs(d2_w, d1_tsb, nA, d2_tmm, nA)
                if c:
                    pe.wait_ge(ct_sb, nC)
                    mm(o_b[:, P:P + E], h_ct[:, :], rw_t[:, :], start=True, stop=True).then_inc(cl_mm, 1)
                if b:
                    pe.wait_ge(v2_sb, nA)
                    project(m1, wk, c_t, kl_mm)
                if nxt:
                    pe.wait_ge(d2_tsb[1], nA)
                    turn_next(k + 2)
                weigh(o_a, v2, d2_tsb, nA, False, oa_mm)
                pe.wait_ge(vl_sb, nA)
                if nxt:
                    first_projections(k + 1)
                if c:
                    pe.wait_ge(cl_s, nC)
                pe.wait_ge(oa_sb, nA)
                if nxt:
                    pe.wait_ge(q2_sb, k + 2)
                join_heads(m0, att_at, wout, x1_mm)

            def first_projections(k):
                pe.wait_ge(n_sb, k + 1)
                loaded(k, 0, wq2_in)
                project(m0, wq2, c_t, q2_mm)
                loaded(k, 0, wk1_in)
                if not (isinstance(k, int) and k == 0):
                    pe.wait_ge(kl_sb, k)
                project(m1, wk1, xn_t, k1_mm)

            def count_choices(n, out=o_a[:, 0:E]):
                pe.wait_ge(g_pick, n)
                mm(out, before[:, :], pick[:, :], start=True, stop=False)
                pe.wait_ge(pick_sum_s, n - 1)
                mm(out, ones[:, :], pick_sum[:, :], start=False, stop=True).then_inc(loc_mm, 1)

            keep_awake(s_even, 1)
            first_projections(0)
            pe.wait_ge(small_in, 48)
            turn(o_a[:, 0:E], rw_rows[:, :], ident[0:E, 0:E])
            turn(o_a[:, 64:64 + E * FC], b1_rows[:, :], ident[0:E * FC, 0:E * FC])
            turn(o_a[:, 128:128 + E], b2_rows[:, :], ident[0:E, 0:E]).then_inc(rw_mm, 1)
            step(0, False, False, True)
            step(1, True, False, True)
            with pe.Fori(2, NT - 1) as k:
                step(k, True, True, True)
            step(NT - 1, True, True, False)

            def hidden0(u):
                c, t0, t1, bank = HID0[u]
                w = (t1 - t0) * P
                at = c * P if bank is m1 and t0 == NT - 1 else 0
                mm(bank[:, at:at + w], w1[:, 0, c * P:(c + 1) * P], ht_all[:, t0 * P:t1 * P],
                   start=True, stop=True).then_inc(hid0_mm, 1)

            def probability_row(bank, t0, t1):
                for t in range(t0, t1):
                    last = turn(chunks(bank)[:, t - t0, :], r_prob[:, t:t + 1].broadcast_to([P, P]), ident[:, :])
                last.then_inc(row_mm, 1)

            def ranks(t, n, start=False, stop=False):
                return mm(o_a[:, n * E:(n + 1) * E], ahead[:, t, n * P:(n + 1) * P], r_pick[:, t, :],
                          start=start, stop=stop, skip_group_check=True)

            def tied(t, stop=False):
                return mm(o_a[:, t * E:(t + 1) * E], ties[:, t, :], r_pick[:, t, :],
                          start=False, stop=stop, skip_group_check=True)

            def out0(t, bank, done=None):
                for c in range(FC):
                    last = mm(chunks(bank)[:, t % 4, :], hid0[:, c, t * P:(t + 1) * P], w2[:, 0, c, :],
                              start=(c == 0), stop=(c == FC - 1))
                if done is not None:
                    last.then_inc(done, 1)

            pe.wait_ge(d2_tsb[0], NT)
            turn_half(0, dl_w, dl_tmm, NT - 1)
            pe.wait_ge(w1_in, 16 * NT)
            pe.wait_ge(ht_all_s, NT - 2)
            pe.wait_ge(kl_sb, NT)
            hidden0(0)
            pe.wait_ge(dl_exp, both(NT - 1))
            hidden0(1)
            pe.wait_ge(b_h, NT)
            pe.wait_ge(dl_tsb[0], NT - 1)
            turn(t_even[:, 0:P], h_b[:, :], ident[:, :]).then_inc(bt_mm, 1)
            pe.wait_ge(d2_tsb[1], NT)
            turn_half(1, dl_w, dl_tmm, NT - 1)
            pe.wait_ge(bt_sb, NT)
            pe.wait_ge(oa_sb, NT)
            mm(o_a[:, 0:D + E], h_bt[:, :], we_wg[:, :], start=True, stop=True).then_inc(y_mm, 1)
            pe.wait_ge(vl_moved, NT - 1)
            weigh(o_b, vl, dl_tsb, NT - 1, True, ob_mm)
            pe.wait_ge(y_s, NT)
            count_choices(NT, o_a[:, 256:256 + E])
            pe.wait_ge(ob_sb, NT - 1)
            pe.wait_ge(x1_s, NT)
            join_heads(m0, att_bt, wo, x3_mm)
            hidden0(2)
            pe.wait_ge(b2_h, NT)
            turn(t_even[:, 0:P], h_2[:, :], ident[:, :]).then_inc(b2t_mm, 1)
            pe.wait_ge(b2t_sb, NT)
            pe.wait_ge(x3_s, NT - 1)
            project(m0, wq, h_2t[:, :], ql_mm)
            pe.wait_ge(c_h, NT - 1)
            pe.wait_ge(dl_tsb[1], NT - 1)
            turn(t_odd[:, 0:P], rows_all[:, NT - 2, 0:D], ident[:, :]).then_inc(ct_mm, 1)
            pe.wait_ge(ct_sb, NT - 1)
            mm(t_even[:, 0:E], ht_all[:, (NT - 2) * P:(NT - 1) * P], rw_t[:, :], start=True, stop=True).then_inc(cl_mm, 1)
            pe.wait_ge(ql_sb, NT)
            pe.wait_ge(kl_sb, NT)
            pe.wait_ge(hid0_sb, 3)
            scores(ql, kl, dl_mm)
            hidden0(3)
            pe.wait_ge(f_prob, 1)
            pe.wait_ge(g_kept, NT)
            probability_row(o_a, 0, 4)
            probability_row(m1, 4, NT - 1)
            hidden0(4)
            pe.wait_ge(dl_exp, half(NT, 0))
            hidden0(5)
            pe.wait_ge(cl_s, NT - 1)
            turn_half(0, dl_w, dl_tmm, NT)
            pe.wait_ge(dl_exp, both(NT))
            hidden0(6)
            turn_half(1, dl_w, dl_tmm, NT)
            pe.wait_ge(row_sb, 2)
            hidden0(7)
            pe.wait_ge(vl_moved, NT)
            pe.wait_ge(hid0_sb, 4)
            weigh(o_b, vl, dl_tsb, NT, True, ob_mm)
            pe.wait_ge(w2_in, 16 * (NT + 1))
            pe.wait_ge(hid0_sb, 6)
            out0(0, s_even)
            pe.wait_ge(ob_sb, NT)
            join_heads(m0, att_bt, wo, x3_mm)
            out0(1, s_even)

            def ranks_of_tile(t):
                pe.wait_ge(ahead_s, t + 1)
                for n in range(NT - 1):
                    ranks(t, n, start=(t == 0 and n == 0))
                tied(t)

            pe.wait_ge(f_pick, 1)
            ranks_of_tile(0)
            ranks_of_tile(1)
            ranks_of_tile(2)
            pe.wait_ge(c_h, NT)
            both_copied(dl_tsb, NT)
            turn(t_even[:, 0:P], rows_all[:, NT - 1, 0:D], ident[:, :]).then_inc(ct_mm, 1)
            pe.wait_ge(ct_sb, NT)
            mm(t_odd[:, 0:E], ht_all[:, (NT - 1) * P:T], rw_t[:, :], start=True, stop=True).then_inc(cl_mm, 1)
            ranks_of_tile(3)
            pe.wait_ge(f_prob, 2)
            probability_row(t_even, NT - 1, NT)
            pe.wait_ge(hid0_sb, 8)
            for u in range(8, 12):
                hidden0(u)
            for t in range(4, NT - 1):
                ranks_of_tile(t)
            pe.wait_ge(f_pick, 2)
            pe.wait_ge(ahead_s, NT)
            for n in range(NT):
                ranks(NT - 1, n)
            tied(NT - 1)
            pe.wait_ge(ahead_s, NT + 1)
            for t in range(NT - 1):
                last = ranks(t, NT - 1, stop=(t == NT - 2))
            last.then_inc(rank_mm, 1)
            pe.wait_ge(hid0_sb, 12)
            for t in range(2, NT):
                out0(t, (s_even, s_odd)[t // 4], y0_mm if t % 4 == 3 else None)

            pe.wait_ge(row_sb, 3)
            pe.wait_ge(cl_s, NT)
            pe.wait_ge(f_idx, 1)
            pe.wait_ge(acc_s, 1)
            keep_awake(s_even, 28)
            for j in range(3):
                pe.wait_ge(xg_in[j], 16)
                for i in range(3):
                    last = turn(chunks((t_even, t_odd, o_a)[j])[:, i, :], xg[:, 3 * j + i, 0:D], ident[:, :])
                last.then_inc(xgt_mm, 1)

            def hidden(e):
                pe.wait_ge(xgt_sb, -(-e * CAP1 // 384))
                for g in range(2):
                    if g == 1 and e > 3:
                        rows(e - 2)
                    if e > 2:
                        pe.wait_ge((hid_sb_act, hid_sb_dve)[g], e - 2)
                    bank = ((m0, m1), (s_even, s_odd))[e % 2][g]
                    for c in range(2):
                        f = 2 * g + c
                        last = mm(bank[:, c * CAP1:(c + 1) * CAP1], w1[:, e, f * P:(f + 1) * P],
                                  xg_t[:, (e - 1) * CAP1:e * CAP1], start=True, stop=True)
                    last.then_inc(hid_mm, 1)

            def expert_out(e, between=None):
                pe.wait_ge(hid_sb_act, e)
                pe.wait_ge(hid_sb_dve, e)
                if e > 2:
                    pe.wait_ge(yt_sb, e - 2)
                else:
                    pe.wait_ge(xgt_sb, 3)
                for c in range(FC):
                    if c == 2 and between is not None:
                        between()
                    last = mm((t_even, t_odd)[e % 2][:, 0:CAP1], w2[:, e, c, :], hid[:, e % 2, c, :],
                              start=(c == 0), stop=(c == FC - 1))
                last.then_inc(yt_mm, 1)

            def rows(e):
                for j in rows_after(e):
                    pe.wait_ge(yt_sb, e)
                    if j >= 2:
                        pe.wait_ge(yr_sb, j - 1)
                    w = min(P, SLOTS - j * P)
                    turn((o_a, o_b)[j % 2][0:w, 0:D], y_t[:, j * P:j * P + w], ident[:, :]).then_inc(yr_mm, 1)

            pe.wait_ge(acc_s, 2)
            pe.wait_ge(ob_sb, NT)
            hidden(1)
            for e in range(2, E):
                hidden(e)
                expert_out(e - 1)
                if e == 3:
                    rows(1)
            expert_out(E - 1, between=lambda: rows(E - 2))
            rows(E - 1)


_INS = ['x', 'ctx_1024', 'L0_xattn_Wq1', 'L0_xattn_Wk1', 'L0_xattn_Wv1', 'L0_xattn_Wq2', 'L0_xattn_Wk2', 'L0_xattn_Wv2',
        'L0_xattn_alpha_attn', 'L0_xattn_Wout', 'L0_xattn_bout', 'L0_ffn_Wg', 'L0_ffn_We', 'L0_ffn_be', 'L1_xattn_Wq',
        'L1_xattn_Wk', 'L1_xattn_Wv', 'L1_xattn_Wo', 'L1_xattn_bo', 'L1_ffn_router_w', 'L1_ffn_W1', 'L1_ffn_b1',
        'L1_ffn_W2', 'L1_ffn_b2']
_OUTS = [((8, 128, 128), 'float32')]


def kernel(**inputs):
    import numpy as _np
    import concourse.bacc as _bacc
    from concourse import mybir as _mybir
    from concourse.bass_utils import run_bass_kernel_spmd as _run

    nc = _bacc.Bacc("TRN2", target_bir_lowering=False, num_devices=1)
    arrays, args = {}, []
    for name in _INS:
        a = _np.ascontiguousarray(inputs[name])
        if a.ndim == 0:
            a = a.reshape(1)
        arrays[f"in_{name}_dram"] = a
        args.append(nc.dram_tensor(f"in_{name}_dram", a.shape, _mybir.dt.from_np(a.dtype), kind="ExternalInput").ap())
    for i, (shape, dtype) in enumerate(_OUTS):
        dt = _mybir.dt.from_np(_np.dtype(dtype))
        args.append(nc.dram_tensor(f"out_{i}_dram", shape, dt, kind="ExternalOutput").ap())
    two_layers(nc, *args)
    r = _run(nc, [arrays], core_ids=[0])
    got = tuple(r.results[0][f"out_{i}_dram"] for i in range(len(_OUTS)))
    return got[0]
```
